# Optimizing a Trainium2 kernel written in Bass

```python
import numpy as np
import jax
import jax.numpy as jnp

def _softmax(x, axis=-1):
    return jax.nn.softmax(x, axis=axis)

def _gelu(x):
    return jax.nn.gelu(x, approximate=True)

def _silu(x):
    return jax.nn.silu(x)

def _sigmoid(x):
    return jax.nn.sigmoid(x)

def _layernorm(x, axis=-1, eps=1e-05):
    m = jnp.mean(x, axis=axis, keepdims=True)
    v = jnp.var(x, axis=axis, keepdims=True)
    return (x - m) / jnp.sqrt(v + eps)

def _scatter_add(tgt, idx, src, axis=0):
    return tgt.at[idx].add(src)

def _segment_sum(src, seg, n):
    return jax.ops.segment_sum(src, seg, n)
kernel_name = 'mk_metaformer_d2_conv_nhwc512_r4_8b817d'

def setup_inputs(seed: int=0):
    np.random.seed(seed)
    _w = jnp.asarray

    def _rec_inputs():
        import jax
        import jax.numpy as jnp
        _gk = jax.random.key(seed)
        x = -0.000125 + 0.9999 * jax.random.normal(jax.random.fold_in(_gk, 1), (16, 16, 16, 128), jnp.float32)
        return x
    x = _rec_inputs()

    def _L0_conv_setup():
        import jax, jax.numpy as jnp
        import numpy as np
        GROUPS = 8
        STRIDES = (1, 1)
        DILATION = (1, 1)
        key = jax.random.key(seed)
        k1, k2, k3 = jax.random.split(key, 3)
        inputs = jax.random.normal(k1, (16, 16, 16, 128), dtype=jnp.float32)
        kernel = jax.random.normal(k2, (3, 3, 128 // GROUPS, 128), dtype=jnp.float32) * 0.05
        bias = jax.random.normal(k3, (128,), dtype=jnp.float32) * 0.05
        return {'inputs': inputs, 'kernel': kernel, 'bias': bias}
    _L0_conv_all = _L0_conv_setup()
    _L0_conv_in = {k: v for k, v in _L0_conv_all.items() if k in ('kernel', 'bias')}
    del _L0_conv_all

    def _L0_ffn_setup():
        import jax, jax.numpy as jnp
        import numpy as np
        NUM_EXPERTS = 32
        GROUP_SIZE = 4
        NUM_GROUPS = NUM_EXPERTS // GROUP_SIZE
        C_CAP = 1.0
        key = jax.random.key(seed)
        ks = jax.random.split(key, 5)
        B, S, H = (16, 512, 128)
        D_FF = int(H * 4 * (2.0 / 3.0))
        x = jax.random.normal(ks[0], (B, S, H), dtype=jnp.float32)
        W_router = jax.random.normal(ks[1], (H, NUM_EXPERTS), dtype=jnp.float32) * (1.0 / np.sqrt(H))
        b_router = jnp.zeros((NUM_EXPERTS,), dtype=jnp.float32)
        W_up = jax.random.normal(ks[2], (NUM_GROUPS, H, D_FF), dtype=jnp.float32) * (1.0 / np.sqrt(H))
        b_up = jnp.zeros((NUM_GROUPS, D_FF), dtype=jnp.float32)
        W_down = jax.random.normal(ks[3], (NUM_EXPERTS, D_FF, H), dtype=jnp.float32) * (1.0 / np.sqrt(D_FF))
        b_down = jnp.zeros((NUM_EXPERTS, H), dtype=jnp.float32)
        return {'x': x, 'W_router': W_router, 'b_router': b_router, 'W_up': W_up, 'b_up': b_up, 'W_down': W_down, 'b_down': b_down}
    _L0_ffn_all = _L0_ffn_setup()
    _L0_ffn_in = {k: v for k, v in _L0_ffn_all.items() if k in ('W_router', 'b_router', 'W_up', 'b_up', 'W_down', 'b_down')}
    del _L0_ffn_all

    def _L1_conv_setup():
        import jax, jax.numpy as jnp
        import numpy as np
        D_MODEL = 128
        N_HEAD = 16
        HEAD_DIM = D_MODEL // N_HEAD
        SCALE = HEAD_DIM ** (-0.5)
        SIZE = (16, 16)
        WINDOW = (8, 8)
        SHIFT = (4, 4)
        WS = WINDOW[0] * WINDOW[1]
        NW = SIZE[0] // WINDOW[0] * (SIZE[1] // WINDOW[1])

        def _rel_pos_index(window):
            w0, w1 = window
            coords = np.stack(np.meshgrid(np.arange(w0), np.arange(w1), indexing='ij')).reshape(2, -1)
            rel = (coords[:, :, None] - coords[:, None, :]).transpose(1, 2, 0)
            rel[:, :, 0] += w0 - 1
            rel[:, :, 1] += w1 - 1
            rel[:, :, 0] *= 2 * w1 - 1
            return rel.sum(-1)

        def _shift_mask(size, window, shift):
            H, W = size
            w0, w1 = window
            s0, s1 = shift
            img = np.zeros((H, W))
            cnt = 0
            h_slices = (slice(0, -w0), slice(-w0, -s0), slice(-s0, None)) if s0 > 0 else (slice(None),)
            w_slices = (slice(0, -w1), slice(-w1, -s1), slice(-s1, None)) if s1 > 0 else (slice(None),)
            for hs in h_slices:
                for ws_ in w_slices:
                    img[hs, ws_] = cnt
                    cnt += 1
            win = img.reshape(H // w0, w0, W // w1, w1).transpose(0, 2, 1, 3).reshape(-1, w0 * w1)
            return (win[:, None, :] != win[:, :, None]).astype(np.float32)
        REL_IDX = jnp.asarray(_rel_pos_index(WINDOW))
        MASK = jnp.asarray(-100.0 * _shift_mask(SIZE, WINDOW, SHIFT))
        key = jax.random.key(seed)
        k1, k2, k3, k4 = jax.random.split(key, 4)
        x = jax.random.normal(k1, (8, SIZE[0], SIZE[1], D_MODEL), dtype=jnp.float32)
        qkv_w = jax.random.normal(k2, (3 * D_MODEL, D_MODEL), dtype=jnp.float32) * D_MODEL ** (-0.5)
        qkv_b = jax.random.normal(k3, (3 * D_MODEL,), dtype=jnp.float32) * 0.02
        bias_table = jax.random.normal(k4, ((2 * WINDOW[0] - 1) * (2 * WINDOW[1] - 1), N_HEAD), dtype=jnp.float32) * 0.02
        return {'x': x, 'qkv_w': qkv_w, 'qkv_b': qkv_b, 'bias_table': bias_table}
    _L1_conv_all = _L1_conv_setup()
    _L1_conv_in = {k: v for k, v in _L1_conv_all.items() if k in ('qkv_w', 'qkv_b', 'bias_table')}
    del _L1_conv_all

    def _L1_ffn_setup():
        import jax, jax.numpy as jnp
        import numpy as np
        NUM_EXPERTS = 8
        TOP_K = 2
        key = jax.random.key(seed)
        ks = jax.random.split(key, 5)
        B, T, D, H, E = (8, 1024, 128, 384, NUM_EXPERTS)
        scale = 0.02
        x = jax.random.normal(ks[0], (B, T, D), dtype=jnp.float32)
        gate_w = jax.random.normal(ks[1], (E, D), dtype=jnp.float32) * scale
        w1 = jax.random.normal(ks[2], (E, H, D), dtype=jnp.float32) * scale
        w3 = jax.random.normal(ks[3], (E, H, D), dtype=jnp.float32) * scale
        w2 = jax.random.normal(ks[4], (E, D, H), dtype=jnp.float32) * scale
        return {'x': x, 'gate_w': gate_w, 'w1': w1, 'w3': w3, 'w2': w2}
    _L1_ffn_all = _L1_ffn_setup()
    _L1_ffn_in = {k: v for k, v in _L1_ffn_all.items() if k in ('gate_w', 'w1', 'w3', 'w2')}
    del _L1_ffn_all
    return {'x': x, 'L0_conv_kernel': _L0_conv_in['kernel'], 'L0_conv_bias': _L0_conv_in['bias'], 'L0_ffn_W_router': _L0_ffn_in['W_router'], 'L0_ffn_b_router': _L0_ffn_in['b_router'], 'L0_ffn_W_up': _L0_ffn_in['W_up'], 'L0_ffn_b_up': _L0_ffn_in['b_up'], 'L0_ffn_W_down': _L0_ffn_in['W_down'], 'L0_ffn_b_down': _L0_ffn_in['b_down'], 'L1_conv_qkv_w': _L1_conv_in['qkv_w'], 'L1_conv_qkv_b': _L1_conv_in['qkv_b'], 'L1_conv_bias_table': _L1_conv_in['bias_table'], 'L1_ffn_gate_w': _L1_ffn_in['gate_w'], 'L1_ffn_w1': _L1_ffn_in['w1'], 'L1_ffn_w3': _L1_ffn_in['w3'], 'L1_ffn_w2': _L1_ffn_in['w2']}

def reference(x, L0_conv_kernel, L0_conv_bias, L0_ffn_W_router, L0_ffn_b_router, L0_ffn_W_up, L0_ffn_b_up, L0_ffn_W_down, L0_ffn_b_down, L1_conv_qkv_w, L1_conv_qkv_b, L1_conv_bias_table, L1_ffn_gate_w, L1_ffn_w1, L1_ffn_w3, L1_ffn_w2):
    import jax
    import jax.numpy as jnp

    def _L0_conv_ref(inputs, kernel, bias):
        import jax, jax.numpy as jnp
        import numpy as np
        GROUPS = 8
        STRIDES = (1, 1)
        DILATION = (1, 1)
        out = jax.lax.conv_general_dilated(inputs, kernel, window_strides=STRIDES, padding='SAME', rhs_dilation=DILATION, dimension_numbers=('NHWC', 'HWIO', 'NHWC'), feature_group_count=GROUPS)
        out = out + bias
        return jax.nn.relu(out)

    def _L0_ffn_ref(x, W_router, b_router, W_up, b_up, W_down, b_down):
        import jax, jax.numpy as jnp
        import numpy as np
        NUM_EXPERTS = 32
        GROUP_SIZE = 4
        NUM_GROUPS = NUM_EXPERTS // GROUP_SIZE
        C_CAP = 1.0
        B, S, H = x.shape
        bs = B * S
        E = NUM_EXPERTS
        k = min(int(bs * C_CAP) // E, bs)
        xf = x.reshape(bs, H)
        h = xf @ W_router + b_router
        Sm = jax.nn.softmax(h, axis=-1)
        G_ek, idx_ek = jax.lax.top_k(Sm.T, k)
        tokens = xf[idx_ek]
        D_FF = W_up.shape[-1]
        tok_g = tokens.reshape(NUM_GROUPS, GROUP_SIZE, k, H)
        up = jnp.einsum('gjkh,ghf->gjkf', tok_g, W_up) + b_up[:, None, None, :]
        act = jax.nn.silu(up).reshape(E, k, D_FF)
        Eout = jnp.einsum('ekf,efh->ekh', act, W_down) + b_down[:, None, :]
        weighted = G_ek[..., None] * Eout
        y = jnp.zeros((bs, H), dtype=x.dtype).at[idx_ek.reshape(-1)].add(weighted.reshape(-1, H))
        return y.reshape(B, S, H)

    def _L1_conv_ref(x, qkv_w, qkv_b, bias_table):
        import jax, jax.numpy as jnp
        import numpy as np
        D_MODEL = 128
        N_HEAD = 16
        HEAD_DIM = D_MODEL // N_HEAD
        SCALE = HEAD_DIM ** (-0.5)
        SIZE = (16, 16)
        WINDOW = (8, 8)
        SHIFT = (4, 4)
        WS = WINDOW[0] * WINDOW[1]
        NW = SIZE[0] // WINDOW[0] * (SIZE[1] // WINDOW[1])

        def _rel_pos_index(window):
            w0, w1 = window
            coords = np.stack(np.meshgrid(np.arange(w0), np.arange(w1), indexing='ij')).reshape(2, -1)
            rel = (coords[:, :, None] - coords[:, None, :]).transpose(1, 2, 0)
            rel[:, :, 0] += w0 - 1
            rel[:, :, 1] += w1 - 1
            rel[:, :, 0] *= 2 * w1 - 1
            return rel.sum(-1)

        def _shift_mask(size, window, shift):
            H, W = size
            w0, w1 = window
            s0, s1 = shift
            img = np.zeros((H, W))
            cnt = 0
            h_slices = (slice(0, -w0), slice(-w0, -s0), slice(-s0, None)) if s0 > 0 else (slice(None),)
            w_slices = (slice(0, -w1), slice(-w1, -s1), slice(-s1, None)) if s1 > 0 else (slice(None),)
            for hs in h_slices:
                for ws_ in w_slices:
                    img[hs, ws_] = cnt
                    cnt += 1
            win = img.reshape(H // w0, w0, W // w1, w1).transpose(0, 2, 1, 3).reshape(-1, w0 * w1)
            return (win[:, None, :] != win[:, :, None]).astype(np.float32)
        REL_IDX = jnp.asarray(_rel_pos_index(WINDOW))
        MASK = jnp.asarray(-100.0 * _shift_mask(SIZE, WINDOW, SHIFT))
        n, H, W, c = x.shape
        w0, w1 = WINDOW
        part = x.reshape(n, H // w0, w0, W // w1, w1, c)
        part = part.transpose(0, 1, 3, 2, 4, 5).reshape(n * NW, WS, c)
        qkv = (part @ qkv_w.T + qkv_b).reshape(n * NW, WS, 3, N_HEAD, HEAD_DIM)
        q, k, v = (qkv[:, :, 0] * SCALE, qkv[:, :, 1], qkv[:, :, 2])
        attn = jnp.einsum('wihd,wjhd->whij', q, k)
        bias = bias_table[REL_IDX].transpose(2, 0, 1)
        attn = attn.reshape(n, NW, N_HEAD, WS, WS) + bias[None, None] + MASK[None, :, None]
        attn = jax.nn.softmax(attn, axis=-1).reshape(n * NW, N_HEAD, WS, WS)
        out = jnp.einsum('whij,wjhd->wihd', attn, v).reshape(n * NW, WS, c)
        out = out.reshape(n, H // w0, W // w1, w0, w1, c)
        return out.transpose(0, 1, 3, 2, 4, 5).reshape(n, H, W, c)

    def _L1_ffn_ref(x, gate_w, w1, w3, w2):
        import jax, jax.numpy as jnp
        import numpy as np
        NUM_EXPERTS = 8
        TOP_K = 2
        B, T, D = x.shape
        E = gate_w.shape[0]
        xf = x.reshape(-1, D)
        N = xf.shape[0]
        gate_logits = xf @ gate_w.T
        weights, indices = jax.lax.top_k(gate_logits, TOP_K)
        weights = jax.nn.softmax(weights, axis=-1)
        combine = jnp.zeros((N, E), dtype=xf.dtype).at[jnp.arange(N)[:, None], indices].add(weights)
        out = jnp.zeros_like(xf)
        for e in range(E):
            h = jax.nn.silu(xf @ w1[e].T) * (xf @ w3[e].T)
            y = h @ w2[e].T
            out = out + combine[:, e:e + 1] * y
        return out.reshape(B, T, D)

    def _gn(v, G=32, eps=1e-05):
        B_, H_, W_, C_ = v.shape
        g = v.reshape(B_, H_, W_, G, C_ // G)
        m = jnp.mean(g, axis=(1, 2, 4), keepdims=True)
        s = jnp.var(g, axis=(1, 2, 4), keepdims=True)
        return ((g - m) / jnp.sqrt(s + eps)).reshape(v.shape)

    def _ln_c(v, eps=1e-06):
        m = jnp.mean(v, axis=-1, keepdims=True)
        s = jnp.var(v, axis=-1, keepdims=True)
        return (v - m) / jnp.sqrt(s + eps)

    def _ln_t(v, eps=1e-05):
        m = jnp.mean(v, axis=-1, keepdims=True)
        s = jnp.var(v, axis=-1, keepdims=True)
        return (v - m) / jnp.sqrt(s + eps)

    def _to_tokens(v):
        B_, H_, W_, C_ = v.shape
        return v.reshape(B_, H_ * W_, C_)

    def _from_tokens(t, like):
        return t.reshape(like.shape)
    x = x + _L0_conv_ref(_ln_c(x), L0_conv_kernel, L0_conv_bias)
    t = _to_tokens(x)
    t = t + _L0_ffn_ref(_ln_t(t), L0_ffn_W_router, L0_ffn_b_router, L0_ffn_W_up, L0_ffn_b_up, L0_ffn_W_down, L0_ffn_b_down)
    x = _from_tokens(t, x)
    x = x + _L1_conv_ref(_ln_c(x), L1_conv_qkv_w, L1_conv_qkv_b, L1_conv_bias_table)
    t = _to_tokens(x)
    t = t + _L1_ffn_ref(_ln_t(t), L1_ffn_gate_w, L1_ffn_w1, L1_ffn_w3, L1_ffn_w2)
    x = _from_tokens(t, x)
    return x

_drawn_inputs = setup_inputs


def setup_inputs(seed=0):
    import zlib

    import numpy as np

    out = dict(_drawn_inputs(seed))
    spreads = {'L0_ffn_b_router': (0.0, 0.495),
     'L0_ffn_b_up': (0.0, 0.714),
     'L0_ffn_b_down': (0.0, 0.434)}
    factors = {'L1_conv_qkv_b': 2.873,
     'L1_conv_bias_table': 8.0,
     'L1_ffn_gate_w': 8.0,
     'L1_ffn_w1': 8.0,
     'L1_ffn_w3': 8.0,
     'L1_ffn_w2': 8.0}
    for name, (base, spread) in spreads.items():
        noise = np.random.default_rng([zlib.crc32(name.encode()), seed]).standard_normal(out[name].shape)
        drawn = base * np.exp(spread * noise) if base else spread * noise
        out[name] = jnp.asarray(drawn.astype(out[name].dtype))
    for name, factor in factors.items():
        out[name] = (out[name] * factor).astype(out[name].dtype)
    return out
```

```python
from contextlib import ExitStack, contextmanager

import concourse.bass as bass
from concourse import mybir

F32 = mybir.dt.float32
F16 = mybir.dt.float16
I32 = mybir.dt.int32
BF16 = mybir.dt.bfloat16
ALU = mybir.AluOpType
ACT = mybir.ActivationFunctionType
AX = mybir.AxisListType

P = 128
IMAGES, SIDE = 16, 16
TOKENS = IMAGES * SIDE * SIDE
TILES = TOKENS // P
BLOCKS = TILES // 4
PAD = SIDE + 2
TAPS = 9
EXPERTS_B, GROUPS_B = 32, 8
CAP = TOKENS // EXPERTS_B
FF_B = 341
CHUNKS_B = [(0, 128), (128, 128), (256, FF_B - 256)]
ROW_B = P + EXPERTS_B
HEADS, HDIM, WIN = 16, 8, 64
SCALE = HDIM ** -0.5
EXPERTS_D, FF_D = 8, 384
CHUNKS_D = FF_D // P
PAIRS = 2 * TOKENS
TILES_D = PAIRS // P + EXPERTS_D
ID_SHIFT = 2048
BITS = 30
SEG = TOKENS // 4


def constants():
    import numpy as np
    p = np.arange(P)
    j, e = p // EXPERTS_B, p % EXPERTS_B
    parts = {}
    parts["ident"] = np.eye(P)
    parts["same_expert"] = e[:, None] == e[None, :]
    parts["earlier_segment"] = (e[:, None] == e[None, :]) & (j[:, None] < j[None, :])
    parts["head_of_8"] = (p[:, None] // HDIM) % 8 == np.arange(8)[None, :]
    parts["half"] = (p[:, None] // WIN) == np.arange(2)[None, :]
    u = np.arange(TILES)
    parts["token_id"] = ((u // 4 + 8 * (u % 4))[None, :] * P + p[:, None]) - ID_SHIFT
    parts["same_e16"] = p[:, None] % 16 == np.arange(16)[None, :]
    parts["tri"] = p[:, None] <= p[None, :]
    parts["rank8"] = np.broadcast_to(EXPERTS_D - np.arange(EXPERTS_D), (P, EXPERTS_D))
    parts["restart"] = np.broadcast_to(np.arange(EXPERTS_D * TILES) % TILES != 0, (P, EXPERTS_D * TILES))
    parts["tile_no"] = np.broadcast_to(np.arange(TILES_D), (P, TILES_D))
    parts["slot_hi"] = np.broadcast_to(np.tile(np.repeat(np.arange(8), 16), 2), (P, 8 * EXPERTS_B))
    parts["slot_lo"] = np.broadcast_to(np.repeat(np.arange(16), EXPERTS_B), (P, 16 * EXPERTS_B))
    at, cols, n = {}, [], 0
    for name, a in parts.items():
        at[name] = (n, n + a.shape[1])
        n += a.shape[1]
        cols.append(a.astype(np.float32))
    return np.ascontiguousarray(np.concatenate(cols, 1)), at


def window_mask():
    import numpy as np
    region = np.zeros((SIDE, SIDE))
    cuts = (slice(0, -8), slice(-8, -4), slice(-4, None))
    for a, hs in enumerate(cuts):
        for b, ws in enumerate(cuts):
            region[hs, ws] = 3 * a + b
    win = region.reshape(2, 8, 2, 8).transpose(0, 2, 1, 3).reshape(2, 2, WIN)
    return (-100.0 * (win[:, :, :, None] != win[:, :, None, :])).astype(np.float32).reshape(2, P, WIN)


class Tally:

    def __init__(self):
        self.base, self.steps, self.i, self.per = 0, 0, None, 0

    def next(self):
        self.steps += 1
        return self.now()

    def now(self):
        if self.i is None:
            return self.base + self.steps
        return self.i * self.per + (self.base + self.steps)

    @contextmanager
    def loop(self, eng, rounds, per):
        self.base, self.steps = self.base + self.steps, 0
        with eng.Fori(0, rounds) as i:
            self.i, self.per = i, per
            yield i
            assert self.steps == per, (self.steps, per)
        self.base, self.steps, self.i = self.base + rounds * per, 0, None


def staggered(eng, n, parts):
    def step(first, k):
        for fn, lag in parts:
            t = first + k - lag
            if not isinstance(t, int) or 0 <= t < n:
                fn(t, (k - lag) % 2)

    depth = max(lag for _, lag in parts)
    head = depth + depth % 2
    for k in range(head):
        step(0, k)
    with eng.Fori(0, (n - head) // 2) as i:
        for k in range(head, head + 2):
            for fn, lag in parts:
                fn(2 * i + (k - lag), (k - lag) % 2)
    for k in range(n, n + depth):
        step(0, k)


def rounds(eng, n, width, step, head=1, tail=1):
    for t in range(head * width):
        step(t, t % width)
    with eng.Fori(head, n // width - tail) as i:
        for k in range(width):
            step(width * i + k, k)
    for t in range(n - tail * width, n):
        step(t, t % width)


def metaformer(nc, const_at, x, conv_w, conv_b, w_router, router_bias, w_up, up_bias, w_down, down_bias,
               qkv_w, qk_bias, v_bias, rel_bias, mask, gate_w, w1, w3, w2, const, out, stop="D"):
    order = "ABCD"
    stages = order[:order.index(stop) + 1]
    with ExitStack() as ctx:
        def sb(name, shape, dt=F32):
            return ctx.enter_context(nc.sbuf_tensor(name, shape, dt))

        def sem(name):
            return ctx.enter_context(nc.semaphore(name))

        def dram(name, shape, dt=F32):
            return nc.dram_tensor(name, shape, dt, kind="Internal").ap()

        psum = ctx.enter_context(nc.psum_tensor("psum", [P, 8, 512], F32))

        table = dram("table", [TOKENS, ROW_B])
        y_even = dram("y_even", [TOKENS, P])
        y_odd = dram("y_odd", [TOKENS, P])
        rows_in = dram("rows_in", [TILES_D * P, P])
        rows_out = dram("rows_out", [TILES_D * P, P])

        x_tok = sb("x_tok", [P, TILES, P])
        extra = sb("extra", [P, TILES, P])
        scratch = sb("scratch", [P, 2 * BLOCKS * PAD * PAD])
        xpad = scratch[:, :].rearrange("p (n a b) -> p n a b", n=IMAGES, a=PAD)
        cst = sb("cst", [P, const.shape[1]])

        def C(name):
            a, b = const_at[name]
            return cst[:, a:b]

        ident = C("ident")
        zeros = sb("zeros", [P, 1024])
        ones_row = sb("ones_row", [1, P])
        arena = sb("arena", [P, 3 * 2 * HEADS * WIN])
        arena_b = sb("arena_b", [P, 2 * 3 * 512])

        def shared(pool_of, offset, shape, dt=F32):
            n = 1
            for d in shape[1:]:
                n *= d
            words = n // 2 if dt == F16 else n
            v = pool_of[:, offset:offset + words]
            if dt != F32:
                v = v.bitcast(dt)
            if len(shape) > 2:
                names = "abcdefg"[:len(shape) - 1]
                v = v.rearrange(f"p ({' '.join(names)}) -> p {' '.join(names)}",
                                **{c: d for c, d in zip(names, shape[1:])})
            return v, offset + words

        stats = sb("stats", [P, TILES, 6])
        mean = sb("mean", [P, TILES])
        gap = sb("gap", [P, TILES])
        spread = sb("spread", [P, TILES])
        var_eps = sb("var_eps", [P, TILES])
        std = sb("std", [P, TILES])
        rstd = sb("rstd", [P, TILES])
        xn = sb("xn", [P, 2, 4, P])
        xt = sb("xt", [P, 2, 512])
        conv_sb = sb("conv_sb", [P, TAPS, P])
        conv_bs = sb("conv_bs", [P, 1])
        conv_t = sb("conv_t", [P, 2, 512])

        wqkv = sb("wqkv", [P, 3 * P])
        qkb = sb("qkb", [P, 2])
        qb_scaled = sb("qb_scaled", [P, 1])
        vb_sb = sb("vb_sb", [P, P])
        rel = sb("rel", [P, 2, HEADS * WIN])
        msk = sb("msk", [P, 2, WIN])
        q_t = sb("q_t", [P, 2, P])
        k_x, _ = shared(arena_b, 0, [P, 2, 8, P])
        v_x = sb("v_x", [P, 2, 2, 8, 2, HDIM + 1])
        score, at = shared(arena, 0, [P, 2, HEADS * WIN])
        prob, at = shared(arena, at, [P, 2, HEADS * WIN])
        prob_t, at = shared(arena, at, [P, 2, HEADS * WIN])
        peak = sb("peak", [P, 2, HEADS])
        inv_sum = sb("inv_sum", [P, 2, HEADS])
        att = sb("att", [P, 2, P])

        gw = sb("gw", [P, EXPERTS_D])
        w1_sb = sb("w1_sb", [P, EXPERTS_D, FF_D])
        w3_sb = sb("w3_sb", [P, EXPERTS_D, FF_D])
        w2_sb = sb("w2_sb", [P, EXPERTS_D, CHUNKS_D, P])
        TE = [P, TILES, EXPERTS_D]
        lg = sb("lg", TE)
        hit = sb("hit", TE)
        first = sb("first", TE)
        second = sb("second", TE)
        chosen = sb("chosen", TE, BF16)
        tri_b = sb("tri_b", [P, P], BF16)
        ones_b = sb("ones_b", [P, P], BF16)
        peak1 = sb("peak1", [P, TILES])
        peak2 = sb("peak2", [P, TILES])
        rank = sb("rank", [P, TILES])
        ratio = sb("ratio", [P, TILES])
        weight1 = sb("weight1", [P, TILES])
        weight2 = sb("weight2", [P, TILES])
        n_tile = sb("n_tile", [P, EXPERTS_D, TILES])
        n_run = sb("n_run", [P, EXPERTS_D, TILES])
        tiles_i = sb("tiles_i", [P, EXPERTS_D], I32)
        tiles_f = sb("tiles_f", [P, EXPERTS_D])
        end_tile = sb("end_tile", [P, EXPERTS_D])
        base = sb("base", [P, EXPERTS_D])
        slot_f = sb("slot_f", TE)
        slot_of = sb("slot_of", [P, 2, TILES])
        slot_i = sb("slot_i", [P, 2, TILES], I32)
        past = sb("past", [P, TILES_D, EXPERTS_D])
        tile_e = sb("tile_e", [P, TILES_D])
        tile_ei = sb("tile_ei", [P, TILES_D], I32)
        rows_d, at = shared(arena, 0, [P, 4, P])
        xt_d, at = shared(arena, at, [P, 2, P])
        silu_d, at = shared(arena, at, [P, 2, FF_D])
        act_d, at = shared(arena, at, [P, 2, FF_D])
        act_dt, at = shared(arena, at, [P, 2, FF_D])
        y_d, at = shared(arena, at, [P, 2, P])
        back1 = extra
        back2 = scratch[:, 0:TILES * P].rearrange("p (t c) -> p t c", c=P)

        wr_sb = sb("wr_sb", [P, EXPERTS_B])
        br_sb = sb("br_sb", [P, EXPERTS_B])
        gate = sb("gate", [P, TILES, EXPERTS_B])
        top = sb("top", [P, TILES])
        total = sb("total", [P, TILES])
        inv = sb("inv", [P, TILES])
        by_expert = sb("by_expert", [P, SEG])
        above, tied, n_above, n_tied = (scratch[:, SEG * k:SEG * (k + 1)] for k in range(4))
        thr = sb("thr", [P, 1], I32)
        cand = sb("cand", [P, 1], I32)
        kept = sb("kept", [P, 1])
        bits = sb("bits", [P, BITS], I32)
        count = sb("count", [P, 2])
        offs = sb("offs", [P, 2])
        place, at = shared(arena_b, 0, [P, TILES, EXPERTS_B], I32)
        place2, at = shared(arena_b, at, [P, TILES, EXPERTS_B], I32)
        hi16, at = shared(arena_b, at, [P, TILES, EXPERTS_B], F16)
        lo16, at = shared(arena_b, at, [P, TILES, EXPERTS_B], F16)
        slot_hi = sb("slot_hi", [P, 2, 8, 16], F16)
        slot_lo = sb("slot_lo", [P, 16, EXPERTS_B], F16)
        oh_hi = sb("oh_hi", [P, 2, 2, 8, 16], F16)
        oh_id = sb("oh_id", [P, 2, 2, 8, 16], F16)
        oh_lo = sb("oh_lo", [P, 2, 16, EXPERTS_B], F16)
        picked = sb("picked", [P, 2, 16, 16])
        ids_f = sb("ids_f", [P, 2, 16])
        ids_e = sb("ids_e", [EXPERTS_B, P])
        idx = sb("idx", [P, EXPERTS_B], I32)
        rows_b, at = shared(arena, 0, [P, 2, 4, ROW_B])
        wu_sb, at = shared(arena, at, [P, 2, FF_B])
        wd_sb, at = shared(arena, at, [P, 2, 4, 3, P])
        bu_sb = sb("bu_sb", [P, GROUPS_B, 3])
        bd_sb = sb("bd_sb", [1, 2, 512])
        act_b, _ = shared(arena_b, 0, [P, 2, 3, 512])
        y_b, at = shared(arena, at, [P, 2, 4, P])

        ld_x = sem("ld_x")
        ld_w = sem("ld_w")
        dve_seq = sem("dve_seq")
        dve_n = Tally()
        s_zero = sem("s_zero")
        s_pad = sem("s_pad")

        a_sqrt, b_sqrt, c_sqrt, d_sqrt = (sem(f"{s}_sqrt") for s in "abcd")
        a_var, b_var, c_var, d_var = (sem(f"{s}_var") for s in "abcd")
        a_xn = sem("a_xn")
        a_tr = sem("a_tr")
        a_pad = sem("a_pad")
        a_conv = sem("a_conv")
        a_relu = sem("a_relu")
        a_back = sem("a_back")
        a_res = sem("a_res")

        b_xn, b_tr, b_xt, b_logit = (sem(f"b_{s}") for s in ("xn", "tr", "xt", "logit"))
        b_tab = [sem(f"b_tab{i}") for i in range(2)]
        b_sub, b_exp, b_gate, b_gtab, b_gtr, b_be = (sem(f"b_{s}") for s in ("sub", "exp", "gate", "gtab", "gtr", "be"))
        b_cnt, b_sum, b_tot, b_off, b_pos, b_ptr = (sem(f"b_{s}") for s in ("cnt", "sum", "tot", "off", "pos", "ptr"))
        b_oh, b_ohmm, b_ids, b_idd, b_idt, b_idx, b_bits = (
            sem(f"b_{s}") for s in ("oh", "ohmm", "ids", "idd", "idt", "idx", "bits"))
        b_xg, b_xgt, b_up, b_act, b_down, b_y = (
            sem(f"b_{s}") for s in ("xg", "xgt", "up", "act", "down", "y"))
        b_w = [sem(f"b_w{i}") for i in range(2)]
        b_gath = [sem(f"b_gath{i}") for i in range(2)]
        b_sc = [sem(f"b_sc{i}") for i in range(2)]
        b_init = sem("b_init")
        done = sem("done")
        (c_ld, c_sum, c_rel, c_one, c_xn, c_tr, c_xt, c_qkv, c_q, c_k, c_v, c_s, c_sb, c_mx, c_sub, c_exp, c_pt,
         c_pe, c_av, c_o, c_res, c_va, c_vb, c_qb) = (sem(f"c_{s}") for s in (
             "ld", "sum", "rel", "one", "xn", "tr", "xt", "qkv", "q", "k", "v", "s", "sb", "mx", "sub", "exp",
             "pt", "pe", "av", "o", "res", "va", "vb", "qb"))
        (d_zero, d_xn, d_tr, d_xt, d_log, d_dm, d_ex, d_sel, d_pre, d_slot, d_map, d_sc) = (
            sem(f"d_{s}") for s in ("zero", "xn", "tr", "xt", "log", "dm", "ex", "sel", "pre", "slot", "map", "sc"))
        e_tr, e_xt, e_h1, e_h3, e_silu, e_act, e_at, e_ate, e_yp, e_y = (
            sem(f"e_{s}") for s in ("tr", "xt", "h1", "h3", "silu", "act", "at", "ate", "yp", "y"))
        e_ld = [sem(f"e_ld{i}") for i in range(4)]
        e_st = [sem(f"e_st{i}") for i in range(2)]
        f_back = [sem(f"f_back{i}") for i in range(BLOCKS)]
        f_sum = sem("f_sum")

        x_v = x.rearrange("(t p) c -> p t c", p=P)
        out_v = out.rearrange("(t p) c -> p t c", p=P)

        block = ctx.enter_context(nc.Block())

        LOADS = [(cst[:], const), (conv_sb[:], conv_w.rearrange("p (t c) -> p t c", t=TAPS)), (conv_bs[:], conv_b),
                 (wr_sb[:], w_router), (br_sb[:], router_bias.partition_broadcast(P)), (bu_sb[:], up_bias),
                 (wqkv[:], qkv_w), (qkb[:], qk_bias), (vb_sb[:], v_bias.partition_broadcast(P)), (rel[:, 0, :], rel_bias),
                 (rel[:, 1, :], rel_bias), (msk[:], mask.rearrange("h p j -> p h j")), (gw[:], gate_w),
                 (w1_sb[:], w1), (w3_sb[:], w3), (w2_sb[:], w2)]

        @block.sync
        def _(sp):
            for c in range(4):
                sp.dma_start(x_tok[:, 8 * c:8 * c + 8, :], x_v[:, 8 * c:8 * c + 8, :]).then_inc(ld_x, 16)
            for dst, src in LOADS:
                sp.dma_start(dst, src).then_inc(ld_w, 16)
            if "B" in stages:
                sp.wait_ge(s_zero, 1)
                for c in range(4):
                    sp.dma_start(y_odd.rearrange("(p r) c -> p (r c)", p=P)[:, 1024 * c:1024 * (c + 1)],
                                 zeros[:]).then_inc(b_init, 16)
                sp.wait_ge(a_res, 2 + BLOCKS)
                sp.dma_start(y_even.rearrange("(t p) c -> p t c", p=P), x_tok[:]).then_inc(b_init, 16)
                tab_v = table.rearrange("(t p) c -> p t c", p=P)
                for b in range(2):
                    sp.sem_inc(b_tab[b], 16)
                with sp.Fori(0, BLOCKS // 2) as i:
                    for b in range(2):
                        sp.wait_ge(b_xn, 2 * i + b + 1)
                        sp.dma_start(tab_v[:, bass.ds(8 * i + 4 * b, 4), 0:P], xn[:, b]).then_inc(b_tab[b], 16)
                sp.wait_ge(b_gate, 1)
                for j in range(4):
                    sp.dma_start(tab_v[:, 8 * j:8 * j + 8, P:ROW_B], gate[:, j:TILES:4, :]).then_inc(b_gtab, 16)
                wd_v = w_down.rearrange("p (g e k c) -> p g e k c", g=GROUPS_B, e=4, k=3)
                with sp.Fori(0, GROUPS_B // 2) as i:
                    for b in range(2):
                        sp.wait_ge(b_down, 2 * i + b + 1)
                        sp.dma_start(wu_sb[:, b, :], w_up[:, bass.ds(2 * i + b, 1), :]).then_inc(b_w[b], 16)
                        sp.dma_start(wd_sb[:, b], wd_v[:, bass.ds(2 * i + b, 1)]).then_inc(b_w[b], 16)
                        sp.dma_start(bd_sb[:, b, :], down_bias[bass.ds(2 * i + b, 1), :]).then_inc(b_w[b], 16)
            if stop == "A":
                sp.wait_ge(a_res, 2 + BLOCKS)
                sp.dma_start(out_v, x_tok[:]).then_inc(done, 16)
                sp.wait_ge(done, 16)
            if "C" in stages:
                for k in range(2):
                    sp.wait_ge(b_sc[k], 16 * 16)
                for dst, src in ((x_tok, y_even), (extra, y_odd)):
                    src_v = src.rearrange("(t r w c) k -> w r c t k", r=8, w=2, c=8)
                    for w in range(2):
                        for r in range(8):
                            at = WIN * w + 8 * r
                            sp.dma_start(dst[at:at + 8], src_v[w, r]).then_inc(c_ld, 16)
            if "D" in stages:
                sp.wait_ge(s_zero, 1)
                zero_v = rows_in.rearrange("(p r) c -> p (r c)", p=P)
                for c in range(9):
                    sp.dma_start(zero_v[:, 1024 * c:1024 * (c + 1)], zeros[:]).then_inc(d_zero, 16)
                in_v = rows_in.rearrange("(t p) c -> p t c", p=P)
                out_t = rows_out.rearrange("(t p) c -> p t c", p=P)
                sp.wait_ge(d_sc, 16 * 2 * TILES)
                for b in range(2):
                    sp.sem_inc(e_st[b], 16)
                for b in range(4):
                    sp.dma_start(rows_d[:, b, :], in_v[:, b, :]).then_inc(e_ld[b], 16)

                def move(t, b):
                    sp.wait_ge(e_y, 1 + t + 1)
                    sp.dma_start(out_t[:, bass.ds(t, 1), :], y_d[:, b % 2:b % 2 + 1, :]).then_inc(e_st[b % 2], 16)
                    if not (isinstance(t, int) and t + 4 >= TILES_D):
                        sp.wait_ge(e_tr, t + 1)
                        sp.dma_start(rows_d[:, b:b + 1, :], in_v[:, bass.ds(t + 4, 1), :]).then_inc(e_ld[b], 16)

                rounds(sp, TILES_D, 4, move, head=0)
            out_w = out.rearrange("(t r w c) k -> w r c t k", r=8, w=2, c=8)

            def store(n):
                for w in range(2):
                    for r in range(8):
                        at = WIN * w + 8 * r
                        sp.dma_start(out_w[w, r], x_tok[at:at + 8]).then_inc(done, 16)
                sp.wait_ge(done, 16 * 16)

            if stop == "A":
                sp.wait_ge(a_res, 2 + BLOCKS)
                sp.dma_start(out_v, x_tok[:]).then_inc(done, 16)
                sp.wait_ge(done, 16)
            if stop == "B":
                for k in range(2):
                    sp.wait_ge(b_sc[k], 16 * 16)
                sp.dma_start(x_tok[:], y_even.rearrange("(t p) c -> p t c", p=P)).then_inc(done, 16)
                sp.dma_start(extra[:], y_odd.rearrange("(t p) c -> p t c", p=P)).then_inc(done, 16)
                sp.wait_ge(d_var, 1)
                sp.dma_start(out_v, x_tok[:]).then_inc(done, 16)
                sp.wait_ge(done, 48)
            if stop == "C":
                sp.wait_ge(c_res, 2 + TILES)
                store(0)
            if stop == "D":
                sp.wait_ge(f_sum, 2 * TILES)
                store(0)

        @block.gpsimd
        def _(pool):
            nc.gpsimd.memset(scratch[:], 0.0).then_inc(s_pad, 1)
            nc.gpsimd.memset(ones_row[:], 1.0).then_inc(s_pad, 1)
            nc.gpsimd.memset(zeros[:], 0.0).then_inc(s_zero, 1)
            if "B" in stages:
                for k in range(BITS):
                    nc.gpsimd.memset(bits[:, k:k + 1], 1 << (BITS - 1 - k)).then_inc(b_bits, 1)

                for b in range(2):
                    pool.wait_ge(b_tab[b], 16 + 8 * BLOCKS)
                pool.wait_ge(b_gtab, 64)
                pool.wait_ge(b_idx, 1)
                pool.wait_ge(b_init, 16 * 5)
                for g in range(GROUPS_B + 1):
                    if g < GROUPS_B:
                        pool.wait_ge(b_y, g + 1)
                        for k in range(4):
                            nc.gpsimd.indirect_dma_start(
                                out=rows_b[:, g % 2, k, :], out_offset=None, in_=table[:, :],
                                in_offset=bass.IndirectOffsetOnAxis(ap=idx[:, 4 * g + k:4 * g + k + 1], axis=0),
                                bounds_check=TOKENS - 1, oob_is_err=True,
                            ).then_inc(b_gath[g % 2], 16)
                    if g > 0:
                        pool.wait_ge(b_y, g + 2)
                        for k in range(4):
                            e = 4 * (g - 1) + k
                            if e > 1:
                                pool.wait_ge(b_sc[k % 2], 16 * (e // 2))
                            nc.gpsimd.indirect_dma_start(
                                out=(y_even, y_odd)[k % 2][:, :],
                                out_offset=bass.IndirectOffsetOnAxis(ap=idx[:, e:e + 1], axis=0),
                                in_=y_b[:, (g - 1) % 2, k, :], in_offset=None, bounds_check=TOKENS - 1,
                                oob_is_err=True, compute_op=ALU.add,
                            ).then_inc(b_sc[k % 2], 16)

            if "C" in stages:
                pool.sem_inc(c_res, 2)

                def value_bias(t, b):
                    pool.wait_ge(c_xn, t + 1)
                    xs = x_tok[:, bass.ds(t, 1), :]
                    nc.gpsimd.tensor_tensor(xs, xs, vb_sb[:].unsqueeze(1), ALU.add).then_inc(c_vb, 1)

                def values(t, b):
                    pool.wait_ge(c_va, t + 1)
                    pool.wait_ge(c_av, t + 1)
                    nc.gpsimd.tensor_tensor(
                        v_x[:, b, :, :, :, 0:HDIM].rearrange("p w a h d -> p (w a) h d"),
                        extra[:, bass.ds(t, 1), :].rearrange("p o (a d) -> p (o a) d", d=HDIM).unsqueeze(2)
                        .to_broadcast([P, 16, 2, HDIM]),
                        C("half").unsqueeze(1).unsqueeze(3).to_broadcast([P, 16, 2, HDIM]), ALU.mult).then_inc(c_v, 1)

                def minus_peak(t, b):
                    pool.wait_ge(c_mx, t + 1)
                    v = score[:, b, :].rearrange("p (h j) -> p h j", j=WIN)
                    nc.gpsimd.tensor_tensor(v, v, peak[:, b, :].unsqueeze(2).to_broadcast([P, HEADS, WIN]),
                                            ALU.subtract).then_inc(c_sub, 1)

                def residual(t, b):
                    pool.wait_ge(c_o, 7 + t + 1)
                    pool.wait_ge(c_vb, t + 1)
                    xs = x_tok[:, bass.ds(t, 1), :]
                    nc.gpsimd.tensor_tensor(xs, xs, att[:, b:b + 1, :], ALU.add).then_inc(c_res, 1)

                staggered(pool, TILES, [(residual, 8), (values, 6), (minus_peak, 4), (value_bias, 1)])
            if "D" in stages:
                pool.wait_ge(d_zero, 16 * 9)
                pool.wait_ge(d_slot, 1)
                for t in range(TILES):
                    for k in range(2):
                        nc.gpsimd.indirect_dma_start(
                            out=rows_in[:, :],
                            out_offset=bass.IndirectOffsetOnAxis(ap=slot_i[:, k, t:t + 1], axis=0),
                            in_=extra[:, t, :], in_offset=None, bounds_check=TILES_D * P - 1, oob_is_err=True,
                        ).then_inc(d_sc, 16)
                for b in range(2):
                    pool.wait_ge(e_st[b], 16 + 16 * TILES_D // 2)
                for t in range(TILES):
                    for k, dst in enumerate((back1, back2)):
                        nc.gpsimd.indirect_dma_start(
                            out=dst[:, t, :], out_offset=None, in_=rows_out[:, :],
                            in_offset=bass.IndirectOffsetOnAxis(ap=slot_i[:, k, t:t + 1], axis=0),
                            bounds_check=TILES_D * P - 1, oob_is_err=True,
                        ).then_inc(f_back[t // 4], 16)

        @block.vector
        def _(dve):
            def norm_stats(var_ready, sqrt_done, eps):
                dve.wait_ge(dve_seq, dve_n.now())
                with dve_n.loop(dve, TILES, 1) as t:
                    nc.vector.bn_stats(stats[:, bass.ds(t, 1), :], x_tok[:, bass.ds(t, 1), :]).then_inc(dve_seq, 1)
                    dve_n.next()
                dve.wait_ge(dve_seq, dve_n.now())
                even, odd = stats[:, :, 1], stats[:, :, 4]
                nc.vector.tensor_tensor(gap[:], even, odd, ALU.subtract).then_inc(dve_seq, 1)
                nc.vector.tensor_tensor(mean[:], even, odd, ALU.add).then_inc(dve_seq, 1)
                nc.vector.tensor_tensor(spread[:], stats[:, :, 2], stats[:, :, 5], ALU.add).then_inc(dve_seq, 1)
                for _ in range(3):
                    dve_n.next()
                dve.wait_ge(dve_seq, dve_n.now())
                nc.vector.tensor_scalar(mean[:], mean[:], 0.5, None, ALU.mult).then_inc(dve_seq, 1)
                nc.vector.scalar_tensor_tensor(gap[:], gap[:], 0.25, gap[:], ALU.mult, ALU.mult).then_inc(dve_seq, 1)
                nc.vector.tensor_scalar(spread[:], spread[:], 1.0 / P, eps, ALU.mult, ALU.add).then_inc(dve_seq, 1)
                for _ in range(3):
                    dve_n.next()
                dve.wait_ge(dve_seq, dve_n.now())
                nc.vector.tensor_tensor(var_eps[:], spread[:], gap[:], ALU.add).then_inc(var_ready, 1)
                dve.wait_ge(sqrt_done, 1)
                nc.vector.reciprocal(rstd[:], std[:]).then_inc(dve_seq, 1)
                dve.wait_ge(dve_seq, dve_n.next())

            def norm(dst, t):
                return nc.vector.tensor_scalar(dst, x_tok[:, bass.ds(t, 1), :], mean[:, bass.ds(t, 1)],
                                               rstd[:, bass.ds(t, 1)], ALU.subtract, ALU.mult)

            dve.wait_ge(ld_x, 64)
            norm_stats(a_var, a_sqrt, 1e-6)
            with dve.Fori(0, BLOCKS // 2) as i:
                for b in range(2):
                    dve.wait_ge(a_tr, 2 * i + b + 1)
                    for k in range(4):
                        ins = norm(xn[:, b, k, :], 8 * i + 4 * b + k)
                    ins.then_inc(a_xn, 1)
            dve.sem_inc(a_res, 2)
            with dve.Fori(0, BLOCKS // 2) as i:
                for b in range(2):
                    dve.wait_ge(a_back, 2 + 2 * i + b + 1)
                    xs = x_tok[:, bass.ds(8 * i + 4 * b, 4), :]
                    nc.vector.tensor_tensor(xs, psum[:, 4 + b, :].rearrange("p (t c) -> p t c", c=P), xs,
                                            ALU.add).then_inc(a_res, 1)
            if "B" not in stages:
                return

            dve.wait_ge(a_res, 2 + BLOCKS)
            norm_stats(b_var, b_sqrt, 1e-5)
            with dve.Fori(0, BLOCKS // 2) as i:
                for b in range(2):
                    dve.wait_ge(b_tr, 2 * i + b + 1)
                    dve.wait_ge(b_tab[b], 16 * i + 16)
                    for k in range(4):
                        ins = norm(xn[:, b, k, :], 8 * i + 4 * b + k)
                    ins.then_inc(b_xn, 1)
            dve.wait_ge(b_logit, BLOCKS)
            dve.wait_ge(ld_w, 16 * len(LOADS))
            logits = psum[:, 6:8, :].rearrange("p a (t e) -> p (a t) e", e=EXPERTS_B)
            nc.vector.tensor_tensor(gate[:].rearrange("p (g j) e -> p g j e", j=4),
                                    logits.rearrange("p (j g) e -> p g j e", j=4),
                                    br_sb[:].unsqueeze(1).unsqueeze(1).to_broadcast([P, 8, 4, EXPERTS_B]),
                                    ALU.add).then_inc(dve_seq, 1)
            dve.wait_ge(dve_seq, dve_n.next())
            nc.vector.tensor_reduce(top[:], gate[:], AX.X, ALU.max).then_inc(dve_seq, 1)
            dve.wait_ge(dve_seq, dve_n.next())
            nc.vector.tensor_tensor(gate[:], gate[:], top[:].unsqueeze(2).to_broadcast([P, TILES, EXPERTS_B]),
                                    ALU.subtract).then_inc(b_sub, 1)
            dve.wait_ge(b_exp, 1)
            nc.vector.tensor_reduce(total[:], gate[:], AX.X, ALU.add).then_inc(dve_seq, 1)
            dve.wait_ge(dve_seq, dve_n.next())
            nc.vector.reciprocal(inv[:], total[:]).then_inc(dve_seq, 1)
            dve.wait_ge(dve_seq, dve_n.next())
            nc.vector.tensor_tensor(gate[:], gate[:], inv[:].unsqueeze(2).to_broadcast([P, TILES, EXPERTS_B]),
                                    ALU.mult).then_inc(b_gate, 1)

            dve.wait_ge(b_gtr, 2)
            nc.vector.tensor_copy(by_expert[:].rearrange("p (a n) -> p a n", a=2), psum[:, 0:2, :]).then_inc(b_be, 1)
            nc.vector.memset(thr[:], 0).then_inc(dve_seq, 1)
            dve_n.next()
            dve.wait_ge(b_be, 1)
            dve.wait_ge(b_bits, BITS)
            with dve_n.loop(dve, BITS, 3) as i:
                dve.wait_ge(dve_seq, dve_n.now())
                nc.vector.tensor_tensor(cand[:], thr[:], bits[:, bass.ds(i, 1)], ALU.bitwise_or).then_inc(dve_seq, 1)
                dve.wait_ge(dve_seq, dve_n.next())
                nc.vector.tensor_scalar(above, by_expert[:], cand[:].bitcast(F32), None, ALU.is_ge, ALU.add,
                                        accum_out=count[:, 0:1]).then_inc(b_cnt, 1)
                dve.wait_ge(b_sum, i + 1)
                nc.vector.tensor_scalar(kept[:], psum[:, 2, 0:1], float(CAP), cand[:].bitcast(F32), ALU.is_ge,
                                        ALU.mult).then_inc(dve_seq, 1)
                dve.wait_ge(dve_seq, dve_n.next())
                nc.vector.tensor_tensor(thr[:].bitcast(F32), thr[:].bitcast(F32), kept[:], ALU.max).then_inc(dve_seq, 1)
                dve_n.next()
            dve.wait_ge(dve_seq, dve_n.now())
            nc.vector.tensor_scalar(above, by_expert[:], thr[:].bitcast(F32), None, ALU.is_gt, ALU.add,
                                    accum_out=count[:, 0:1]).then_inc(b_tot, 1)
            nc.vector.tensor_scalar(tied, by_expert[:], thr[:].bitcast(F32), None, ALU.is_equal, ALU.add,
                                    accum_out=count[:, 1:2]).then_inc(b_tot, 1)
            dve.wait_ge(b_tot, 2)
            nc.vector.tensor_tensor_scan(n_above, zeros[:], above, 0.0, ALU.add, ALU.add).then_inc(dve_seq, 1)
            dve_n.next()
            nc.vector.tensor_tensor_scan(n_tied, zeros[:], tied, 0.0, ALU.add, ALU.add).then_inc(dve_seq, 1)
            dve_n.next()
            dve.wait_ge(b_off, 1)
            nc.vector.tensor_copy(offs[:], psum[:, 3, 0:2]).then_inc(dve_seq, 1)
            dve.wait_ge(dve_seq, dve_n.next())
            nc.vector.scalar_tensor_tensor(n_above, n_above, offs[:, 0:1], above, ALU.add, ALU.mult).then_inc(dve_seq, 1)
            dve_n.next()
            nc.vector.scalar_tensor_tensor(n_tied, n_tied, offs[:, 1:2], tied, ALU.add, ALU.mult).then_inc(dve_seq, 1)
            dve.wait_ge(dve_seq, dve_n.next())
            nc.vector.scalar_tensor_tensor(n_above, n_above, -1.0, n_tied, ALU.add, ALU.add).then_inc(b_pos, 1)

            dve.wait_ge(b_ptr, 2)
            nc.vector.tensor_copy(place[:].rearrange("p (a t) e -> p a (t e)", a=2), psum[:, 0:2, :]).then_inc(dve_seq, 1)
            dve_n.next()
            nc.vector.tensor_copy(slot_hi[:].rearrange("p h a e -> p (h a e)"), C("slot_hi")).then_inc(dve_seq, 1)
            dve_n.next()
            nc.vector.tensor_copy(slot_lo[:].rearrange("p a e -> p (a e)"), C("slot_lo")).then_inc(dve_seq, 1)
            dve.wait_ge(dve_seq, dve_n.next())
            nc.vector.tensor_scalar(place2[:], place[:], 4, None, ALU.arith_shift_right).then_inc(dve_seq, 1)
            dve.wait_ge(dve_seq, dve_n.next())
            nc.vector.tensor_copy(hi16[:], place2[:]).then_inc(dve_seq, 1)
            dve.wait_ge(dve_seq, dve_n.next())
            nc.vector.tensor_scalar(place2[:], place[:], 15, None, ALU.bitwise_and).then_inc(dve_seq, 1)
            dve.wait_ge(dve_seq, dve_n.next())
            nc.vector.tensor_copy(lo16[:], place2[:]).then_inc(dve_seq, 1)
            dve.wait_ge(dve_seq, dve_n.next())
            with dve_n.loop(dve, TILES // 2, 2) as i:
                for b in range(2):
                    u = 2 * i + b
                    dve.wait_ge(b_ohmm, u + 1)
                    nc.vector.tensor_tensor(oh_hi[:, b], hi16[:, bass.ds(u, 1), :].rearrange("p o (h e) -> p (o h) e", h=2)
                                            .unsqueeze(2).to_broadcast([P, 2, 8, 16]),
                                            slot_hi[:], ALU.is_equal).then_inc(dve_seq, 1)
                    nc.vector.tensor_tensor(oh_lo[:, b], lo16[:, bass.ds(u, 1), :].to_broadcast([P, 16, EXPERTS_B]),
                                            slot_lo[:], ALU.is_equal)
                    dve.wait_ge(dve_seq, dve_n.next())
                    a0 = const_at["token_id"][0]
                    nc.vector.tensor_scalar(oh_id[:, b].rearrange("p h a e -> p (h a e)"), oh_hi[:, b].rearrange("p h a e -> p (h a e)"), cst[:, bass.ds(u + a0, 1)], None,
                                            ALU.mult).then_inc(b_oh, 1)
            dve.wait_ge(b_ohmm, 2 + TILES)
            for h in range(2):
                nc.vector.tensor_tensor(picked[:, h], psum[:, 4 + h, 0:256].rearrange("p (l e) -> p l e", e=16),
                                        C("same_e16").unsqueeze(1).to_broadcast([P, 16, 16]),
                                        ALU.mult).then_inc(dve_seq, 1)
                dve_n.next()
            dve.wait_ge(dve_seq, dve_n.now())
            nc.vector.tensor_reduce(ids_f[:], picked[:], AX.X, ALU.add).then_inc(dve_seq, 1)
            dve.wait_ge(dve_seq, dve_n.next())
            nc.vector.tensor_scalar(ids_f[:], ids_f[:], float(ID_SHIFT), None, ALU.add).then_inc(b_ids, 1)
            dve.wait_ge(b_idt, 1)
            nc.vector.tensor_copy(idx[:], psum[:, 2, 0:EXPERTS_B]).then_inc(b_idx, 1)

            dve.sem_inc(b_y, 2)
            dve.sem_inc(b_xgt, 2)

            def experts(g, b, reused):
                dve.wait_ge(b_xg, g + 1)
                nc.vector.tensor_copy(xt[:, b, :], psum[:, b, :]).then_inc(b_xgt, 1)
                dve.wait_ge(b_down, g + 3)
                if reused:
                    for k in range(2):
                        dve.wait_ge(b_sc[k], 32 * g - 32)
                for k in range(4):
                    e = 4 * g + k
                    ins = nc.vector.tensor_scalar(y_b[:, b, k, :], psum[:, 5 + b, P * k:P * (k + 1)],
                                                  rows_b[:, b, k, bass.ds(P + e, 1)], None, ALU.mult)
                ins.then_inc(b_y, 1)

            for b in range(2):
                experts(b, b, False)
            with dve.Fori(1, GROUPS_B // 2) as i:
                for b in range(2):
                    experts(2 * i + b, b, True)
            if stop == "B":
                dve.wait_ge(done, 32)
                nc.vector.tensor_tensor(x_tok[:], x_tok[:], extra[:], ALU.add).then_inc(d_var, 1)
            if "C" not in stages:
                return

            def heads(ap):
                return ap.rearrange("p (h j) -> p h j", j=WIN)

            for w in range(2):
                nc.vector.tensor_tensor(heads(rel[:, w, :]), heads(rel[:, w, :]),
                                        msk[:, w, :].unsqueeze(1).to_broadcast([P, HEADS, WIN]),
                                        ALU.add).then_inc(c_rel, 1)
                nc.vector.tensor_copy(v_x[:, w, :, :, :, HDIM].rearrange("p w a h -> p (w a) h"),
                                      C("half").unsqueeze(1).to_broadcast([P, 16, 2])).then_inc(c_one, 1)
            dve.wait_ge(c_rel, 2)
            dve.wait_ge(c_ld, 16 * 32)
            nc.vector.tensor_tensor(x_tok[:], x_tok[:], extra[:], ALU.add).then_inc(c_sum, 1)
            dve.wait_ge(c_sum, 1)
            norm_stats(c_var, c_sqrt, 1e-6)
            dve.sem_inc(c_k, 1)
            dve.sem_inc(c_sb, 2)
            dve.sem_inc(c_o, 7)

            def norm_tile(t, b):
                dve.wait_ge(c_tr, t + 1)
                norm(xn[:, b, 0, :], t).then_inc(c_xn, 1)

            def keys(t, b):
                dve.wait_ge(c_q, t + 1)
                dve.wait_ge(c_va, t + 1)
                dve.wait_ge(c_s, t + 1)
                nc.vector.scalar_tensor_tensor(k_x[:, b], psum[:, 1, P:2 * P].unsqueeze(1).to_broadcast([P, 8, P]),
                                               qkb[:, 1:2], C("head_of_8").unsqueeze(2).to_broadcast([P, 8, P]),
                                               ALU.add, ALU.mult).then_inc(c_k, 1)

            def add_bias(t, b):
                dve.wait_ge(c_s, 2 + t + 1)
                dve.wait_ge(c_exp, t + 1)
                nc.vector.tensor_tensor(score[:, b, :].rearrange("p (q n) -> p q n", q=2),
                                        psum[:, 2 + 2 * b:4 + 2 * b, :],
                                        rel[:, b, :].rearrange("p (q n) -> p q n", q=2), ALU.add).then_inc(c_sb, 1)

            def find_peak(t, b):
                dve.wait_ge(c_sb, 2 + t + 1)
                nc.vector.tensor_reduce(peak[:, b, :], heads(score[:, b, :]), AX.X, ALU.max).then_inc(c_mx, 1)

            def normalize(t, b):
                dve.wait_ge(c_av, 2 + t + 1)
                dve.wait_ge(c_res, t + 1)
                o = psum[:, 0, P:P + HEADS * (HDIM + 1)].rearrange("p (h d) -> p h d", d=HDIM + 1)
                nc.vector.reciprocal(inv_sum[:, b, :], o[:, :, HDIM]).then_inc(c_one, 1)
                dve.wait_ge(c_one, 2 + t + 1)
                nc.vector.tensor_tensor(att[:, b, :].rearrange("p (h d) -> p h d", d=HDIM), o[:, :, 0:HDIM],
                                        inv_sum[:, b, :].unsqueeze(2).to_broadcast([P, HEADS, HDIM]),
                                        ALU.mult).then_inc(c_o, 1)

            staggered(dve, TILES, [(add_bias, 4), (normalize, 8), (keys, 2), (find_peak, 4), (norm_tile, 0)])
            if "D" not in stages:
                return

            dve.wait_ge(c_res, 2 + TILES)
            norm_stats(d_var, d_sqrt, 1e-5)
            with dve.Fori(0, BLOCKS) as i:
                for k in range(4):
                    ins = norm(extra[:, bass.ds(4 * i + k, 1), :], 4 * i + k)
                ins.then_inc(d_xn, 1)

            def link(ins):
                ins.then_inc(dve_seq, 1)
                dve.wait_ge(dve_seq, dve_n.next())

            def wide(ap):
                return ap.unsqueeze(2).to_broadcast(TE)

            rank8 = C("rank8").unsqueeze(1).to_broadcast(TE)
            dve.wait_ge(d_log, BLOCKS)
            nc.vector.tensor_copy(tri_b[:], C("tri"))
            nc.vector.memset(ones_b[:], 1.0)
            link(nc.vector.tensor_copy(lg[:].rearrange("p t e -> p (t e)"), psum[:, 2, 0:TILES * EXPERTS_D]))

            def best(top_of, onehot):
                link(nc.vector.tensor_reduce(top_of[:], lg[:], AX.X, ALU.max))
                link(nc.vector.tensor_tensor(hit[:], lg[:], wide(top_of[:]), ALU.is_equal))
                link(nc.vector.tensor_tensor(hit[:], hit[:], rank8, ALU.mult))
                link(nc.vector.tensor_reduce(rank[:], hit[:], AX.X, ALU.max))
                link(nc.vector.tensor_tensor(onehot[:], rank8, wide(rank[:]), ALU.is_equal))

            best(peak1, first)
            link(nc.vector.scalar_tensor_tensor(lg[:], first[:], -3.0e38, lg[:], ALU.mult, ALU.add))
            best(peak2, second)
            nc.vector.tensor_tensor(ratio[:], peak2[:], peak1[:], ALU.subtract).then_inc(d_dm, 1)
            nc.vector.tensor_tensor(chosen[:], first[:], second[:], ALU.add).then_inc(d_sel, 1)
            dve.wait_ge(d_ex, 1)
            link(nc.vector.tensor_scalar(weight2[:], ratio[:], 1.0, None, ALU.add))
            link(nc.vector.reciprocal(weight1[:], weight2[:]))
            link(nc.vector.tensor_tensor(weight2[:], ratio[:], weight1[:], ALU.mult))
            dve.wait_ge(d_pre, 1)
            inside = psum[:, 3, 0:256].rearrange("p (t e) -> p t e", e=EXPERTS_D)
            link(nc.vector.tensor_copy(n_tile[:], psum[:, 3, 256:512].rearrange("p (t e) -> p e t", e=EXPERTS_D)))
            link(nc.vector.tensor_tensor_scan(n_run[:].rearrange("p e t -> p (e t)"), C("restart"),
                                              n_tile[:].rearrange("p e t -> p (e t)"), 0.0, ALU.mult, ALU.add))
            link(nc.vector.tensor_scalar(tiles_i[:], n_run[:, :, TILES - 1], float(P - 1), None, ALU.add))
            link(nc.vector.tensor_scalar(tiles_i[:], tiles_i[:], 7, None, ALU.arith_shift_right))
            link(nc.vector.tensor_copy(tiles_f[:], tiles_i[:]))
            link(nc.vector.tensor_tensor_scan(end_tile[:], zeros[:, 0:EXPERTS_D], tiles_f[:], 0.0, ALU.add, ALU.add))
            link(nc.vector.tensor_tensor(base[:], end_tile[:], tiles_f[:], ALU.subtract))
            link(nc.vector.tensor_scalar(base[:], base[:], float(P), -1.0, ALU.mult, ALU.add))
            link(nc.vector.tensor_tensor(n_run[:], n_run[:], n_tile[:], ALU.subtract))
            link(nc.vector.tensor_tensor(n_run[:], n_run[:], base[:].unsqueeze(2).to_broadcast([P, EXPERTS_D, TILES]),
                                         ALU.add))
            link(nc.vector.tensor_tensor(slot_f[:], inside, n_run[:].rearrange("p e t -> p t e"), ALU.add))
            for k, onehot in enumerate((first, second)):
                link(nc.vector.tensor_tensor(hit[:], slot_f[:], onehot[:], ALU.mult))
                link(nc.vector.tensor_reduce(slot_of[:, k, :], hit[:], AX.X, ALU.add))
            nc.vector.tensor_copy(slot_i[:], slot_of[:]).then_inc(d_slot, 1)
            link(nc.vector.tensor_tensor(past[:], C("tile_no").unsqueeze(2).to_broadcast([P, TILES_D, EXPERTS_D]),
                                         end_tile[:].unsqueeze(1).to_broadcast([P, TILES_D, EXPERTS_D]), ALU.is_ge))
            link(nc.vector.tensor_reduce(tile_e[:], past[:], AX.X, ALU.add))
            nc.vector.tensor_scalar(tile_ei[:], tile_e[:], float(EXPERTS_D - 1), None, ALU.min).then_inc(d_map, 1)

            dve.sem_inc(e_act, 2)
            dve.sem_inc(e_ate, 1)

            def product(t, b):
                dve.wait_ge(e_silu, 2 + t + 1)
                dve.wait_ge(e_h3, t + 1)
                nc.vector.tensor_tensor(act_d[:, b, :], silu_d[:, b, :], psum[:, 3 + b, 0:FF_D],
                                        ALU.mult).then_inc(e_act, 1)

            def step(t, b):
                b %= 2
                dve.wait_ge(e_at, t + 1)
                nc.vector.tensor_copy(act_dt[:, b, :], psum[:, 5, 0:FF_D]).then_inc(e_ate, 1)
                if not (isinstance(t, int) and t == TILES_D - 1):
                    product(t + 1, 1 - b)

            product(0, 0)
            rounds(dve, TILES_D, 2, step, head=0)

            for n in range(BLOCKS):
                dve.wait_ge(f_back[n], 16 * 8)
                for k, (w, rows) in enumerate(((weight1, back1), (weight2, back2))):
                    if k:
                        dve.wait_ge(f_sum, 8 * n + 4)
                    for t in range(4 * n, 4 * n + 4):
                        nc.vector.scalar_tensor_tensor(x_tok[:, t, :], rows[:, t, :], w[:, t:t + 1], x_tok[:, t, :],
                                                       ALU.mult, ALU.add).then_inc(f_sum, 1)

        @block.scalar
        def _(act):
            def root(var_ready, sqrt_done):
                act.wait_ge(var_ready, 1)
                nc.scalar.activation(std[:], var_eps[:], ACT.Sqrt).then_inc(sqrt_done, 1)

            root(a_var, a_sqrt)
            act.wait_ge(s_pad, 1)
            act.sem_inc(a_pad, 2)
            with act.Fori(0, BLOCKS // 2) as i:
                for b in range(2):
                    act.wait_ge(a_tr, 2 + 2 * i + b + 1)
                    nc.scalar.copy(xpad[:, bass.ds(4 * i + 2 * b, 2), 1:SIDE + 1, 1:SIDE + 1],
                                   psum[:, b, :].rearrange("p (n a c) -> p n a c", n=2, a=SIDE)).then_inc(a_pad, 1)
            act.wait_ge(ld_w, 16 * len(LOADS))
            act.sem_inc(a_relu, 2)
            with act.Fori(0, BLOCKS // 2) as i:
                for b in range(2):
                    act.wait_ge(a_conv, 2 * i + b + 1)
                    act.wait_ge(a_back, 2 * i + b + 1)
                    nc.scalar.activation(conv_t[:, b, :], psum[:, 2 + b, :], ACT.Relu,
                                         bias=conv_bs[:, 0:1]).then_inc(a_relu, 1)
            if "B" not in stages:
                return
            root(b_var, b_sqrt)
            act.sem_inc(b_xt, 2)
            with act.Fori(0, BLOCKS // 2) as i:
                for b in range(2):
                    act.wait_ge(b_tr, 2 + 2 * i + b + 1)
                    nc.scalar.copy(xt[:, b, :], psum[:, b, :]).then_inc(b_xt, 1)
            act.wait_ge(b_sub, 1)
            nc.scalar.activation(gate[:], gate[:], ACT.Exp).then_inc(b_exp, 1)
            act.wait_ge(b_ids, 1)
            for h in range(2):
                for a in range(8):
                    act.dma_start(ids_e[16 * h:16 * h + 16, 16 * a:16 * a + 16],
                                  ids_f[16 * a:16 * a + 16, h, :]).then_inc(b_idd, 16)
            act.sem_inc(b_act, 3)
            with act.Fori(0, GROUPS_B // 2) as i:
                for b in range(2):
                    g = 2 * i + b
                    for c, (_, n) in enumerate(CHUNKS_B):
                        act.wait_ge(b_up, 3 * g + c + 1)
                        nc.scalar.activation(act_b[0:n, b, c, :], psum[0:n, 2 + c, :], ACT.Silu,
                                             bias=bu_sb[0:n, bass.ds(g, 1), c]).then_inc(b_act, 1)

            if "C" not in stages:
                return
            root(c_var, c_sqrt)
            nc.scalar.mul(qb_scaled[:], qkb[:, 0:1], SCALE).then_inc(c_qb, 1)
            act.sem_inc(c_xt, 1)
            act.sem_inc(c_exp, 2)
            act.sem_inc(c_pe, 2)
            act.wait_ge(c_qb, 1)

            def evac_normed(t, b):
                act.wait_ge(c_tr, 2 + t + 1)
                act.wait_ge(c_qkv, t + 1)
                nc.scalar.copy(xt[:, b, 0:P], psum[:, 0, 0:P]).then_inc(c_xt, 1)

            def evac_query_value(t, b):
                act.wait_ge(c_qkv, 2 + t + 1)
                act.wait_ge(c_s, t + 1)
                nc.scalar.activation(q_t[:, b, :], psum[:, 1, 0:P], ACT.Identity, bias=qb_scaled[:, 0:1],
                                     scale=SCALE).then_inc(c_q, 1)
                nc.scalar.copy(extra[:, bass.ds(t, 1), :], psum[:, 1:2, 2 * P:3 * P]).then_inc(c_va, 1)

            def exponent(t, b):
                act.wait_ge(c_sub, t + 1)
                act.wait_ge(c_pt, 2 * t + 2)
                nc.scalar.activation(prob[:, b, :], score[:, b, :], ACT.Exp).then_inc(c_exp, 1)

            def evac_prob(t, b):
                act.wait_ge(c_av, t + 1)
                for h in range(2):
                    act.wait_ge(c_pt, 4 + 2 * t + h + 1)
                    nc.scalar.copy(prob_t[:, b, 512 * h:512 * h + 512], psum[:, 6 + h, :]).then_inc(c_pe, 1)

            staggered(act, TILES, [(evac_query_value, 2), (evac_normed, 1), (exponent, 5), (evac_prob, 6)])
            if "D" not in stages:
                return
            root(d_var, d_sqrt)
            act.sem_inc(d_xt, 2)
            for n in range(BLOCKS):
                act.wait_ge(d_tr, n + 1)
                nc.scalar.copy(xt[:, n % 2, :], psum[:, n % 2, :]).then_inc(d_xt, 1)
            act.wait_ge(d_dm, 1)
            nc.scalar.activation(ratio[:], ratio[:], ACT.Exp).then_inc(d_ex, 1)

            act.sem_inc(e_silu, 2)
            act.sem_inc(e_xt, 1)
            act.sem_inc(e_y, 1)

            def rows_t(t, b):
                act.wait_ge(e_tr, t + 1)
                nc.scalar.copy(xt_d[:, b, :], psum[:, 0, 0:P]).then_inc(e_xt, 1)

            def silu(t, b):
                act.wait_ge(e_h1, t + 1)
                act.wait_ge(e_act, t + 1)
                nc.scalar.activation(silu_d[:, b, :], psum[:, 1 + b, 0:FF_D], ACT.Silu).then_inc(e_silu, 1)

            def step(t, b):
                c = b % 2
                if not (isinstance(t, int) and t == TILES_D - 1):
                    silu(t + 1, 1 - c)
                if not (isinstance(t, int) and t >= TILES_D - 2):
                    rows_t(t + 2, c)
                act.wait_ge(e_yp, t + 1)
                act.wait_ge(e_st[c], 16 + 8 * (t - c))
                nc.scalar.copy(y_d[:, c, :], psum[:, 6, 0:P]).then_inc(e_y, 1)

            rows_t(0, 0)
            rows_t(1, 1)
            silu(0, 0)
            rounds(act, TILES_D, 4, step, head=0)

        @block.tensor
        def _(pe):
            def transpose(dst, src):
                return nc.tensor.transpose(dst, src, ident)

            pe.wait_ge(ld_w, 16 * len(LOADS))
            pe.sem_inc(a_tr, 2)
            with pe.Fori(0, BLOCKS // 2) as i:
                for b in range(2):
                    pe.wait_ge(a_xn, 2 * i + b + 1)
                    pe.wait_ge(a_pad, 2 * i + b + 1)
                    for k in range(4):
                        ins = transpose(psum[:, b, P * k:P * (k + 1)], xn[:, b, k, :])
                    ins.then_inc(a_tr, 1)
            pe.sem_inc(a_back, 2)
            with pe.Fori(0, BLOCKS // 2) as i:
                for b in range(2):
                    pe.wait_ge(a_pad, 2 + 2 * i + b + 1)
                    pe.wait_ge(a_relu, 2 * i + b + 1)
                    for tap in range(TAPS):
                        dy, dx = tap // 3, tap % 3
                        ins = nc.tensor.matmul(psum[:, 2 + b, :], conv_sb[:, tap, :],
                                               xpad[:, bass.ds(4 * i + 2 * b, 2), dy:dy + SIDE, dx:dx + SIDE],
                                               start=tap == 0, stop=tap == TAPS - 1)
                    ins.then_inc(a_conv, 1)
                for b in range(2):
                    pe.wait_ge(a_relu, 2 + 2 * i + b + 1)
                    pe.wait_ge(a_res, 2 * i + b + 1)
                    for k in range(4):
                        ins = transpose(psum[:, 4 + b, P * k:P * (k + 1)], conv_t[:, b, P * k:P * (k + 1)])
                    ins.then_inc(a_back, 1)
            if "B" not in stages:
                return

            pe.sem_inc(b_down, 2)
            pe.sem_inc(b_tr, 2)
            with pe.Fori(0, BLOCKS // 2) as i:
                for b in range(2):
                    pe.wait_ge(b_xn, 2 * i + b + 1)
                    pe.wait_ge(b_xt, 2 * i + b + 1)
                    for k in range(4):
                        ins = transpose(psum[:, b, P * k:P * (k + 1)], xn[:, b, k, :])
                    ins.then_inc(b_tr, 1)
                for b in range(2):
                    pe.wait_ge(b_xt, 2 + 2 * i + b + 1)
                    flat = psum[:, 6:8, :].rearrange("p a n -> p (a n)")
                    for k in range(4):
                        ins = nc.tensor.matmul(flat[:, bass.ds((8 * i + 4 * b + k) * EXPERTS_B, EXPERTS_B)],
                                               xt[:, b, P * k:P * (k + 1)], wr_sb[:], start=True, stop=True)
                    ins.then_inc(b_logit, 1)
            pe.wait_ge(b_gate, 1)
            for g in range(8):
                ins = transpose(psum[:, g // 4, P * (g % 4):P * (g % 4 + 1)], gate[:, 4 * g:4 * g + 4, :].rearrange("p j e -> p (j e)"))
                if g % 4 == 3:
                    ins.then_inc(b_gtr, 1)
            with pe.Fori(0, BITS) as i:
                pe.wait_ge(b_cnt, i + 1)
                nc.tensor.matmul(psum[:, 2, 0:1], C("same_expert"), count[:, 0:1], start=True,
                                 stop=True).then_inc(b_sum, 1)
            pe.wait_ge(b_tot, 2)
            nc.tensor.matmul(psum[:, 3, 0:2], C("earlier_segment"), count[:, 0:2], start=True, stop=False,
                             skip_group_check=True)
            nc.tensor.matmul(psum[:, 3, 1:2], C("same_expert"), count[:, 0:1], start=False, stop=True,
                             skip_group_check=True).then_inc(b_off, 1)
            pe.wait_ge(b_pos, 1)
            for g in range(8):
                ins = transpose(psum[:, g // 4, P * (g % 4):P * (g % 4 + 1)], n_above[:, P * g:P * (g + 1)])
                if g % 4 == 3:
                    ins.then_inc(b_ptr, 1)
            pe.sem_inc(b_ohmm, 2)
            for u in range(TILES):
                pe.wait_ge(b_oh, u + 1)
                for h in range(2):
                    ins = nc.tensor.matmul(psum[:, 4 + h, 0:256], oh_id[:, u % 2, h].rearrange("p a e -> p (a e)"),
                                           oh_lo[:, u % 2, :, 16 * h:16 * h + 16], start=u == 0, stop=u == TILES - 1)
                ins.then_inc(b_ohmm, 1)

            pe.wait_ge(b_idd, 16 * 16)
            nc.tensor.transpose(psum[:, 2, 0:EXPERTS_B], ids_e[:], ident[0:EXPERTS_B, 0:EXPERTS_B]).then_inc(b_idt, 1)

            with pe.Fori(0, GROUPS_B // 2) as i:
                for b in range(2):
                    g = 2 * i + b
                    pe.wait_ge(b_gath[b], 64 * i + 64)
                    pe.wait_ge(b_xgt, g + 1)
                    for k in range(4):
                        ins = transpose(psum[:, b, P * k:P * (k + 1)], rows_b[:, b, k, 0:P])
                    ins.then_inc(b_xg, 1)
                    pe.wait_ge(b_xgt, 2 + g + 1)
                    pe.wait_ge(b_w[b], 48 * i + 48)
                    for c, (f, n) in enumerate(CHUNKS_B):
                        pe.wait_ge(b_act, 3 * g + c + 1)
                        nc.tensor.matmul(psum[0:n, 2 + c, :], wu_sb[:, b, f:f + n], xt[:, b, :], start=True,
                                         stop=True).then_inc(b_up, 1)
                    pe.wait_ge(b_y, g + 1)
                    nc.tensor.matmul(psum[:, 5 + b, :], ones_row[:], bd_sb[:, b, :], start=True, stop=False,
                                     skip_group_check=True)
                    for c, (f, n) in enumerate(CHUNKS_B):
                        pe.wait_ge(b_act, 3 + 3 * g + c + 1)
                        for k in range(4):
                            ins = nc.tensor.matmul(psum[:, 5 + b, P * k:P * (k + 1)],
                                                   act_b[0:n, b, c, P * k:P * (k + 1)], wd_sb[0:n, b, k, c, :],
                                                   start=False, stop=c == 2, skip_group_check=True)
                    ins.then_inc(b_down, 1)
            if "C" not in stages:
                return

            pe.sem_inc(c_tr, 2)
            pe.sem_inc(c_qkv, 2)
            pe.sem_inc(c_s, 2)
            pe.sem_inc(c_pt, 4)
            pe.sem_inc(c_av, 2)

            def products(t, b):
                pe.wait_ge(c_xt, 1 + t + 1)
                pe.wait_ge(c_k, t + 1)
                for k in range(2):
                    nc.tensor.matmul(psum[:, 1, P * k:P * (k + 1)], wqkv[:, P * k:P * (k + 1)], xt[:, b, 0:P],
                                     start=True, stop=True)
                for w in range(2):
                    for h in range(2):
                        o = psum[WIN * h:WIN * h + WIN, 1, 2 * P + WIN * w:2 * P + WIN * (w + 1)]
                        cols = slice(2 * P + WIN * h, 2 * P + WIN * (h + 1))
                        ins = nc.tensor.matmul(o, xt[:, b, WIN * w:WIN * (w + 1)], wqkv[:, cols], start=True, stop=True)
                ins.then_inc(c_qkv, 1)

            def transpose_normed(t, b):
                pe.wait_ge(c_xn, t + 1)
                pe.wait_ge(c_xt, t + 1)
                pe.wait_ge(c_o, t + 1)
                transpose(psum[:, 0, 0:P], xn[:, b, 0, :]).then_inc(c_tr, 1)

            def scores_wait(t, b):
                pe.wait_ge(c_q, t + 1)
                pe.wait_ge(c_k, 1 + t + 1)
                pe.wait_ge(c_sb, t + 1)

            def scores(t, b):
                for q in range(2):
                    rows = slice(64 * q, 64 * q + 64)
                    for w in range(2):
                        ins = nc.tensor.matmul(psum[WIN * w:WIN * (w + 1), 2 + 2 * b + q, :],
                                               q_t[rows, b, WIN * w:WIN * (w + 1)],
                                               k_x[rows, b, :, WIN * w:WIN * (w + 1)], start=True, stop=True)
                ins.then_inc(c_s, 1)

            def transpose_prob(t, b):
                pe.wait_ge(c_exp, 2 + t + 1)
                for h in range(2):
                    pe.wait_ge(c_pe, 2 * t + h + 1)
                    for k in range(4):
                        at = 512 * h + P * k
                        ins = transpose(psum[:, 6 + h, P * k:P * (k + 1)], prob[:, b, at:at + P])
                    ins.then_inc(c_pt, 1)

            def weigh_values(t, b):
                pe.wait_ge(c_pe, 2 + 2 * t + 2)
                pe.wait_ge(c_v, t + 1)
                pe.wait_ge(c_o, 7 + t)
                last = min(t + 6, TILES - 1) if isinstance(t, int) else t + 6
                pe.wait_ge(c_xt, 1 + last + 1)
                for pair in range(8):
                    for w in range(2):
                        n = 2 * (HDIM + 1)
                        ins = nc.tensor.matmul(psum[WIN * w:WIN * (w + 1), 0, P + n * pair:P + n * (pair + 1)],
                                               prob_t[:, b, P * pair + WIN * w:P * pair + WIN * (w + 1)],
                                               v_x[:, b, w, pair].rearrange("p h d -> p (h d)"), start=True, stop=True)
                ins.then_inc(c_av, 1)

            pe.wait_ge(c_one, 2)
            staggered(pe, TILES, [(products, 2), (scores_wait, 3), (transpose_normed, 1), (scores, 3), (transpose_prob, 6),
                                  (weigh_values, 7)])
            if "D" not in stages:
                return

            for n in range(BLOCKS + 1):
                if n < BLOCKS:
                    pe.wait_ge(d_xn, n + 1)
                    pe.wait_ge(d_xt, n + 1)
                    for k in range(4):
                        ins = transpose(psum[:, n % 2, P * k:P * (k + 1)], extra[:, 4 * n + k, :])
                    ins.then_inc(d_tr, 1)
                if n > 0:
                    pe.wait_ge(d_xt, 2 + n)
                    for k in range(4):
                        t = 4 * (n - 1) + k
                        ins = nc.tensor.matmul(psum[:, 2, EXPERTS_D * t:EXPERTS_D * (t + 1)],
                                               xt[:, (n - 1) % 2, P * k:P * (k + 1)], gw[:], start=True, stop=True)
                    ins.then_inc(d_log, 1)
            pe.wait_ge(d_sel, 1)
            flat = chosen[:].rearrange("p t e -> p (t e)")
            nc.tensor.matmul(psum[:, 3, 0:256], tri_b[:], flat, start=True, stop=True)
            nc.tensor.matmul(psum[:, 3, 256:512], ones_b[:], flat, start=True, stop=True).then_inc(d_pre, 1)

            pe.wait_ge(d_map, 1)

            def rows_t(t, b):
                pe.wait_ge(e_ld[b], 4 * (t - b) + 16)
                pe.wait_ge(e_xt, t + 1)
                transpose(psum[:, 0, 0:P], rows_d[:, b, :]).then_inc(e_tr, 1)

            def up(weights, bank, ready, t, b, e):
                nc.tensor.matmul(psum[:, bank, 0:FF_D], xt_d[:, b, :], weights[:, bass.ds(e, 1), :], start=True,
                                 stop=True).then_inc(ready, 1)

            def expert_of(t):
                return pe.value_load(tile_ei[0:1, bass.ds(t, 1)], min_val=0, max_val=EXPERTS_D - 1)

            def experts_of(t, n):
                return nc.values_load_multi_w_load_instructions(
                    tile_ei[0:1, bass.ds(t, n)], engines=(mybir.EngineType.PE,), min_val=0, max_val=EXPERTS_D - 1)[1]

            def first_up(t, b, e):
                pe.wait_ge(e_xt, 1 + t + 1)
                pe.wait_ge(e_silu, t + 1)
                up(w1_sb, 1 + b, e_h1, t, b, e)

            def second_up(t, b, e):
                pe.wait_ge(e_act, t + 1)
                up(w3_sb, 3 + b, e_h3, t, b, e)

            def step(t, b, e_now, e_next):
                c = b % 2
                last = isinstance(t, int) and t == TILES_D - 1
                if not last:
                    first_up(t + 1, 1 - c, e_next)
                pe.wait_ge(e_act, 2 + t + 1)
                pe.wait_ge(e_ate, t + 1)
                for k in range(CHUNKS_D):
                    ins = transpose(psum[:, 5, P * k:P * (k + 1)], act_d[:, c, P * k:P * (k + 1)])
                ins.then_inc(e_at, 1)
                if not last:
                    second_up(t + 1, 1 - c, e_next)
                if not (isinstance(t, int) and t >= TILES_D - 2):
                    rows_t(t + 2, (b + 2) % 4)
                pe.wait_ge(e_ate, 1 + t + 1)
                pe.wait_ge(e_y, t + 1)
                for k in range(CHUNKS_D):
                    ins = nc.tensor.matmul(psum[:, 6, 0:P], act_dt[:, c, P * k:P * (k + 1)],
                                           w2_sb[:, bass.ds(e_now, 1), k, :], start=k == 0, stop=k == CHUNKS_D - 1)
                ins.then_inc(e_yp, 1)

            rows_t(0, 0)
            rows_t(1, 1)
            e = expert_of(0)
            first_up(0, 0, e)
            second_up(0, 0, e)
            with pe.Fori(0, TILES_D // 8 - 1) as i:
                e = experts_of(8 * i, 9)
                for k in range(8):
                    step(8 * i + k, k, e[k], e[k + 1])
            e = experts_of(TILES_D - 8, 8)
            for k in range(8):
                step(TILES_D - 8 + k, k, e[k], e[min(k + 1, 7)])


_IN_NAMES = ["x", "conv_w", "conv_b", "w_router", "b_router", "w_up", "b_up", "w_down", "b_down",
             "qkv_w", "qk_bias", "v_bias", "rel_bias", "mask", "gate_w", "w1", "w3", "w2", "const"]


def lay_out(inputs):
    import numpy as np
    a = {k: np.asarray(v) for k, v in inputs.items()}
    k = a["L0_conv_kernel"]
    width = k.shape[2]
    conv = np.zeros((P, TAPS, P), k.dtype)
    for g in range(P // width):
        s = slice(g * width, (g + 1) * width)
        conv[s, :, s] = k.reshape(TAPS, width, P)[:, :, s].transpose(1, 0, 2)
    up = a["L0_ffn_W_up"]
    b_up = np.zeros((GROUPS_B, 3 * P), up.dtype)
    b_up[:, :FF_B] = a["L0_ffn_b_up"]
    down = np.zeros((EXPERTS_B, 3 * P, P), up.dtype)
    down[:, :FF_B] = a["L0_ffn_W_down"]
    w0 = np.stack(np.meshgrid(np.arange(8), np.arange(8), indexing="ij")).reshape(2, -1)
    rel = w0[:, :, None] - w0[:, None, :] + 7
    rel = rel[0] * 15 + rel[1]
    bias = a["L1_conv_bias_table"][rel].transpose(0, 2, 1)
    qb = a["L1_conv_qkv_b"]
    w2 = a["L1_ffn_w2"]
    v_cols = np.arange(P).reshape(HEADS // 2, 2, HDIM).transpose(1, 0, 2).ravel()
    qkv_cols = np.concatenate([np.arange(2 * P), 2 * P + v_cols])
    return {
        "x": a["x"].reshape(TOKENS, P),
        "conv_w": conv.reshape(P, TAPS * P),
        "conv_b": a["L0_conv_bias"].reshape(P, 1),
        "w_router": a["L0_ffn_W_router"],
        "b_router": a["L0_ffn_b_router"],
        "w_up": up.transpose(1, 0, 2),
        "b_up": b_up.reshape(GROUPS_B, 3, P).transpose(2, 0, 1),
        "w_down": down.reshape(EXPERTS_B, 3, P, P).transpose(2, 0, 1, 3).reshape(P, -1),
        "b_down": a["L0_ffn_b_down"].reshape(GROUPS_B, 4 * P),
        "qkv_w": a["L1_conv_qkv_w"].T[:, qkv_cols],
        "qk_bias": qb[:2 * P].reshape(2, P).T,
        "v_bias": qb[2 * P:].reshape(1, P),
        "rel_bias": np.concatenate([bias, bias]).reshape(P, HEADS * WIN),
        "mask": window_mask(),
        "gate_w": a["L1_ffn_gate_w"].T,
        "w1": a["L1_ffn_w1"].transpose(2, 0, 1),
        "w3": a["L1_ffn_w3"].transpose(2, 0, 1),
        "w2": w2.transpose(2, 0, 1).reshape(CHUNKS_D, P, EXPERTS_D, P).transpose(1, 2, 0, 3),
    }


STOP = "D"


def kernel(**inputs):
    import numpy as _np
    import concourse.bacc as _bacc
    from concourse import mybir as _mybir
    from concourse.bass_utils import run_bass_kernel_spmd as _run

    nc = _bacc.Bacc("TRN2", target_bir_lowering=False, num_devices=1)
    laid = lay_out(inputs)
    laid["const"], const_at = constants()
    arrays, args = {}, []
    for name in _IN_NAMES:
        a = _np.ascontiguousarray(laid[name])
        arrays[f"in_{name}_dram"] = a
        args.append(nc.dram_tensor(f"in_{name}_dram", a.shape, _mybir.dt.from_np(a.dtype), kind="ExternalInput").ap())
    args.append(nc.dram_tensor("out_0_dram", (TOKENS, P), F32, kind="ExternalOutput").ap())
    metaformer(nc, const_at, *args, stop=STOP)
    r = _run(nc, [arrays], core_ids=[0])
    return r.results[0]["out_0_dram"].reshape(IMAGES, SIDE, SIDE, P)
```

```python
from contextlib import ExitStack, contextmanager

import concourse.bass as bass
from concourse import mybir

F32 = mybir.dt.float32
F16 = mybir.dt.float16
I32 = mybir.dt.int32
BF16 = mybir.dt.bfloat16
ALU = mybir.AluOpType
ACT = mybir.ActivationFunctionType
AX = mybir.AxisListType

P = 128
IMAGES, SIDE = 16, 16
TOKENS = IMAGES * SIDE * SIDE
TILES = TOKENS // P
BLOCKS = TILES // 4
PAD = SIDE + 2
TAPS = 9
EXPERTS_B, GROUPS_B = 32, 8
CAP = TOKENS // EXPERTS_B
FF_B = 341
CHUNKS_B = [(0, 128), (128, 128), (256, FF_B - 256)]
ROW_B = P + EXPERTS_B
HEADS, HDIM, WIN = 16, 8, 64
SCALE = HDIM ** -0.5
EXPERTS_D, FF_D = 8, 384
CHUNKS_D = FF_D // P
PAIRS = 2 * TOKENS
TILES_D = PAIRS // P + EXPERTS_D
ID_SHIFT = 2048
BITS = 30
SEG = TOKENS // 4


def constants():
    import numpy as np
    p = np.arange(P)
    j, e = p // EXPERTS_B, p % EXPERTS_B
    parts = {}
    parts["ident"] = np.eye(P)
    parts["same_expert"] = e[:, None] == e[None, :]
    parts["earlier_segment"] = (e[:, None] == e[None, :]) & (j[:, None] < j[None, :])
    parts["head_of_8"] = (p[:, None] // HDIM) % 8 == np.arange(8)[None, :]
    parts["half"] = (p[:, None] // WIN) == np.arange(2)[None, :]
    u = np.arange(TILES)
    parts["token_id"] = ((u // 4 + 8 * (u % 4))[None, :] * P + p[:, None]) - ID_SHIFT
    parts["same_e16"] = p[:, None] % 16 == np.arange(16)[None, :]
    parts["same_slot_hi"] = p[:, None] // 16 == np.arange(8)[None, :]
    parts["tri"] = p[:, None] <= p[None, :]
    parts["rank8"] = np.broadcast_to(EXPERTS_D - np.arange(EXPERTS_D), (P, EXPERTS_D))
    parts["restart"] = np.broadcast_to(np.arange(EXPERTS_D * TILES) % TILES != 0, (P, EXPERTS_D * TILES))
    parts["tile_no"] = np.broadcast_to(np.arange(TILES_D), (P, TILES_D))
    parts["lane"] = np.broadcast_to(np.arange(P), (P, P))
    parts["partition"] = p[:, None]
    parts["pair_no"] = np.broadcast_to(1 + np.arange(2 * TILES), (P, 2 * TILES))
    parts["spare_row"] = PAIRS + P + np.arange(TILES_D)[None, :] * P + p[:, None]
    parts["slot_hi"] = np.broadcast_to(np.tile(np.repeat(np.arange(8), 16), 2), (P, 8 * EXPERTS_B))
    parts["slot_lo"] = np.broadcast_to(np.repeat(np.arange(16), EXPERTS_B), (P, 16 * EXPERTS_B))
    at, cols, n = {}, [], 0
    for name, a in parts.items():
        at[name] = (n, n + a.shape[1])
        n += a.shape[1]
        cols.append(a.astype(np.float32))
    return np.ascontiguousarray(np.concatenate(cols, 1)), at


def window_mask():
    import numpy as np
    region = np.zeros((SIDE, SIDE))
    cuts = (slice(0, -8), slice(-8, -4), slice(-4, None))
    for a, hs in enumerate(cuts):
        for b, ws in enumerate(cuts):
            region[hs, ws] = 3 * a + b
    win = region.reshape(2, 8, 2, 8).transpose(0, 2, 1, 3).reshape(2, 2, WIN)
    return (-100.0 * (win[:, :, :, None] != win[:, :, None, :])).astype(np.float32).reshape(2, P, WIN)


class Tally:

    def __init__(self):
        self.base, self.steps, self.i, self.per = 0, 0, None, 0

    def next(self):
        self.steps += 1
        return self.now()

    def now(self):
        if self.i is None:
            return self.base + self.steps
        return self.i * self.per + (self.base + self.steps)

    @contextmanager
    def loop(self, eng, rounds, per):
        self.base, self.steps = self.base + self.steps, 0
        with eng.Fori(0, rounds) as i:
            self.i, self.per = i, per
            yield i
            assert self.steps == per, (self.steps, per)
        self.base, self.steps, self.i = self.base + rounds * per, 0, None


def staggered(eng, n, parts):
    def step(first, k):
        for fn, lag in parts:
            t = first + k - lag
            if not isinstance(t, int) or 0 <= t < n:
                fn(t, (k - lag) % 2)

    depth = max(lag for _, lag in parts)
    head = depth + depth % 2
    for k in range(head):
        step(0, k)
    with eng.Fori(0, (n - head) // 2) as i:
        for k in range(head, head + 2):
            for fn, lag in parts:
                fn(2 * i + (k - lag), (k - lag) % 2)
    for k in range(n, n + depth):
        step(0, k)


def rounds(eng, n, width, step, head=1, tail=1):
    for t in range(head * width):
        step(t, t % width)
    with eng.Fori(head, n // width - tail) as i:
        for k in range(width):
            step(width * i + k, k)
    for t in range(n - tail * width, n):
        step(t, t % width)


def metaformer(nc, const_at, x, conv_w, conv_b, w_router, router_bias, w_up, up_bias, w_down, down_bias,
               qkv_w, qk_bias, v_bias, rel_bias, mask, gate_w, w1, w3, w2, const, out, stop="D"):
    order = "ABCD"
    stages = order[:order.index(stop) + 1]
    with ExitStack() as ctx:
        def sb(name, shape, dt=F32):
            return ctx.enter_context(nc.sbuf_tensor(name, shape, dt))

        def sem(name):
            return ctx.enter_context(nc.semaphore(name))

        def dram(name, shape, dt=F32):
            return nc.dram_tensor(name, shape, dt, kind="Internal").ap()

        psum = ctx.enter_context(nc.psum_tensor("psum", [P, 8, 512], F32))

        table = dram("table", [TOKENS, ROW_B])
        y_even = dram("y_even", [TOKENS, P])
        y_odd = dram("y_odd", [TOKENS, P])
        normed = dram("normed", [TOKENS, P])
        results = dram("results", [PAIRS + TILES_D * P, P])

        x_tok = sb("x_tok", [P, TILES, P])
        extra = sb("extra", [P, TILES, P])
        scratch = sb("scratch", [P, 2 * BLOCKS * PAD * PAD])
        xpad = scratch[:, :].rearrange("p (n a b) -> p n a b", n=IMAGES, a=PAD)
        cst = sb("cst", [P, const.shape[1]])

        def C(name):
            a, b = const_at[name]
            return cst[:, a:b]

        ident = C("ident")
        zeros = sb("zeros", [P, 1024])
        ones_row = sb("ones_row", [1, P])
        arena = sb("arena", [P, 3 * 2 * HEADS * WIN])
        arena_b = sb("arena_b", [P, 2 * 3 * 512])

        def shared(pool_of, offset, shape, dt=F32):
            n = 1
            for d in shape[1:]:
                n *= d
            words = n // 2 if dt in (F16, BF16) else n
            v = pool_of[:, offset:offset + words]
            if dt != F32:
                v = v.bitcast(dt)
            if len(shape) > 2:
                names = "abcdefg"[:len(shape) - 1]
                v = v.rearrange(f"p ({' '.join(names)}) -> p {' '.join(names)}",
                                **{c: d for c, d in zip(names, shape[1:])})
            return v, offset + words

        stats = sb("stats", [P, TILES, 6])
        mean = sb("mean", [P, TILES])
        gap = sb("gap", [P, TILES])
        spread = sb("spread", [P, TILES])
        var_eps = sb("var_eps", [P, TILES])
        std = sb("std", [P, TILES])
        rstd = sb("rstd", [P, TILES])
        xn = sb("xn", [P, 2, 4, P])
        xt = sb("xt", [P, 2, 512])
        conv_sb = sb("conv_sb", [P, TAPS, P])
        conv_bs = sb("conv_bs", [P, 1])
        conv_t = sb("conv_t", [P, 2, 512])

        wqkv = sb("wqkv", [P, 3 * P])
        qkb = sb("qkb", [P, 2])
        qb_scaled = sb("qb_scaled", [P, 1])
        vb_sb = sb("vb_sb", [P, P])
        rel = sb("rel", [P, 2, HEADS * WIN])
        msk = sb("msk", [P, 2, WIN])
        q_t = sb("q_t", [P, 2, P])
        k_x, _ = shared(arena_b, 0, [P, 2, 8, P])
        v_x = sb("v_x", [P, 2, 2, 8, 2, HDIM + 1])
        score, at = shared(arena, 0, [P, 2, HEADS * WIN])
        prob, at = shared(arena, at, [P, 2, HEADS * WIN])
        prob_t, at = shared(arena, at, [P, 2, HEADS * WIN])
        peak = sb("peak", [P, 2, HEADS])
        inv_sum = sb("inv_sum", [P, 2, HEADS])
        att = sb("att", [P, 2, P])

        gw = sb("gw", [P, EXPERTS_D])
        w1_sb = sb("w1_sb", [P, EXPERTS_D, FF_D])
        w3_sb = sb("w3_sb", [P, EXPERTS_D, FF_D])
        w2_sb = sb("w2_sb", [P, EXPERTS_D, CHUNKS_D, P])
        TE = [P, TILES, EXPERTS_D]
        lg = sb("lg", TE)
        hit = sb("hit", TE)
        first = sb("first", TE)
        second = sb("second", TE)
        chosen = sb("chosen", TE, BF16)
        tri_b = sb("tri_b", [P, P], BF16)
        ones_b = sb("ones_b", [P, P], BF16)
        peak1 = sb("peak1", [P, TILES])
        peak2 = sb("peak2", [P, TILES])
        rank = sb("rank", [P, TILES])
        ratio = sb("ratio", [P, TILES])
        weight1 = sb("weight1", [P, TILES])
        weight2 = sb("weight2", [P, TILES])
        n_tile = sb("n_tile", [P, EXPERTS_D, TILES])
        n_run = sb("n_run", [P, EXPERTS_D, TILES])
        tiles_i = sb("tiles_i", [P, EXPERTS_D], I32)
        tiles_f = sb("tiles_f", [P, EXPERTS_D])
        end_tile = sb("end_tile", [P, EXPERTS_D])
        base = sb("base", [P, EXPERTS_D])
        slot_f = sb("slot_f", TE)
        slot_of = sb("slot_of", [P, 2, TILES])
        slot_i = sb("slot_i", [P, 2, TILES], I32)
        part_i = sb("part_i", [P, 2, TILES], I32)
        slot_tile = sb("slot_tile", [P, 2 * TILES])
        slot_lane = sb("slot_lane", [P, 2 * TILES])
        PT = [P, 2 * TILES]
        oh_lane, _ = shared(scratch, 0, PT + [P], BF16)
        oh_tile, _ = shared(arena_b, 0, PT + [TILES_D], BF16)
        oh_value, _ = shared(arena, 0, PT + [2, TILES_D], BF16)
        pair_f = sb("pair_f", [P, TILES_D])
        dest_f = sb("dest_f", [P, TILES_D])
        gather_i = sb("gather_i", [P, TILES_D], I32)
        dest_i = sb("dest_i", [P, TILES_D], I32)
        past = sb("past", [P, TILES_D, EXPERTS_D])
        tile_e = sb("tile_e", [P, TILES_D])
        tile_ei = sb("tile_ei", [P, TILES_D], I32)
        rows_d, at = shared(arena, 0, [P, 4, P])
        xt_d, at = shared(arena, at, [P, 2, P])
        silu_d, at = shared(arena, at, [P, 2, FF_D])
        act_d, at = shared(arena, at, [P, 2, FF_D])
        act_dt, at = shared(arena, at, [P, 2, FF_D])
        y_d, at = shared(arena, at, [P, 4, P])
        back1 = extra
        back2 = scratch[:, 0:TILES * P].rearrange("p (t c) -> p t c", c=P)

        wr_sb = sb("wr_sb", [P, EXPERTS_B])
        br_sb = sb("br_sb", [P, EXPERTS_B])
        gate = sb("gate", [P, TILES, EXPERTS_B])
        top = sb("top", [P, TILES])
        total = sb("total", [P, TILES])
        inv = sb("inv", [P, TILES])
        by_expert = sb("by_expert", [P, SEG])
        above, tied, n_above, n_tied = (scratch[:, SEG * k:SEG * (k + 1)] for k in range(4))
        thr = sb("thr", [P, 1], I32)
        cand = sb("cand", [P, 1], I32)
        kept = sb("kept", [P, 1])
        bits = sb("bits", [P, BITS + 1], I32)
        count16 = sb("count16", [P, 1], F16)
        same16 = sb("same16", [P, P], F16)
        count = sb("count", [P, 2])
        offs = sb("offs", [P, 2])
        place, at = shared(arena_b, 0, [P, TILES, EXPERTS_B], I32)
        place2, at = shared(arena_b, at, [P, TILES, EXPERTS_B], I32)
        hi16, at = shared(arena_b, at, [P, TILES, EXPERTS_B], F16)
        lo16, at = shared(arena_b, at, [P, TILES, EXPERTS_B], F16)
        slot_hi = sb("slot_hi", [P, 2, 8, 16], F16)
        slot_lo = sb("slot_lo", [P, 16, EXPERTS_B], F16)
        oh_hi = sb("oh_hi", [P, 4, 2, 8, 16], F16)
        oh_id = sb("oh_id", [P, 4, 2, 8, 16], F16)
        oh_lo = sb("oh_lo", [P, 4, 16, EXPERTS_B], F16)
        picked = sb("picked", [P, 2, 16, 16])
        ids_f = sb("ids_f", [P, 2, 16])
        ids_x = sb("ids_x", [P, 2, 8, 16])
        idx = sb("idx", [P, EXPERTS_B], I32)
        idx_w, id_row, id_win = (sb(n, [P, EXPERTS_B], I32) for n in ("idx_w", "id_row", "id_win"))
        rows_b, _ = shared(scratch, 0, [P, 4, 4, ROW_B])
        wu_sb, at = shared(arena, 0, [P, 2, FF_B])
        wd_sb, at = shared(arena, at, [P, 2, 4, 3, P])
        bu_sb = sb("bu_sb", [P, GROUPS_B, 3])
        act_b, _ = shared(arena_b, 0, [P, 2, 3, 512])
        y_b, at = shared(arena, at, [P, 2, 4, P])
        bd_sb, at = shared(arena, at, [P, 2, 512])
        bd_sb = bd_sb[0:1]

        ld_x = [sem(f"ld_x{i}") for i in range(4)]
        ld_conv = sem("ld_conv")
        ld_w = sem("ld_w")
        dve_seq = sem("dve_seq")
        dve_n = Tally()
        s_zero = sem("s_zero")
        s_pad = sem("s_pad")

        a_sqrt, b_sqrt, c_sqrt, d_sqrt = (sem(f"{s}_sqrt") for s in "abcd")
        a_var, b_var, c_var, d_var = (sem(f"{s}_var") for s in "abcd")
        a_xn = sem("a_xn")
        a_tr = sem("a_tr")
        a_pad = sem("a_pad")
        a_conv = sem("a_conv")
        a_relu = sem("a_relu")
        a_back = sem("a_back")
        a_res = sem("a_res")

        b_xn, b_tr, b_xt, b_logit = (sem(f"b_{s}") for s in ("xn", "tr", "xt", "logit"))
        b_tab = [sem(f"b_tab{i}") for i in range(2)]
        b_sub, b_exp, b_gate, b_gtab, b_gtr, b_be = (sem(f"b_{s}") for s in ("sub", "exp", "gate", "gtab", "gtr", "be"))
        b_cnt, b_sum, b_tot, b_off, b_pos, b_ptr = (sem(f"b_{s}") for s in ("cnt", "sum", "tot", "off", "pos", "ptr"))
        b_oh, b_ohmm, b_ids, b_idt, b_idx, b_bits = (
            sem(f"b_{s}") for s in ("oh", "ohmm", "ids", "idt", "idx", "bits"))
        b_xg, b_xgt, b_up, b_act, b_down, b_y = (
            sem(f"b_{s}") for s in ("xg", "xgt", "up", "act", "down", "y"))
        b_w = [sem(f"b_w{i}") for i in range(2)]
        b_gath = [sem(f"b_gath{i}") for i in range(4)]
        b_sc = [sem(f"b_sc{i}") for i in range(2)]
        b_init = sem("b_init")
        b_ohhi, b_ohid = sem("b_ohhi"), sem("b_ohid")
        done = sem("done")
        c_ld = [sem(f"c_ld{i}") for i in range(4)]
        (c_sum, c_rel, c_one, c_xn, c_tr, c_xt, c_qkv, c_q, c_k, c_v, c_s, c_sb, c_mx, c_sub, c_exp, c_pt,
         c_pe, c_av, c_o, c_res, c_va, c_vb, c_qb) = (sem(f"c_{s}") for s in (
             "sum", "rel", "one", "xn", "tr", "xt", "qkv", "q", "k", "v", "s", "sb", "mx", "sub", "exp",
             "pt", "pe", "av", "o", "res", "va", "vb", "qb"))
        (d_xn, d_tr, d_xt, d_log, d_dm, d_ex, d_sel, d_pre, d_map, d_oh, d_ohp, d_oht, d_inv, d_idx) = (
            sem(f"d_{s}") for s in ("xn", "tr", "xt", "log", "dm", "ex", "sel", "pre", "map", "oh", "ohp", "oht", "inv", "idx"))
        d_tab = sem("d_tab")
        d_lane = sem("d_lane")
        e_tr, e_xt, e_h1, e_h3, e_silu, e_act, e_at, e_ate, e_yp, e_y = (
            sem(f"e_{s}") for s in ("tr", "xt", "h1", "h3", "silu", "act", "at", "ate", "yp", "y"))
        e_ld = [sem(f"e_ld{i}") for i in range(4)]
        e_st = [sem(f"e_st{i}") for i in range(4)]
        f_back = [sem(f"f_back{i}") for i in range(BLOCKS)]
        f_sum = sem("f_sum")

        x_v = x.rearrange("(t p) c -> p t c", p=P)
        out_v = out.rearrange("(t p) c -> p t c", p=P)

        block = ctx.enter_context(nc.Block())

        CONV_LOADS = [(cst[:], const), (conv_sb[:], conv_w.rearrange("p (t c) -> p t c", t=TAPS)),
                      (conv_bs[:], conv_b)]
        LOADS = [(wr_sb[:], w_router), (br_sb[:], router_bias.partition_broadcast(P)), (bu_sb[:], up_bias),
                 (wqkv[:], qkv_w), (qkb[:], qk_bias), (vb_sb[:], v_bias.partition_broadcast(P)), (rel[:, 0, :], rel_bias),
                 (rel[:, 1, :], rel_bias), (msk[:], mask.rearrange("h p j -> p h j")), (gw[:], gate_w),
                 (w1_sb[:], w1), (w3_sb[:], w3), (w2_sb[:], w2)]

        def reload(queue, src, dst):
            src_v = src.rearrange("(t p) c -> p t c", p=P)
            for c in range(4):
                queue.dma_start(dst[:, 8 * c:8 * c + 8], src_v[:, 8 * c:8 * c + 8]).then_inc(c_ld[c], 16)

        @block.sync
        def _(sp):
            for c in range(4):
                sp.dma_start(x_tok[:, 8 * c:8 * c + 8, :], x_v[:, 8 * c:8 * c + 8, :]).then_inc(ld_x[c], 16)
            for dst, src in LOADS:
                sp.dma_start(dst, src).then_inc(ld_w, 16)
            if "B" in stages:
                sp.wait_ge(s_zero, 1)
                for c in range(4):
                    sp.dma_start(y_odd.rearrange("(p r) c -> p (r c)", p=P)[:, 1024 * c:1024 * (c + 1)],
                                 zeros[:]).then_inc(b_init, 16)
                sp.wait_ge(a_res, 2 + BLOCKS)
                y_w = y_even.rearrange("(t w r c) k -> r w c t k", w=2, r=8, c=8)
                for r in range(8):
                    for w in range(2):
                        at = 16 * r + 8 * w
                        sp.dma_start(y_w[r, w], x_tok[at:at + 8]).then_inc(b_init, 16)
                tab_v = table.rearrange("(t p) c -> p t c", p=P)
                for b in range(2):
                    sp.sem_inc(b_tab[b], 16)
                with sp.Fori(0, BLOCKS // 2) as i:
                    for b in range(2):
                        sp.wait_ge(b_xn, 2 * i + b + 1)
                        sp.dma_start(tab_v[:, bass.ds(8 * i + 4 * b, 4), 0:P], xn[:, b]).then_inc(b_tab[b], 16)
                sp.wait_ge(b_gate, 1)
                for j in range(4):
                    sp.dma_start(tab_v[:, 8 * j:8 * j + 8, P:ROW_B], gate[:, j:TILES:4, :]).then_inc(b_gtab, 16)
                wd_v = w_down.rearrange("p (g e k c) -> p g e k c", g=GROUPS_B, e=4, k=3)

                def group_weights(g, b):
                    sp.dma_start(wu_sb[:, b, :], w_up[:, bass.ds(g, 1), :]).then_inc(b_w[b], 16)
                    sp.dma_start(wd_sb[:, b], wd_v[:, bass.ds(g, 1)]).then_inc(b_w[b], 16)
                    sp.dma_start(bd_sb[:, b, :], down_bias[bass.ds(g, 1), :]).then_inc(b_w[b], 16)

                for b in range(2):
                    group_weights(b, b)
                with sp.Fori(1, GROUPS_B // 2) as i:
                    for b in range(2):
                        sp.wait_ge(b_down, 2 * i + b + 1)
                        group_weights(2 * i + b, b)
            if stop == "A":
                sp.wait_ge(a_res, 2 + BLOCKS)
                sp.dma_start(out_v, x_tok[:]).then_inc(done, 16)
                sp.wait_ge(done, 16)
            if "C" in stages:
                for k in range(2):
                    sp.wait_ge(b_sc[k], 16 * 16)
                reload(sp, y_even, x_tok)
            if "D" in stages:
                normed_v = normed.rearrange("(t p) c -> p t c", p=P)
                for n in range(BLOCKS):
                    sp.wait_ge(d_xn, n + 1)
                    sp.dma_start(normed_v[:, 4 * n:4 * n + 4, :], extra[:, 4 * n:4 * n + 4, :]).then_inc(d_tab, 16)
                results_v = results[0:PAIRS, :].rearrange("(k t p) c -> k p t c", k=2, p=P)
                for b in range(4):
                    sp.wait_ge(e_st[b], 16 * TILES_D // 4)
                for n in range(BLOCKS):
                    for k, dst in enumerate((back1, back2)):
                        sp.dma_start(dst[:, 4 * n:4 * n + 4, :],
                                     results_v[k, :, 4 * n:4 * n + 4, :]).then_inc(f_back[n], 16)
            out_w = out.rearrange("(t r w c) k -> w r c t k", r=8, w=2, c=8)

            def store(n):
                for w in range(2):
                    for r in range(8):
                        at = WIN * w + 8 * r
                        sp.dma_start(out_w[w, r], x_tok[at:at + 8]).then_inc(done, 16)
                sp.wait_ge(done, 16 * 16)

            if stop == "A":
                sp.wait_ge(a_res, 2 + BLOCKS)
                sp.dma_start(out_v, x_tok[:]).then_inc(done, 16)
                sp.wait_ge(done, 16)
            if stop == "B":
                for k in range(2):
                    sp.wait_ge(b_sc[k], 16 * 16)
                sp.dma_start(x_tok[:], y_even.rearrange("(t p) c -> p t c", p=P)).then_inc(done, 16)
                sp.dma_start(extra[:], y_odd.rearrange("(t p) c -> p t c", p=P)).then_inc(done, 16)
                sp.wait_ge(d_var, 1)
                sp.dma_start(out_v, x_tok[:]).then_inc(done, 16)
                sp.wait_ge(done, 48)
            if stop == "C":
                sp.wait_ge(c_res, 2 + TILES)
                store(0)
            if stop == "D":
                sp.wait_ge(f_sum, 2 * TILES)
                store(0)

        @block.gpsimd
        def _(pool):
            nc.gpsimd.memset(scratch[:], 0.0).then_inc(s_pad, 1)
            nc.gpsimd.memset(ones_row[:], 1.0).then_inc(s_pad, 1)
            nc.gpsimd.memset(zeros[:], 0.0).then_inc(s_zero, 1)
            if "B" in stages:
                for k in range(BITS):
                    nc.gpsimd.memset(bits[:, k:k + 1], 1 << (BITS - 1 - k)).then_inc(b_bits, 1)
                nc.gpsimd.memset(bits[:, BITS:], 0).then_inc(b_bits, 1)

                for b in range(2):
                    pool.wait_ge(b_tab[b], 16 + 8 * BLOCKS)
                pool.wait_ge(b_gtab, 64)
                pool.wait_ge(b_idx, 2)
                pool.wait_ge(b_init, 16 * (4 + 16))
                LAG = 3
                for g in range(GROUPS_B + LAG):
                    done_g = g - LAG
                    if done_g >= 0:
                        pool.wait_ge(b_y, 2 + done_g + 1)
                    for k in range(4):
                        if done_g >= 0:
                            e = 4 * done_g + k
                            if e > 1:
                                pool.wait_ge(b_sc[k % 2], 16 * (e // 2))
                            nc.gpsimd.indirect_dma_start(
                                out=(y_even, y_odd)[k % 2][:, :],
                                out_offset=bass.IndirectOffsetOnAxis(ap=idx_w[:, e:e + 1], axis=0),
                                in_=y_b[:, done_g % 2, k, :], in_offset=None, bounds_check=TOKENS - 1,
                                oob_is_err=True, compute_op=ALU.add,
                            ).then_inc(b_sc[k % 2], 16)
                        if g < GROUPS_B and k % 2:
                            for e in (4 * g + k - 1, 4 * g + k):
                                nc.gpsimd.indirect_dma_start(
                                    out=rows_b[:, g % 4, e % 4, :], out_offset=None, in_=table[:, :],
                                    in_offset=bass.IndirectOffsetOnAxis(ap=idx[:, e:e + 1], axis=0),
                                    bounds_check=TOKENS - 1, oob_is_err=True,
                                ).then_inc(b_gath[g % 4], 16)

            if "C" in stages:
                pool.sem_inc(c_res, 2)

                def value_bias(t, b):
                    pool.wait_ge(c_xn, t + 1)
                    xs = x_tok[:, bass.ds(t, 1), :]
                    nc.gpsimd.tensor_tensor(xs, xs, vb_sb[:].unsqueeze(1), ALU.add).then_inc(c_vb, 1)

                def values(t, b):
                    pool.wait_ge(c_va, t + 1)
                    pool.wait_ge(c_av, t + 1)
                    nc.gpsimd.tensor_tensor(
                        v_x[:, b, :, :, :, 0:HDIM].rearrange("p w a h d -> p (w a) h d"),
                        extra[:, bass.ds(t, 1), :].rearrange("p o (a d) -> p (o a) d", d=HDIM).unsqueeze(2)
                        .to_broadcast([P, 16, 2, HDIM]),
                        C("half").unsqueeze(1).unsqueeze(3).to_broadcast([P, 16, 2, HDIM]), ALU.mult).then_inc(c_v, 1)

                def minus_peak(t, b):
                    pool.wait_ge(c_mx, t + 1)
                    v = score[:, b, :].rearrange("p (h j) -> p h j", j=WIN)
                    nc.gpsimd.tensor_tensor(v, v, peak[:, b, :].unsqueeze(2).to_broadcast([P, HEADS, WIN]),
                                            ALU.subtract).then_inc(c_sub, 1)

                def residual(t, b):
                    pool.wait_ge(c_o, 7 + t + 1)
                    pool.wait_ge(c_vb, t + 1)
                    xs = x_tok[:, bass.ds(t, 1), :]
                    nc.gpsimd.tensor_tensor(xs, xs, att[:, b:b + 1, :], ALU.add).then_inc(c_res, 1)

                staggered(pool, TILES, [(residual, 8), (values, 6), (minus_peak, 4), (value_bias, 1)])
            if "D" in stages:
                for k in range(2):
                    pairs = slice(TILES * k, TILES * (k + 1))
                    pool.wait_ge(d_oh, k + 1)
                    nc.gpsimd.tensor_tensor(oh_value[:, pairs, 1, :], oh_tile[:, pairs, :],
                                            C("pair_no")[:, pairs].unsqueeze(2).to_broadcast([P, TILES, TILES_D]),
                                            ALU.mult).then_inc(d_oht, 1)
                pool.wait_ge(d_tab, 16 * BLOCKS)
                pool.wait_ge(d_idx, 2)

                def gather(t):
                    nc.gpsimd.indirect_dma_start(
                        out=rows_d[:, t % 4, :], out_offset=None, in_=normed[:, :],
                        in_offset=bass.IndirectOffsetOnAxis(ap=gather_i[:, t:t + 1], axis=0),
                        bounds_check=TOKENS - 1, oob_is_err=True).then_inc(e_ld[t % 4], 16)

                for t in range(4):
                    gather(t)
                for t in range(TILES_D):
                    if t + 4 < TILES_D:
                        pool.wait_ge(e_tr, t + 1)
                        gather(t + 4)
                    pool.wait_ge(e_y, 1 + t + 1)
                    nc.gpsimd.indirect_dma_start(
                        out=results[:, :],
                        out_offset=bass.IndirectOffsetOnAxis(ap=dest_i[:, t:t + 1], axis=0),
                        in_=y_d[:, t % 4, :], in_offset=None, bounds_check=PAIRS + TILES_D * P - 1,
                        oob_is_err=True).then_inc(e_st[t % 4], 16)

        @block.vector
        def _(dve):
            def norm_stats(var_ready, sqrt_done, eps, loaded=None):
                def stats_of(t, n):
                    for k in range(n):
                        ins = nc.vector.bn_stats(stats[:, bass.ds(t + k, 1), :], x_tok[:, bass.ds(t + k, 1), :])
                    ins.then_inc(dve_seq, 1)
                    dve_n.next()

                dve.wait_ge(dve_seq, dve_n.now())
                if loaded:
                    for c in range(4):
                        loaded(c)
                        stats_of(8 * c, 8)
                else:
                    with dve_n.loop(dve, TILES // 8, 1) as i:
                        stats_of(8 * i, 8)
                dve.wait_ge(dve_seq, dve_n.now())
                even, odd = stats[:, :, 1], stats[:, :, 4]
                nc.vector.tensor_tensor(gap[:], even, odd, ALU.subtract).then_inc(dve_seq, 1)
                nc.vector.tensor_tensor(mean[:], even, odd, ALU.add).then_inc(dve_seq, 1)
                nc.vector.tensor_tensor(spread[:], stats[:, :, 2], stats[:, :, 5], ALU.add).then_inc(dve_seq, 1)
                for _ in range(3):
                    dve_n.next()
                dve.wait_ge(dve_seq, dve_n.now())
                nc.vector.tensor_scalar(mean[:], mean[:], 0.5, None, ALU.mult).then_inc(dve_seq, 1)
                nc.vector.scalar_tensor_tensor(gap[:], gap[:], 0.25, gap[:], ALU.mult, ALU.mult).then_inc(dve_seq, 1)
                nc.vector.tensor_scalar(spread[:], spread[:], 1.0 / P, eps, ALU.mult, ALU.add).then_inc(dve_seq, 1)
                for _ in range(3):
                    dve_n.next()
                dve.wait_ge(dve_seq, dve_n.now())
                nc.vector.tensor_tensor(var_eps[:], spread[:], gap[:], ALU.add).then_inc(var_ready, 1)
                dve.wait_ge(sqrt_done, 1)
                nc.vector.reciprocal(rstd[:], std[:]).then_inc(dve_seq, 1)
                dve.wait_ge(dve_seq, dve_n.next())

            def norm(dst, t):
                return nc.vector.tensor_scalar(dst, x_tok[:, bass.ds(t, 1), :], mean[:, bass.ds(t, 1)],
                                               rstd[:, bass.ds(t, 1)], ALU.subtract, ALU.mult)

            norm_stats(a_var, a_sqrt, 1e-6, lambda c: dve.wait_ge(ld_x[c], 16))
            with dve.Fori(0, BLOCKS // 2) as i:
                for b in range(2):
                    dve.wait_ge(a_tr, 2 * i + b + 1)
                    for k in range(4):
                        ins = norm(xn[:, b, k, :], 8 * i + 4 * b + k)
                    ins.then_inc(a_xn, 1)
            dve.sem_inc(a_res, 2)
            with dve.Fori(0, BLOCKS // 2) as i:
                for b in range(2):
                    dve.wait_ge(a_back, 2 + 2 * i + b + 1)
                    xs = x_tok[:, bass.ds(8 * i + 4 * b, 4), :]
                    nc.vector.tensor_tensor(xs, psum[:, 4 + b, :].rearrange("p (t c) -> p t c", c=P), xs,
                                            ALU.add).then_inc(a_res, 1)
            if "B" not in stages:
                return

            dve.wait_ge(a_res, 2 + BLOCKS)
            norm_stats(b_var, b_sqrt, 1e-5)
            with dve.Fori(0, BLOCKS // 2) as i:
                for b in range(2):
                    dve.wait_ge(b_tr, 2 * i + b + 1)
                    dve.wait_ge(b_tab[b], 16 * i + 16)
                    for k in range(4):
                        ins = norm(xn[:, b, k, :], 8 * i + 4 * b + k)
                    ins.then_inc(b_xn, 1)
            dve.wait_ge(b_logit, BLOCKS)
            dve.wait_ge(ld_w, 16 * len(LOADS))
            logits = psum[:, 6:8, :].rearrange("p a (t e) -> p (a t) e", e=EXPERTS_B)
            nc.vector.tensor_tensor(gate[:].rearrange("p (g j) e -> p g j e", j=4),
                                    logits.rearrange("p (j g) e -> p g j e", j=4),
                                    br_sb[:].unsqueeze(1).unsqueeze(1).to_broadcast([P, 8, 4, EXPERTS_B]),
                                    ALU.add).then_inc(dve_seq, 1)
            dve.wait_ge(dve_seq, dve_n.next())
            nc.vector.tensor_reduce(top[:], gate[:], AX.X, ALU.max).then_inc(dve_seq, 1)
            dve.wait_ge(dve_seq, dve_n.next())
            nc.vector.tensor_tensor(gate[:], gate[:], top[:].unsqueeze(2).to_broadcast([P, TILES, EXPERTS_B]),
                                    ALU.subtract).then_inc(b_sub, 1)
            dve.wait_ge(b_exp, 1)
            nc.vector.tensor_reduce(total[:], gate[:], AX.X, ALU.add).then_inc(dve_seq, 1)
            dve.wait_ge(dve_seq, dve_n.next())
            nc.vector.reciprocal(inv[:], total[:]).then_inc(dve_seq, 1)
            dve.wait_ge(dve_seq, dve_n.next())
            nc.vector.tensor_tensor(gate[:], gate[:], inv[:].unsqueeze(2).to_broadcast([P, TILES, EXPERTS_B]),
                                    ALU.mult).then_inc(b_gate, 1)

            dve.wait_ge(b_gtr, 2)
            nc.vector.tensor_copy(by_expert[:].rearrange("p (a n) -> p a n", a=2), psum[:, 0:2, :]).then_inc(b_be, 1)
            nc.vector.memset(thr[:], 0)
            nc.vector.memset(kept[:], 0.0)
            nc.vector.tensor_copy(same16[:], C("same_expert")).then_inc(dve_seq, 1)
            dve_n.next()
            dve.wait_ge(b_be, 1)
            dve.wait_ge(b_bits, BITS + 1)
            nc.vector.tensor_copy(cand[:], bits[:, 0:1]).then_inc(dve_seq, 1)
            dve_n.next()
            with dve_n.loop(dve, BITS // 5, 15) as i:
                for k in range(5):
                    dve.wait_ge(dve_seq, dve_n.now())
                    nc.vector.tensor_scalar(above, by_expert[:], cand[:].bitcast(F32), None, ALU.is_ge, ALU.add,
                                            accum_out=count16[:]).then_inc(b_cnt, 1)
                    nc.vector.tensor_tensor(thr[:].bitcast(F32), thr[:].bitcast(F32), kept[:],
                                            ALU.max).then_inc(dve_seq, 1)
                    dve.wait_ge(dve_seq, dve_n.next())
                    dve.wait_ge(b_sum, 5 * i + k + 1)
                    nc.vector.tensor_scalar(kept[:], psum[:, 2, 0:1], float(CAP), cand[:].bitcast(F32), ALU.is_ge,
                                            ALU.mult).then_inc(dve_seq, 1)
                    dve.wait_ge(dve_seq, dve_n.next())
                    nc.vector.scalar_tensor_tensor(cand[:], kept[:].bitcast(I32), bits[:, bass.ds(5 * i + k + 1, 1)],
                                                   thr[:], ALU.bitwise_or, ALU.bitwise_or).then_inc(dve_seq, 1)
                    dve_n.next()
            dve.wait_ge(dve_seq, dve_n.now())
            nc.vector.tensor_tensor(thr[:].bitcast(F32), thr[:].bitcast(F32), kept[:], ALU.max).then_inc(dve_seq, 1)
            dve.wait_ge(dve_seq, dve_n.next())
            nc.vector.tensor_scalar(above, by_expert[:], thr[:].bitcast(F32), None, ALU.is_gt, ALU.add,
                                    accum_out=count[:, 0:1]).then_inc(b_tot, 1)
            nc.vector.tensor_scalar(tied, by_expert[:], thr[:].bitcast(F32), None, ALU.is_equal, ALU.add,
                                    accum_out=count[:, 1:2]).then_inc(b_tot, 1)
            dve.wait_ge(b_tot, 2)
            nc.vector.tensor_tensor_scan(n_above, zeros[:], above, 0.0, ALU.add, ALU.add).then_inc(dve_seq, 1)
            dve_n.next()
            nc.vector.tensor_tensor_scan(n_tied, zeros[:], tied, 0.0, ALU.add, ALU.add).then_inc(dve_seq, 1)
            dve_n.next()
            dve.wait_ge(b_off, 1)
            nc.vector.tensor_copy(offs[:], psum[:, 3, 0:2]).then_inc(dve_seq, 1)
            dve.wait_ge(dve_seq, dve_n.next())
            nc.vector.scalar_tensor_tensor(n_above, n_above, offs[:, 0:1], above, ALU.add, ALU.mult).then_inc(dve_seq, 1)
            dve_n.next()
            nc.vector.scalar_tensor_tensor(n_tied, n_tied, offs[:, 1:2], tied, ALU.add, ALU.mult).then_inc(dve_seq, 1)
            dve.wait_ge(dve_seq, dve_n.next())
            nc.vector.scalar_tensor_tensor(n_above, n_above, -1.0, n_tied, ALU.add, ALU.add).then_inc(b_pos, 1)

            dve.wait_ge(b_ptr, 2)
            nc.vector.tensor_copy(place[:].rearrange("p (a t) e -> p a (t e)", a=2), psum[:, 0:2, :]).then_inc(dve_seq, 1)
            dve_n.next()
            nc.vector.tensor_copy(slot_hi[:].rearrange("p h a e -> p (h a e)"), C("slot_hi")).then_inc(dve_seq, 1)
            dve_n.next()
            nc.vector.tensor_copy(slot_lo[:].rearrange("p a e -> p (a e)"), C("slot_lo")).then_inc(dve_seq, 1)
            dve.wait_ge(dve_seq, dve_n.next())
            nc.vector.tensor_scalar(place2[:], place[:], 4, None, ALU.arith_shift_right).then_inc(dve_seq, 1)
            dve.wait_ge(dve_seq, dve_n.next())
            nc.vector.tensor_copy(hi16[:], place2[:]).then_inc(dve_seq, 1)
            dve.wait_ge(dve_seq, dve_n.next())
            nc.vector.tensor_scalar(place2[:], place[:], 15, None, ALU.bitwise_and).then_inc(dve_seq, 1)
            dve.wait_ge(dve_seq, dve_n.next())
            nc.vector.tensor_copy(lo16[:], place2[:]).then_inc(dve_seq, 1)
            dve.wait_ge(dve_seq, dve_n.next())
            with dve.Fori(0, TILES // 4) as i:
                for k in range(4):
                    u, b = 4 * i + k, k
                    dve.wait_ge(b_ohmm, u + 1)
                    nc.vector.tensor_tensor(oh_hi[:, b], hi16[:, bass.ds(u, 1), :].rearrange("p o (h e) -> p (o h) e", h=2)
                                            .unsqueeze(2).to_broadcast([P, 2, 8, 16]),
                                            slot_hi[:], ALU.is_equal).then_inc(b_ohhi, 1)
                    nc.vector.tensor_tensor(oh_lo[:, b], lo16[:, bass.ds(u, 1), :].to_broadcast([P, 16, EXPERTS_B]),
                                            slot_lo[:], ALU.is_equal).then_inc(b_oh, 1)
            dve.wait_ge(b_ohmm, 4 + TILES)
            for h in range(2):
                nc.vector.tensor_tensor(picked[:, h], psum[:, 4 + h, 0:256].rearrange("p (l e) -> p l e", e=16),
                                        C("same_e16").unsqueeze(1).to_broadcast([P, 16, 16]),
                                        ALU.mult).then_inc(dve_seq, 1)
                dve_n.next()
            dve.wait_ge(dve_seq, dve_n.now())
            nc.vector.tensor_reduce(ids_f[:], picked[:], AX.X, ALU.add).then_inc(dve_seq, 1)
            dve.wait_ge(dve_seq, dve_n.next())
            nc.vector.tensor_tensor(ids_x[:], ids_f[:].unsqueeze(2).to_broadcast([P, 2, 8, 16]),
                                    C("same_slot_hi").unsqueeze(1).unsqueeze(3).to_broadcast([P, 2, 8, 16]),
                                    ALU.mult).then_inc(b_ids, 1)
            dve.wait_ge(b_idt, 1)
            nc.vector.tensor_scalar(idx[:], psum[:, 2, 0:EXPERTS_B], float(ID_SHIFT), None, ALU.add).then_inc(b_idx, 1)
            dve.wait_ge(b_idx, 1)
            nc.vector.tensor_scalar(idx_w[:], idx[:], TOKENS - P + 7, None, ALU.bitwise_and)
            nc.vector.tensor_scalar(id_row[:], idx[:], 7 * 16, 1, ALU.bitwise_and, ALU.arith_shift_right)
            nc.vector.tensor_scalar(id_win[:], idx[:], 8, 3, ALU.bitwise_and, ALU.logical_shift_left).then_inc(dve_seq, 1)
            dve.wait_ge(dve_seq, dve_n.next())
            nc.vector.tensor_tensor(idx_w[:], idx_w[:], id_row[:], ALU.bitwise_or).then_inc(dve_seq, 1)
            dve.wait_ge(dve_seq, dve_n.next())
            nc.vector.tensor_tensor(idx_w[:], idx_w[:], id_win[:], ALU.bitwise_or).then_inc(b_idx, 1)

            dve.sem_inc(b_y, 2)
            dve.sem_inc(b_xgt, 2)

            def experts(g, slot, reused):
                b = slot % 2
                dve.wait_ge(b_xg, g + 1)
                nc.vector.tensor_copy(xt[:, b, :], psum[:, b, :]).then_inc(b_xgt, 1)
                dve.wait_ge(b_down, g + 3)
                if reused:
                    for k in range(2):
                        dve.wait_ge(b_sc[k], 32 * g - 32)
                for k in range(4):
                    e = 4 * g + k
                    ins = nc.vector.tensor_scalar(y_b[:, b, k, :], psum[:, 5 + b, P * k:P * (k + 1)],
                                                  rows_b[:, slot, k, bass.ds(P + e, 1)], None, ALU.mult)
                ins.then_inc(b_y, 1)

            for g in range(4):
                experts(g, g, g > 1)
            with dve.Fori(1, GROUPS_B // 4) as i:
                for slot in range(4):
                    experts(4 * i + slot, slot, True)
            if stop == "B":
                dve.wait_ge(done, 32)
                nc.vector.tensor_tensor(x_tok[:], x_tok[:], extra[:], ALU.add).then_inc(d_var, 1)
            if "C" not in stages:
                return

            def heads(ap):
                return ap.rearrange("p (h j) -> p h j", j=WIN)

            for w in range(2):
                nc.vector.tensor_tensor(heads(rel[:, w, :]), heads(rel[:, w, :]),
                                        msk[:, w, :].unsqueeze(1).to_broadcast([P, HEADS, WIN]),
                                        ALU.add).then_inc(c_rel, 1)
                nc.vector.tensor_copy(v_x[:, w, :, :, :, HDIM].rearrange("p w a h -> p (w a) h"),
                                      C("half").unsqueeze(1).to_broadcast([P, 16, 2])).then_inc(c_one, 1)
            dve.wait_ge(c_rel, 2)

            def sum_chunk(c):
                dve.wait_ge(c_ld[c], 16 * 2)
                xs = x_tok[:, 8 * c:8 * c + 8, :]
                nc.vector.tensor_tensor(xs, xs, extra[:, 8 * c:8 * c + 8, :], ALU.add).then_inc(c_sum, 1)
                dve.wait_ge(c_sum, c + 1)

            norm_stats(c_var, c_sqrt, 1e-6, sum_chunk)
            dve.sem_inc(c_k, 1)
            dve.sem_inc(c_sb, 2)
            dve.sem_inc(c_o, 7)

            def norm_tile(t, b):
                dve.wait_ge(c_tr, t + 1)
                norm(xn[:, b, 0, :], t).then_inc(c_xn, 1)

            def keys(t, b):
                dve.wait_ge(c_q, t + 1)
                dve.wait_ge(c_va, t + 1)
                dve.wait_ge(c_s, t + 1)
                nc.vector.scalar_tensor_tensor(k_x[:, b], psum[:, 1, P:2 * P].unsqueeze(1).to_broadcast([P, 8, P]),
                                               qkb[:, 1:2], C("head_of_8").unsqueeze(2).to_broadcast([P, 8, P]),
                                               ALU.add, ALU.mult).then_inc(c_k, 1)

            def add_bias(t, b):
                dve.wait_ge(c_s, 2 + t + 1)
                dve.wait_ge(c_exp, t + 1)
                nc.vector.tensor_tensor(score[:, b, :].rearrange("p (q n) -> p q n", q=2),
                                        psum[:, 2 + 2 * b:4 + 2 * b, :],
                                        rel[:, b, :].rearrange("p (q n) -> p q n", q=2), ALU.add).then_inc(c_sb, 1)

            def find_peak(t, b):
                dve.wait_ge(c_sb, 2 + t + 1)
                nc.vector.tensor_reduce(peak[:, b, :], heads(score[:, b, :]), AX.X, ALU.max).then_inc(c_mx, 1)

            def normalize(t, b):
                dve.wait_ge(c_av, 2 + t + 1)
                dve.wait_ge(c_res, t + 1)
                o = psum[:, 0, P:P + HEADS * (HDIM + 1)].rearrange("p (h d) -> p h d", d=HDIM + 1)
                nc.vector.reciprocal(inv_sum[:, b, :], o[:, :, HDIM]).then_inc(c_one, 1)
                dve.wait_ge(c_one, 2 + t + 1)
                nc.vector.tensor_tensor(att[:, b, :].rearrange("p (h d) -> p h d", d=HDIM), o[:, :, 0:HDIM],
                                        inv_sum[:, b, :].unsqueeze(2).to_broadcast([P, HEADS, HDIM]),
                                        ALU.mult).then_inc(c_o, 1)

            staggered(dve, TILES, [(add_bias, 4), (normalize, 8), (keys, 2), (find_peak, 4), (norm_tile, 0)])
            if "D" not in stages:
                return

            dve.wait_ge(c_res, 2 + TILES)
            norm_stats(d_var, d_sqrt, 1e-5)
            with dve.Fori(0, BLOCKS) as i:
                for k in range(4):
                    ins = norm(extra[:, bass.ds(4 * i + k, 1), :], 4 * i + k)
                ins.then_inc(d_xn, 1)

            def link(ins):
                ins.then_inc(dve_seq, 1)
                dve.wait_ge(dve_seq, dve_n.next())

            def wide(ap):
                return ap.unsqueeze(2).to_broadcast(TE)

            rank8 = C("rank8").unsqueeze(1).to_broadcast(TE)
            dve.wait_ge(d_log, BLOCKS)
            nc.vector.tensor_copy(tri_b[:], C("tri"))
            nc.vector.memset(ones_b[:], 1.0)
            link(nc.vector.tensor_copy(lg[:].rearrange("p t e -> p (t e)"), psum[:, 2, 0:TILES * EXPERTS_D]))

            def best(top_of, onehot):
                link(nc.vector.tensor_reduce(top_of[:], lg[:], AX.X, ALU.max))
                link(nc.vector.tensor_tensor(hit[:], lg[:], wide(top_of[:]), ALU.is_equal))
                link(nc.vector.tensor_tensor(hit[:], hit[:], rank8, ALU.mult))
                link(nc.vector.tensor_reduce(rank[:], hit[:], AX.X, ALU.max))
                link(nc.vector.tensor_tensor(onehot[:], rank8, wide(rank[:]), ALU.is_equal))

            best(peak1, first)
            link(nc.vector.scalar_tensor_tensor(lg[:], first[:], -3.0e38, lg[:], ALU.mult, ALU.add))
            best(peak2, second)
            nc.vector.tensor_tensor(ratio[:], peak2[:], peak1[:], ALU.subtract).then_inc(d_dm, 1)
            nc.vector.tensor_tensor(chosen[:], first[:], second[:], ALU.add).then_inc(d_sel, 1)
            dve.wait_ge(d_ex, 1)
            link(nc.vector.tensor_scalar(weight2[:], ratio[:], 1.0, None, ALU.add))
            link(nc.vector.reciprocal(weight1[:], weight2[:]))
            link(nc.vector.tensor_tensor(weight2[:], ratio[:], weight1[:], ALU.mult))
            dve.wait_ge(d_pre, 1)
            inside = psum[:, 3, 0:256].rearrange("p (t e) -> p t e", e=EXPERTS_D)
            link(nc.vector.tensor_copy(n_tile[:], psum[:, 3, 256:512].rearrange("p (t e) -> p e t", e=EXPERTS_D)))
            link(nc.vector.tensor_tensor_scan(n_run[:].rearrange("p e t -> p (e t)"), C("restart"),
                                              n_tile[:].rearrange("p e t -> p (e t)"), 0.0, ALU.mult, ALU.add))
            link(nc.vector.tensor_scalar(tiles_i[:], n_run[:, :, TILES - 1], float(P - 1), None, ALU.add))
            link(nc.vector.tensor_scalar(tiles_i[:], tiles_i[:], 7, None, ALU.arith_shift_right))
            link(nc.vector.tensor_copy(tiles_f[:], tiles_i[:]))
            link(nc.vector.tensor_tensor_scan(end_tile[:], zeros[:, 0:EXPERTS_D], tiles_f[:], 0.0, ALU.add, ALU.add))
            link(nc.vector.tensor_tensor(base[:], end_tile[:], tiles_f[:], ALU.subtract))
            link(nc.vector.tensor_scalar(base[:], base[:], float(P), -1.0, ALU.mult, ALU.add))
            link(nc.vector.tensor_tensor(n_run[:], n_run[:], n_tile[:], ALU.subtract))
            link(nc.vector.tensor_tensor(n_run[:], n_run[:], base[:].unsqueeze(2).to_broadcast([P, EXPERTS_D, TILES]),
                                         ALU.add))
            link(nc.vector.tensor_tensor(slot_f[:], inside, n_run[:].rearrange("p e t -> p t e"), ALU.add))
            for k, onehot in enumerate((first, second)):
                link(nc.vector.tensor_tensor(hit[:], slot_f[:], onehot[:], ALU.mult))
                link(nc.vector.tensor_reduce(slot_of[:, k, :], hit[:], AX.X, ALU.add))
            link(nc.vector.tensor_copy(slot_i[:], slot_of[:]))
            pair_list = "p k t -> p (k t)"
            link(nc.vector.tensor_scalar(part_i[:], slot_i[:], P - 1, None, ALU.bitwise_and))
            link(nc.vector.tensor_copy(slot_lane[:], part_i[:].rearrange(pair_list)))
            link(nc.vector.tensor_scalar(part_i[:], slot_i[:], 7, None, ALU.arith_shift_right))
            link(nc.vector.tensor_copy(slot_tile[:], part_i[:].rearrange(pair_list)))
            for k in range(2):
                pairs = slice(TILES * k, TILES * (k + 1))
                n_p = [P, TILES, TILES_D]
                nc.vector.tensor_tensor(oh_tile[:, pairs, :], C("tile_no").unsqueeze(1).to_broadcast(n_p),
                                        slot_tile[:, pairs].unsqueeze(2).to_broadcast(n_p),
                                        ALU.is_equal).then_inc(d_oh, 1)
                nc.vector.tensor_tensor(oh_lane[:, pairs, :], C("lane").unsqueeze(1).to_broadcast([P, TILES, P]),
                                        slot_lane[:, pairs].unsqueeze(2).to_broadcast([P, TILES, P]),
                                        ALU.is_equal).then_inc(d_lane, 1)
            link(nc.vector.tensor_tensor(past[:], C("tile_no").unsqueeze(2).to_broadcast([P, TILES_D, EXPERTS_D]),
                                         end_tile[:].unsqueeze(1).to_broadcast([P, TILES_D, EXPERTS_D]), ALU.is_ge))
            link(nc.vector.tensor_reduce(tile_e[:], past[:], AX.X, ALU.add))
            nc.vector.tensor_scalar(tile_ei[:], tile_e[:], float(EXPERTS_D - 1), None, ALU.min).then_inc(d_map, 1)
            dve.wait_ge(d_inv, 1)
            link(nc.vector.tensor_copy(pair_f[:], psum[:, 4, 0:TILES_D]))
            link(nc.vector.scalar_tensor_tensor(pair_f[:], psum[:, 4, TILES_D:2 * TILES_D], float(P), pair_f[:],
                                                ALU.mult, ALU.add))
            link(nc.vector.scalar_tensor_tensor(dest_f[:], pair_f[:], 0.0, C("spare_row"), ALU.is_equal, ALU.mult))
            link(nc.vector.tensor_tensor(dest_f[:], dest_f[:], pair_f[:], ALU.add))
            nc.vector.tensor_scalar(dest_i[:], dest_f[:], float(-P), None, ALU.add).then_inc(d_idx, 1)
            link(nc.vector.tensor_scalar(gather_i[:], pair_f[:], float(TOKENS - P), None, ALU.add))
            nc.vector.tensor_scalar(gather_i[:], gather_i[:], TOKENS - 1, None, ALU.bitwise_and).then_inc(d_idx, 1)

            dve.sem_inc(e_act, 2)
            dve.sem_inc(e_ate, 1)

            def product(t, b):
                dve.wait_ge(e_silu, 2 + t + 1)
                dve.wait_ge(e_h3, t + 1)
                nc.vector.tensor_tensor(act_d[:, b, :], silu_d[:, b, :], psum[:, 3 + b, 0:FF_D],
                                        ALU.mult).then_inc(e_act, 1)

            def step(t, b):
                b %= 2
                dve.wait_ge(e_at, t + 1)
                nc.vector.tensor_copy(act_dt[:, b, :], psum[:, 5, 0:FF_D]).then_inc(e_ate, 1)
                if not (isinstance(t, int) and t == TILES_D - 1):
                    product(t + 1, 1 - b)

            product(0, 0)
            rounds(dve, TILES_D, 2, step, head=0)

            for n in range(BLOCKS):
                dve.wait_ge(f_back[n], 16 * 2)
                for k, (w, rows) in enumerate(((weight1, back1), (weight2, back2))):
                    if k:
                        dve.wait_ge(f_sum, 8 * n + 4)
                    for t in range(4 * n, 4 * n + 4):
                        nc.vector.scalar_tensor_tensor(x_tok[:, t, :], rows[:, t, :], w[:, t:t + 1], x_tok[:, t, :],
                                                       ALU.mult, ALU.add).then_inc(f_sum, 1)

        @block.scalar
        def _(act):
            for dst, src in CONV_LOADS:
                act.dma_start(dst, src).then_inc(ld_conv, 16)

            def root(var_ready, sqrt_done):
                act.wait_ge(var_ready, 1)
                nc.scalar.activation(std[:], var_eps[:], ACT.Sqrt).then_inc(sqrt_done, 1)

            root(a_var, a_sqrt)
            act.wait_ge(s_pad, 1)
            act.sem_inc(a_pad, 2)
            with act.Fori(0, BLOCKS // 2) as i:
                for b in range(2):
                    act.wait_ge(a_tr, 2 + 2 * i + b + 1)
                    nc.scalar.copy(xpad[:, bass.ds(4 * i + 2 * b, 2), 1:SIDE + 1, 1:SIDE + 1],
                                   psum[:, b, :].rearrange("p (n a c) -> p n a c", n=2, a=SIDE)).then_inc(a_pad, 1)
            act.wait_ge(ld_conv, 16 * len(CONV_LOADS))
            act.sem_inc(a_relu, 2)
            with act.Fori(0, BLOCKS // 2) as i:
                for b in range(2):
                    act.wait_ge(a_conv, 2 * i + b + 1)
                    act.wait_ge(a_back, 2 * i + b + 1)
                    nc.scalar.activation(conv_t[:, b, :], psum[:, 2 + b, :], ACT.Relu,
                                         bias=conv_bs[:, 0:1]).then_inc(a_relu, 1)
            if "B" not in stages:
                return
            root(b_var, b_sqrt)
            act.sem_inc(b_xt, 2)
            with act.Fori(0, BLOCKS // 2) as i:
                for b in range(2):
                    act.wait_ge(b_tr, 2 + 2 * i + b + 1)
                    nc.scalar.copy(xt[:, b, :], psum[:, b, :]).then_inc(b_xt, 1)
            act.wait_ge(b_sub, 1)
            nc.scalar.activation(gate[:], gate[:], ACT.Exp).then_inc(b_exp, 1)
            token0 = const_at["token_id"][0]
            with act.Fori(0, TILES // 4) as i:
                for k in range(4):
                    u, b = 4 * i + k, k
                    act.wait_ge(b_ohhi, u + 1)
                    act.wait_ge(b_ohmm, u + 1)
                    nc.scalar.activation(oh_id[:, b].rearrange("p h a e -> p (h a e)"),
                                         oh_hi[:, b].rearrange("p h a e -> p (h a e)"), ACT.Copy,
                                         scale=cst[:, bass.ds(token0 + u, 1)]).then_inc(b_ohid, 1)
            act.sem_inc(b_act, 3)
            with act.Fori(0, GROUPS_B // 2) as i:
                for b in range(2):
                    g = 2 * i + b
                    for c, (_, n) in enumerate(CHUNKS_B):
                        act.wait_ge(b_up, 3 * g + c + 1)
                        nc.scalar.activation(act_b[0:n, b, c, :], psum[0:n, 2 + c, :], ACT.Silu,
                                             bias=bu_sb[0:n, bass.ds(g, 1), c]).then_inc(b_act, 1)

            if "C" not in stages:
                return
            for k in range(2):
                act.wait_ge(b_sc[k], 16 * 16)
            reload(act, y_odd, extra)
            root(c_var, c_sqrt)
            nc.scalar.mul(qb_scaled[:], qkb[:, 0:1], SCALE).then_inc(c_qb, 1)
            act.sem_inc(c_xt, 1)
            act.sem_inc(c_exp, 2)
            act.sem_inc(c_pe, 2)
            act.wait_ge(c_qb, 1)

            def evac_normed(t, b):
                act.wait_ge(c_tr, 2 + t + 1)
                act.wait_ge(c_qkv, t + 1)
                nc.scalar.copy(xt[:, b, 0:P], psum[:, 0, 0:P]).then_inc(c_xt, 1)

            def evac_query_value(t, b):
                act.wait_ge(c_qkv, 2 + t + 1)
                act.wait_ge(c_s, t + 1)
                nc.scalar.activation(q_t[:, b, :], psum[:, 1, 0:P], ACT.Identity, bias=qb_scaled[:, 0:1],
                                     scale=SCALE).then_inc(c_q, 1)
                nc.scalar.copy(extra[:, bass.ds(t, 1), :], psum[:, 1:2, 2 * P:3 * P]).then_inc(c_va, 1)

            def exponent(t, b):
                act.wait_ge(c_sub, t + 1)
                act.wait_ge(c_pt, 2 * t + 2)
                nc.scalar.activation(prob[:, b, :], score[:, b, :], ACT.Exp).then_inc(c_exp, 1)

            def evac_prob(t, b):
                act.wait_ge(c_av, t + 1)
                for h in range(2):
                    act.wait_ge(c_pt, 4 + 2 * t + h + 1)
                    nc.scalar.copy(prob_t[:, b, 512 * h:512 * h + 512], psum[:, 6 + h, :]).then_inc(c_pe, 1)

            staggered(act, TILES, [(evac_query_value, 2), (evac_normed, 1), (exponent, 5), (evac_prob, 6)])
            if "D" not in stages:
                return
            root(d_var, d_sqrt)
            act.sem_inc(d_xt, 2)
            for n in range(BLOCKS):
                act.wait_ge(d_tr, n + 1)
                nc.scalar.copy(xt[:, n % 2, :], psum[:, n % 2, :]).then_inc(d_xt, 1)
            act.wait_ge(d_dm, 1)
            nc.scalar.activation(ratio[:], ratio[:], ACT.Exp).then_inc(d_ex, 1)

            for k in range(2):
                pairs = slice(TILES * k, TILES * (k + 1))
                act.wait_ge(d_oh, k + 1)
                nc.scalar.activation(oh_value[:, pairs, 0, :], oh_tile[:, pairs, :], ACT.Copy,
                                     scale=C("partition")).then_inc(d_ohp, 1)

            act.sem_inc(e_silu, 2)
            act.sem_inc(e_xt, 1)
            act.sem_inc(e_y, 1)

            def rows_t(t, b):
                act.wait_ge(e_tr, t + 1)
                nc.scalar.copy(xt_d[:, b, :], psum[:, 0, 0:P]).then_inc(e_xt, 1)

            def silu(t, b):
                act.wait_ge(e_h1, t + 1)
                act.wait_ge(e_act, t + 1)
                nc.scalar.activation(silu_d[:, b, :], psum[:, 1 + b, 0:FF_D], ACT.Silu).then_inc(e_silu, 1)

            def step(t, b):
                c = b % 2
                if not (isinstance(t, int) and t == TILES_D - 1):
                    silu(t + 1, 1 - c)
                if not (isinstance(t, int) and t >= TILES_D - 2):
                    rows_t(t + 2, c)
                act.wait_ge(e_yp, t + 1)
                if not (isinstance(t, int) and t < 4):
                    act.wait_ge(e_st[b], 4 * (t - b))
                nc.scalar.copy(y_d[:, b, :], psum[:, 6, 0:P]).then_inc(e_y, 1)

            rows_t(0, 0)
            rows_t(1, 1)
            silu(0, 0)
            rounds(act, TILES_D, 4, step)

        @block.tensor
        def _(pe):
            def transpose(dst, src):
                return nc.tensor.transpose(dst, src, ident)

            pe.wait_ge(ld_conv, 16 * len(CONV_LOADS))
            pe.sem_inc(a_tr, 2)
            with pe.Fori(0, BLOCKS // 2) as i:
                for b in range(2):
                    pe.wait_ge(a_xn, 2 * i + b + 1)
                    pe.wait_ge(a_pad, 2 * i + b + 1)
                    for k in range(4):
                        ins = transpose(psum[:, b, P * k:P * (k + 1)], xn[:, b, k, :])
                    ins.then_inc(a_tr, 1)
            pe.sem_inc(a_back, 2)
            with pe.Fori(0, BLOCKS // 2) as i:
                for b in range(2):
                    pe.wait_ge(a_pad, 2 + 2 * i + b + 1)
                    pe.wait_ge(a_relu, 2 * i + b + 1)
                    for tap in range(TAPS):
                        dy, dx = tap // 3, tap % 3
                        ins = nc.tensor.matmul(psum[:, 2 + b, :], conv_sb[:, tap, :],
                                               xpad[:, bass.ds(4 * i + 2 * b, 2), dy:dy + SIDE, dx:dx + SIDE],
                                               start=tap == 0, stop=tap == TAPS - 1)
                    ins.then_inc(a_conv, 1)
                for b in range(2):
                    pe.wait_ge(a_relu, 2 + 2 * i + b + 1)
                    pe.wait_ge(a_res, 2 * i + b + 1)
                    for k in range(4):
                        ins = transpose(psum[:, 4 + b, P * k:P * (k + 1)], conv_t[:, b, P * k:P * (k + 1)])
                    ins.then_inc(a_back, 1)
            if "B" not in stages:
                return

            pe.wait_ge(ld_w, 16 * len(LOADS))
            pe.sem_inc(b_down, 2)
            pe.sem_inc(b_tr, 2)
            with pe.Fori(0, BLOCKS // 2) as i:
                for b in range(2):
                    pe.wait_ge(b_xn, 2 * i + b + 1)
                    pe.wait_ge(b_xt, 2 * i + b + 1)
                    for k in range(4):
                        ins = transpose(psum[:, b, P * k:P * (k + 1)], xn[:, b, k, :])
                    ins.then_inc(b_tr, 1)
                for b in range(2):
                    pe.wait_ge(b_xt, 2 + 2 * i + b + 1)
                    flat = psum[:, 6:8, :].rearrange("p a n -> p (a n)")
                    for k in range(4):
                        ins = nc.tensor.matmul(flat[:, bass.ds((8 * i + 4 * b + k) * EXPERTS_B, EXPERTS_B)],
                                               xt[:, b, P * k:P * (k + 1)], wr_sb[:], start=True, stop=True)
                    ins.then_inc(b_logit, 1)
            pe.wait_ge(b_gate, 1)
            for g in range(8):
                ins = transpose(psum[:, g // 4, P * (g % 4):P * (g % 4 + 1)], gate[:, 4 * g:4 * g + 4, :].rearrange("p j e -> p (j e)"))
                if g % 4 == 3:
                    ins.then_inc(b_gtr, 1)
            with pe.Fori(0, BITS) as i:
                pe.wait_ge(b_cnt, i + 1)
                nc.tensor.matmul(psum[:, 2, 0:1], same16[:], count16[:], start=True,
                                 stop=True).then_inc(b_sum, 1)
            pe.wait_ge(b_tot, 2)
            nc.tensor.matmul(psum[:, 3, 0:2], C("earlier_segment"), count[:, 0:2], start=True, stop=False,
                             skip_group_check=True)
            nc.tensor.matmul(psum[:, 3, 1:2], C("same_expert"), count[:, 0:1], start=False, stop=True,
                             skip_group_check=True).then_inc(b_off, 1)
            pe.wait_ge(b_pos, 1)
            for g in range(8):
                ins = transpose(psum[:, g // 4, P * (g % 4):P * (g % 4 + 1)], n_above[:, P * g:P * (g + 1)])
                if g % 4 == 3:
                    ins.then_inc(b_ptr, 1)
            pe.sem_inc(b_ohmm, 4)
            for u in range(TILES):
                pe.wait_ge(b_oh, u + 1)
                pe.wait_ge(b_ohid, u + 1)
                for h in range(2):
                    ins = nc.tensor.matmul(psum[:, 4 + h, 0:256], oh_id[:, u % 4, h].rearrange("p a e -> p (a e)"),
                                           oh_lo[:, u % 4, :, 16 * h:16 * h + 16], start=u == 0, stop=u == TILES - 1)
                ins.then_inc(b_ohmm, 1)

            pe.wait_ge(b_ids, 1)
            for h in range(2):
                ins = nc.tensor.matmul(psum[:, 2, 16 * h:16 * h + 16], ids_x[:, h].rearrange("p a l -> p (a l)"),
                                       C("same_e16"), start=True, stop=True)
            ins.then_inc(b_idt, 1)

            with pe.Fori(0, GROUPS_B // 4) as i:
                for slot in range(4):
                    g, b = 4 * i + slot, slot % 2
                    pe.wait_ge(b_gath[slot], 64 * i + 64)
                    pe.wait_ge(b_xgt, g + 1)
                    for k in range(4):
                        ins = transpose(psum[:, b, P * k:P * (k + 1)], rows_b[:, slot, k, 0:P])
                    ins.then_inc(b_xg, 1)
                    pe.wait_ge(b_xgt, 2 + g + 1)
                    pe.wait_ge(b_w[b], 96 * i + 48 * (slot // 2 + 1))
                    for c, (f, n) in enumerate(CHUNKS_B):
                        pe.wait_ge(b_act, 3 * g + c + 1)
                        nc.tensor.matmul(psum[0:n, 2 + c, :], wu_sb[:, b, f:f + n], xt[:, b, :], start=True,
                                         stop=True).then_inc(b_up, 1)
                    pe.wait_ge(b_y, g + 1)
                    nc.tensor.matmul(psum[:, 5 + b, :], ones_row[:], bd_sb[:, b, :], start=True, stop=False,
                                     skip_group_check=True)
                    for c, (f, n) in enumerate(CHUNKS_B):
                        pe.wait_ge(b_act, 3 + 3 * g + c + 1)
                        for k in range(4):
                            ins = nc.tensor.matmul(psum[:, 5 + b, P * k:P * (k + 1)],
                                                   act_b[0:n, b, c, P * k:P * (k + 1)], wd_sb[0:n, b, k, c, :],
                                                   start=False, stop=c == 2, skip_group_check=True)
                    ins.then_inc(b_down, 1)
            if "C" not in stages:
                return

            pe.sem_inc(c_tr, 2)
            pe.sem_inc(c_qkv, 2)
            pe.sem_inc(c_s, 2)
            pe.sem_inc(c_pt, 4)
            pe.sem_inc(c_av, 2)

            def products(t, b):
                pe.wait_ge(c_xt, 1 + t + 1)
                pe.wait_ge(c_k, t + 1)
                for k in range(2):
                    nc.tensor.matmul(psum[:, 1, P * k:P * (k + 1)], wqkv[:, P * k:P * (k + 1)], xt[:, b, 0:P],
                                     start=True, stop=True)
                for w in range(2):
                    for h in range(2):
                        o = psum[WIN * h:WIN * h + WIN, 1, 2 * P + WIN * w:2 * P + WIN * (w + 1)]
                        cols = slice(2 * P + WIN * h, 2 * P + WIN * (h + 1))
                        ins = nc.tensor.matmul(o, xt[:, b, WIN * w:WIN * (w + 1)], wqkv[:, cols], start=True, stop=True)
                ins.then_inc(c_qkv, 1)

            def transpose_normed(t, b):
                pe.wait_ge(c_xn, t + 1)
                pe.wait_ge(c_xt, t + 1)
                pe.wait_ge(c_o, t + 1)
                transpose(psum[:, 0, 0:P], xn[:, b, 0, :]).then_inc(c_tr, 1)

            def scores_wait(t, b):
                pe.wait_ge(c_q, t + 1)
                pe.wait_ge(c_k, 1 + t + 1)
                pe.wait_ge(c_sb, t + 1)

            def scores(t, b):
                for q in range(2):
                    rows = slice(64 * q, 64 * q + 64)
                    for w in range(2):
                        ins = nc.tensor.matmul(psum[WIN * w:WIN * (w + 1), 2 + 2 * b + q, :],
                                               q_t[rows, b, WIN * w:WIN * (w + 1)],
                                               k_x[rows, b, :, WIN * w:WIN * (w + 1)], start=True, stop=True)
                ins.then_inc(c_s, 1)

            def transpose_prob(t, b):
                pe.wait_ge(c_exp, 2 + t + 1)
                for h in range(2):
                    pe.wait_ge(c_pe, 2 * t + h + 1)
                    for k in range(4):
                        at = 512 * h + P * k
                        ins = transpose(psum[:, 6 + h, P * k:P * (k + 1)], prob[:, b, at:at + P])
                    ins.then_inc(c_pt, 1)

            def weigh_values(t, b):
                pe.wait_ge(c_pe, 2 + 2 * t + 2)
                pe.wait_ge(c_v, t + 1)
                pe.wait_ge(c_o, 7 + t)
                last = min(t + 6, TILES - 1) if isinstance(t, int) else t + 6
                pe.wait_ge(c_xt, 1 + last + 1)
                for pair in range(8):
                    for w in range(2):
                        n = 2 * (HDIM + 1)
                        ins = nc.tensor.matmul(psum[WIN * w:WIN * (w + 1), 0, P + n * pair:P + n * (pair + 1)],
                                               prob_t[:, b, P * pair + WIN * w:P * pair + WIN * (w + 1)],
                                               v_x[:, b, w, pair].rearrange("p h d -> p (h d)"), start=True, stop=True)
                ins.then_inc(c_av, 1)

            pe.wait_ge(c_one, 2)
            staggered(pe, TILES, [(products, 2), (scores_wait, 3), (transpose_normed, 1), (scores, 3), (transpose_prob, 6),
                                  (weigh_values, 7)])
            if "D" not in stages:
                return

            for n in range(BLOCKS + 1):
                if n < BLOCKS:
                    pe.wait_ge(d_xn, n + 1)
                    pe.wait_ge(d_xt, n + 1)
                    for k in range(4):
                        ins = transpose(psum[:, n % 2, P * k:P * (k + 1)], extra[:, 4 * n + k, :])
                    ins.then_inc(d_tr, 1)
                if n > 0:
                    pe.wait_ge(d_xt, 2 + n)
                    for k in range(4):
                        t = 4 * (n - 1) + k
                        ins = nc.tensor.matmul(psum[:, 2, EXPERTS_D * t:EXPERTS_D * (t + 1)],
                                               xt[:, (n - 1) % 2, P * k:P * (k + 1)], gw[:], start=True, stop=True)
                    ins.then_inc(d_log, 1)
            pe.wait_ge(d_sel, 1)
            flat = chosen[:].rearrange("p t e -> p (t e)")
            nc.tensor.matmul(psum[:, 3, 0:256], tri_b[:], flat, start=True, stop=True)
            nc.tensor.matmul(psum[:, 3, 256:512], ones_b[:], flat, start=True, stop=True).then_inc(d_pre, 1)

            for j in range(2 * TILES):
                if j % TILES == 0:
                    pe.wait_ge(d_lane, j // TILES + 1)
                    pe.wait_ge(d_oht, j // TILES + 1)
                    pe.wait_ge(d_ohp, j // TILES + 1)
                ins = nc.tensor.matmul(psum[:, 4, 0:2 * TILES_D], oh_lane[:, j, :],
                                       oh_value[:, j].rearrange("p a n -> p (a n)"), start=j == 0,
                                       stop=j == 2 * TILES - 1)
            ins.then_inc(d_inv, 1)
            pe.wait_ge(d_map, 1)
            pe.wait_ge(d_idx, 2)

            def rows_t(t, b):
                pe.wait_ge(e_ld[b], 4 * (t - b) + 16)
                pe.wait_ge(e_xt, t + 1)
                transpose(psum[:, 0, 0:P], rows_d[:, b, :]).then_inc(e_tr, 1)

            def up(weights, bank, ready, t, b, e):
                nc.tensor.matmul(psum[:, bank, 0:FF_D], xt_d[:, b, :], weights[:, bass.ds(e, 1), :], start=True,
                                 stop=True).then_inc(ready, 1)

            def expert_of(t):
                return pe.value_load(tile_ei[0:1, bass.ds(t, 1)], min_val=0, max_val=EXPERTS_D - 1)

            def experts_of(t, n):
                return nc.values_load_multi_w_load_instructions(
                    tile_ei[0:1, bass.ds(t, n)], engines=(mybir.EngineType.PE,), min_val=0, max_val=EXPERTS_D - 1)[1]

            def first_up(t, b, e):
                pe.wait_ge(e_xt, 1 + t + 1)
                pe.wait_ge(e_silu, t + 1)
                up(w1_sb, 1 + b, e_h1, t, b, e)

            def second_up(t, b, e):
                pe.wait_ge(e_act, t + 1)
                up(w3_sb, 3 + b, e_h3, t, b, e)

            def step(t, b, e_now, e_next):
                c = b % 2
                last = isinstance(t, int) and t == TILES_D - 1
                if not last:
                    first_up(t + 1, 1 - c, e_next)
                pe.wait_ge(e_act, 2 + t + 1)
                pe.wait_ge(e_ate, t + 1)
                for k in range(CHUNKS_D):
                    ins = transpose(psum[:, 5, P * k:P * (k + 1)], act_d[:, c, P * k:P * (k + 1)])
                ins.then_inc(e_at, 1)
                if not last:
                    second_up(t + 1, 1 - c, e_next)
                if not (isinstance(t, int) and t >= TILES_D - 2):
                    rows_t(t + 2, (b + 2) % 4)
                pe.wait_ge(e_ate, 1 + t + 1)
                pe.wait_ge(e_y, t + 1)
                for k in range(CHUNKS_D):
                    ins = nc.tensor.matmul(psum[:, 6, 0:P], act_dt[:, c, P * k:P * (k + 1)],
                                           w2_sb[:, bass.ds(e_now, 1), k, :], start=k == 0, stop=k == CHUNKS_D - 1)
                ins.then_inc(e_yp, 1)

            rows_t(0, 0)
            rows_t(1, 1)
            e = expert_of(0)
            first_up(0, 0, e)
            second_up(0, 0, e)
            with pe.Fori(0, TILES_D // 8 - 1) as i:
                e = experts_of(8 * i, 9)
                for k in range(8):
                    step(8 * i + k, k, e[k], e[k + 1])
            e = experts_of(TILES_D - 8, 8)
            for k in range(8):
                step(TILES_D - 8 + k, k, e[k], e[min(k + 1, 7)])


_IN_NAMES = ["x", "conv_w", "conv_b", "w_router", "b_router", "w_up", "b_up", "w_down", "b_down",
             "qkv_w", "qk_bias", "v_bias", "rel_bias", "mask", "gate_w", "w1", "w3", "w2", "const"]


def lay_out(inputs):
    import numpy as np
    a = {k: np.asarray(v) for k, v in inputs.items()}
    k = a["L0_conv_kernel"]
    width = k.shape[2]
    conv = np.zeros((P, TAPS, P), k.dtype)
    for g in range(P // width):
        s = slice(g * width, (g + 1) * width)
        conv[s, :, s] = k.reshape(TAPS, width, P)[:, :, s].transpose(1, 0, 2)
    up = a["L0_ffn_W_up"]
    b_up = np.zeros((GROUPS_B, 3 * P), up.dtype)
    b_up[:, :FF_B] = a["L0_ffn_b_up"]
    down = np.zeros((EXPERTS_B, 3 * P, P), up.dtype)
    down[:, :FF_B] = a["L0_ffn_W_down"]
    w0 = np.stack(np.meshgrid(np.arange(8), np.arange(8), indexing="ij")).reshape(2, -1)
    rel = w0[:, :, None] - w0[:, None, :] + 7
    rel = rel[0] * 15 + rel[1]
    bias = a["L1_conv_bias_table"][rel].transpose(0, 2, 1)
    qb = a["L1_conv_qkv_b"]
    w2 = a["L1_ffn_w2"]
    v_cols = np.arange(P).reshape(HEADS // 2, 2, HDIM).transpose(1, 0, 2).ravel()
    qkv_cols = np.concatenate([np.arange(2 * P), 2 * P + v_cols])
    return {
        "x": a["x"].reshape(TOKENS, P),
        "conv_w": conv.reshape(P, TAPS * P),
        "conv_b": a["L0_conv_bias"].reshape(P, 1),
        "w_router": a["L0_ffn_W_router"],
        "b_router": a["L0_ffn_b_router"],
        "w_up": up.transpose(1, 0, 2),
        "b_up": b_up.reshape(GROUPS_B, 3, P).transpose(2, 0, 1),
        "w_down": down.reshape(EXPERTS_B, 3, P, P).transpose(2, 0, 1, 3).reshape(P, -1),
        "b_down": a["L0_ffn_b_down"].reshape(GROUPS_B, 4 * P),
        "qkv_w": a["L1_conv_qkv_w"].T[:, qkv_cols],
        "qk_bias": qb[:2 * P].reshape(2, P).T,
        "v_bias": qb[2 * P:].reshape(1, P),
        "rel_bias": np.concatenate([bias, bias]).reshape(P, HEADS * WIN),
        "mask": window_mask(),
        "gate_w": a["L1_ffn_gate_w"].T,
        "w1": a["L1_ffn_w1"].transpose(2, 0, 1),
        "w3": a["L1_ffn_w3"].transpose(2, 0, 1),
        "w2": w2.transpose(2, 0, 1).reshape(CHUNKS_D, P, EXPERTS_D, P).transpose(1, 2, 0, 3),
    }


STOP = "D"


def kernel(**inputs):
    import numpy as _np
    import concourse.bacc as _bacc
    from concourse import mybir as _mybir
    from concourse.bass_utils import run_bass_kernel_spmd as _run

    nc = _bacc.Bacc("TRN2", target_bir_lowering=False, num_devices=1)
    laid = lay_out(inputs)
    laid["const"], const_at = constants()
    arrays, args = {}, []
    for name in _IN_NAMES:
        a = _np.ascontiguousarray(laid[name])
        arrays[f"in_{name}_dram"] = a
        args.append(nc.dram_tensor(f"in_{name}_dram", a.shape, _mybir.dt.from_np(a.dtype), kind="ExternalInput").ap())
    args.append(nc.dram_tensor("out_0_dram", (TOKENS, P), F32, kind="ExternalOutput").ap())
    metaformer(nc, const_at, *args, stop=STOP)
    r = _run(nc, [arrays], core_ids=[0])
    return r.results[0]["out_0_dram"].reshape(IMAGES, SIDE, SIDE, P)
```

```python
from contextlib import ExitStack, contextmanager

import concourse.bass as bass
from concourse import mybir

F32 = mybir.dt.float32
F16 = mybir.dt.float16
I32 = mybir.dt.int32
BF16 = mybir.dt.bfloat16
ALU = mybir.AluOpType
ACT = mybir.ActivationFunctionType
AX = mybir.AxisListType

P = 128
IMAGES, SIDE = 16, 16
TOKENS = IMAGES * SIDE * SIDE
TILES = TOKENS // P
BLOCKS = TILES // 4
PAD = SIDE + 2
TAPS = 9
EXPERTS_B, GROUPS_B = 32, 8
CAP = TOKENS // EXPERTS_B
FF_B = 341
CHUNKS_B = [(0, 128), (128, 128), (256, FF_B - 256)]
ROW_B = P + EXPERTS_B
HEADS, HDIM, WIN = 16, 8, 64
SCALE = HDIM ** -0.5
CHUNKS_C = 4
EXPERTS_D, FF_D = 8, 384
CHUNKS_D = FF_D // P
PAIRS = 2 * TOKENS
UNROLL_D = 8
EARLY_D = 6
DIGITS = 5
TILES_D = PAIRS // P + EXPERTS_D
ID_SHIFT = 2048
RANK_DIGITS, DIGIT_BITS = 3, 10
STRIDES = [4 ** k for k in reversed(range(DIGIT_BITS // 2))]
SEG = TOKENS // 4


def constants():
    import numpy as np
    p = np.arange(P)
    j, e = p // EXPERTS_B, p % EXPERTS_B
    parts = {}
    parts["ident"] = np.eye(P)
    parts["same_expert"] = e[:, None] == e[None, :]
    parts["earlier_segment"] = (e[:, None] == e[None, :]) & (j[:, None] < j[None, :])
    parts["head_of_8"] = (p[:, None] // HDIM) % 8 == np.arange(8)[None, :]
    parts["half"] = (p[:, None] // WIN) == np.arange(2)[None, :]
    u = np.arange(TILES)
    parts["token_id"] = ((u // 4 + 8 * (u % 4))[None, :] * P + p[:, None]) - ID_SHIFT
    parts["same_e16"] = p[:, None] % 16 == np.arange(16)[None, :]
    parts["same_slot_hi"] = p[:, None] // 16 == np.arange(8)[None, :]
    parts["tri"] = p[:, None] <= p[None, :]
    parts["rank8"] = np.broadcast_to(EXPERTS_D - np.arange(EXPERTS_D), (P, EXPERTS_D))
    parts["restart"] = np.broadcast_to(np.arange(EXPERTS_D * TILES) % TILES != 0, (P, EXPERTS_D * TILES))
    parts["tile_no"] = np.broadcast_to(np.arange(TILES_D), (P, TILES_D))
    parts["lane"] = np.broadcast_to(np.arange(P), (P, P))
    parts["partition"] = p[:, None]
    windowed = (p // 8) % 2 * WIN + p // 16 * 8 + p % 8
    parts["to_window"] = p[:, None] == windowed[None, :]
    parts["pair_no"] = np.broadcast_to(1 + np.arange(2 * TILES), (P, 2 * TILES))
    parts["spare_row"] = PAIRS + P + np.arange(TILES_D)[None, :] * P + p[:, None]
    parts["digit"] = np.broadcast_to(8 ** np.arange(DIGITS), (P, DIGITS))
    parts["slot_hi"] = np.broadcast_to(np.tile(np.repeat(np.arange(8), 16), 2), (P, 8 * EXPERTS_B))
    parts["slot_lo"] = np.broadcast_to(np.repeat(np.arange(16), EXPERTS_B), (P, 16 * EXPERTS_B))
    def candidates(stride):
        return np.array([0, stride, 2 * stride, 0.5 - 3 * stride])
    signs = np.array([1, 1, 1, -1])
    moves = [candidates(b) - candidates(a) for a, b in zip(STRIDES, STRIDES[1:] + [0])]
    parts["first_candidates"] = np.broadcast_to(signs + candidates(STRIDES[0]), (P, 4))
    parts["won"] = np.broadcast_to(np.concatenate([signs * n for n in STRIDES]), (P, 4 * len(STRIDES)))
    parts["move"] = np.broadcast_to(np.concatenate(moves), (P, 4 * len(STRIDES)))
    at, cols, n = {}, [], 0
    for name, a in parts.items():
        at[name] = (n, n + a.shape[1])
        n += a.shape[1]
        cols.append(a.astype(np.float32))
    return np.ascontiguousarray(np.concatenate(cols, 1)), at


def window_mask():
    import numpy as np
    region = np.zeros((SIDE, SIDE))
    cuts = (slice(0, -8), slice(-8, -4), slice(-4, None))
    for a, hs in enumerate(cuts):
        for b, ws in enumerate(cuts):
            region[hs, ws] = 3 * a + b
    win = region.reshape(2, 8, 2, 8).transpose(0, 2, 1, 3).reshape(2, 2, WIN)
    return (-100.0 * (win[:, :, :, None] != win[:, :, None, :])).astype(np.float32).reshape(2, P, WIN)


class Tally:

    def __init__(self):
        self.base, self.steps, self.i, self.per = 0, 0, None, 0

    def next(self):
        self.steps += 1
        return self.now()

    def now(self):
        if self.i is None:
            return self.base + self.steps
        return self.i * self.per + (self.base + self.steps)

    @contextmanager
    def loop(self, eng, rounds, per):
        self.base, self.steps = self.base + self.steps, 0
        with eng.Fori(0, rounds) as i:
            self.i, self.per = i, per
            yield i
            assert self.steps == per, (self.steps, per)
        self.base, self.steps, self.i = self.base + rounds * per, 0, None


def staggered(eng, n, parts):
    def step(first, k):
        for fn, lag in parts:
            t = first + k - lag
            if not isinstance(t, int) or 0 <= t < n:
                fn(t, (k - lag) % 2)

    depth = max(lag for _, lag in parts)
    head = depth + depth % 2
    for k in range(head):
        step(0, k)
    with eng.Fori(0, (n - head) // 2) as i:
        for k in range(head, head + 2):
            for fn, lag in parts:
                fn(2 * i + (k - lag), (k - lag) % 2)
    for k in range(n, n + depth):
        step(0, k)


def short_pipeline(n, parts):
    for k in range(n + max(lag for _, lag in parts)):
        for fn, lag in parts:
            if 0 <= k - lag < n:
                fn(k - lag)


def rounds(eng, n, width, step, head=1, tail=1):
    for t in range(head * width):
        step(t, t % width)
    with eng.Fori(head, n // width - tail) as i:
        for k in range(width):
            step(width * i + k, k)
    for t in range(n - tail * width, n):
        step(t, t % width)


def metaformer(nc, const_at, x, conv_w, conv_b, w_router, router_bias, w_up, up_bias, w_down, down_bias,
               qkv_w, qk_bias, v_bias, rel_bias, mask, gate_w, w1, w3, w2, const, out):
    with ExitStack() as ctx:
        def sb(name, shape, dt=F32):
            return ctx.enter_context(nc.sbuf_tensor(name, shape, dt))

        def sem(name):
            return ctx.enter_context(nc.semaphore(name))

        def dram(name, shape, dt=F32):
            return nc.dram_tensor(name, shape, dt, kind="Internal").ap()

        psum = ctx.enter_context(nc.psum_tensor("psum", [P, 8, 512], F32))

        table = dram("table", [TOKENS, ROW_B])
        y_even = dram("y_even", [TOKENS, P])
        y_odd = dram("y_odd", [TOKENS, P])
        normed = dram("normed", [TOKENS, P])
        results = dram("results", [PAIRS + TILES_D * P, P])

        x_tok = sb("x_tok", [P, TILES, P])
        extra = sb("extra", [P, TILES, P])
        scratch = sb("scratch", [P, 2 * BLOCKS * PAD * PAD])
        xpad = scratch[:, :].rearrange("p (n a b) -> p n a b", n=IMAGES, a=PAD)
        cst = sb("cst", [P, const.shape[1]])

        def C(name):
            a, b = const_at[name]
            return cst[:, a:b]

        ident = C("ident")
        zeros = sb("zeros", [P, 1024])
        ones_row = sb("ones_row", [1, P])
        arena = sb("arena", [P, 3 * 2 * HEADS * WIN])
        arena_b = sb("arena_b", [P, 2 * 3 * 512])

        def shared(pool_of, offset, shape, dt=F32):
            n = 1
            for d in shape[1:]:
                n *= d
            words = n // 2 if dt in (F16, BF16) else n
            v = pool_of[:, offset:offset + words]
            if dt != F32:
                v = v.bitcast(dt)
            if len(shape) > 2:
                names = "abcdefg"[:len(shape) - 1]
                v = v.rearrange(f"p ({' '.join(names)}) -> p {' '.join(names)}",
                                **{c: d for c, d in zip(names, shape[1:])})
            return v, offset + words

        stats = sb("stats", [P, TILES, 6])
        mean = sb("mean", [P, TILES])
        gap = sb("gap", [P, TILES])
        spread = sb("spread", [P, TILES])
        var_eps = sb("var_eps", [P, TILES])
        std = sb("std", [P, TILES])
        rstd = sb("rstd", [P, TILES])
        xn = sb("xn", [P, 2, 4, P])
        xt = sb("xt", [P, 2, 512])
        conv_sb = sb("conv_sb", [P, TAPS, P])
        conv_bs = sb("conv_bs", [P, 1])
        conv_t = sb("conv_t", [P, 2, 512])

        wqkv = sb("wqkv", [P, 3 * P])
        qkb = sb("qkb", [P, 2, 2])
        qb_scaled = sb("qb_scaled", [P, 2])
        vb_sb = sb("vb_sb", [P, P])
        rel = sb("rel", [P, 2, HEADS * WIN])
        msk = sb("msk", [P, 2, WIN])
        k_x, at = shared(arena_b, 0, [P, 2, 2, 8, WIN])
        q_x, at = shared(arena_b, at, [P, 2, 2, P])
        v_x = sb("v_x", [P, 2, 2, 8, 2, HDIM + 1])
        score, at = shared(arena, 0, [P, 2, HEADS * WIN])
        prob, at = shared(arena, at, [P, 2, HEADS * WIN])
        prob_t, at = shared(arena, at, [P, 2, HEADS * WIN])
        peak = sb("peak", [P, 2, HEADS])
        inv_sum = sb("inv_sum", [P, 2, HEADS])
        att = sb("att", [P, 2, P])

        gw = sb("gw", [P, EXPERTS_D])
        w13_sb = sb("w13_sb", [P, EXPERTS_D, 2, FF_D])
        w2_sb = sb("w2_sb", [P, EXPERTS_D, CHUNKS_D, P])
        TE = [P, TILES, EXPERTS_D]
        lg = sb("lg", TE)
        hit = sb("hit", TE)
        first = sb("first", TE)
        second = sb("second", TE)
        chosen = sb("chosen", TE, BF16)
        tri_b = sb("tri_b", [P, P], BF16)
        ones_b = sb("ones_b", [P, P], BF16)
        peak1 = sb("peak1", [P, TILES])
        peak2 = sb("peak2", [P, TILES])
        rank = sb("rank", [P, TILES])
        ratio = sb("ratio", [P, TILES])
        weights = sb("weights", [P, 2, TILES])
        weight1, weight2 = weights[:, 0, :], weights[:, 1, :]
        weights_i = sb("weights_i", [P, 2, TILES])
        n_tile = sb("n_tile", [P, EXPERTS_D, TILES])
        n_run = sb("n_run", [P, EXPERTS_D, TILES])
        tiles_i = sb("tiles_i", [P, EXPERTS_D], I32)
        tiles_f = sb("tiles_f", [P, EXPERTS_D])
        end_tile = sb("end_tile", [P, EXPERTS_D])
        base = sb("base", [P, EXPERTS_D])
        slot_f = sb("slot_f", TE)
        slot_of = sb("slot_of", [P, 2, TILES])
        slot_i = sb("slot_i", [P, 2, TILES], I32)
        part_i = sb("part_i", [P, 2, TILES], I32)
        slot_tile = sb("slot_tile", [P, 2 * TILES], BF16)
        slot_lane = sb("slot_lane", [P, 2 * TILES], BF16)
        lane_b = sb("lane_b", [P, P], BF16)
        tile_no_b = sb("tile_no_b", [P, TILES_D], BF16)
        PT = [P, 2 * TILES]
        oh_lane, _ = shared(scratch, 0, PT + [P], BF16)
        oh_tile, _ = shared(arena_b, 0, PT + [TILES_D], BF16)
        oh_value, _ = shared(arena, 0, PT + [2, TILES_D], BF16)
        pair_f = sb("pair_f", [P, TILES_D])
        dest_f = sb("dest_f", [P, TILES_D])
        gather_i = sb("gather_i", [P, TILES_D], I32)
        dest_i, dest_row, dest_win = (sb(n, [P, TILES_D], I32) for n in ("dest_i", "dest_row", "dest_win"))
        x_image = dram("x_image", [TOKENS, P])
        past = sb("past", [P, TILES_D, EXPERTS_D])
        tile_e = sb("tile_e", [P, TILES_D + UNROLL_D])
        digits = sb("digits", [P, 2, TILES_D // UNROLL_D, DIGITS])
        packed = sb("packed", [P, TILES_D // UNROLL_D, 2])
        packed_i = sb("packed_i", [P, TILES_D // UNROLL_D, 2], I32)
        rows_d, at = shared(arena, 0, [P, 4, P])
        xt_d, at = shared(arena, at, [P, 2, P])
        silu_d, at = shared(arena, at, [P, 2, FF_D])
        act_d, at = shared(arena, at, [P, 2, FF_D])
        y_d, at = shared(arena, at, [P, 4, P])
        w13_t, at = shared(arena, at, [P, 2, 2, FF_D])
        back1 = extra
        back2 = scratch[:, 0:TILES * P].rearrange("p (t c) -> p t c", c=P)

        wr_sb = sb("wr_sb", [P, EXPERTS_B])
        br_sb = sb("br_sb", [P, EXPERTS_B])
        gate = sb("gate", [P, TILES, EXPERTS_B])
        top = sb("top", [P, TILES])
        total = sb("total", [P, TILES])
        inv = sb("inv", [P, TILES])
        above, tied, n_above, n_tied = (scratch[:, SEG * k:SEG * (k + 1)] for k in range(4))
        gate_bits, at = shared(scratch, 0, [P, RANK_DIGITS, SEG], I32)
        digit16, at = shared(scratch, at, [P, RANK_DIGITS, SEG], F16)
        key, at = shared(arena_b, 0, [P, SEG], F16)
        is_above, at = shared(arena_b, at, [P, 2, SEG], F16)
        signs16, at = shared(arena_b, at, [P, SEG], F16)
        cand = sb("cand", [P, 4])
        moved = sb("moved", [P, 4])
        strides_won = sb("strides_won", [P, 1])
        reached = sb("reached", [P, 3])
        need = sb("need", [P, 1])
        thr_digit = sb("thr_digit", [P, RANK_DIGITS], I32)
        thr = sb("thr", [P, 1], I32)
        n_reach = sb("n_reach", [P, 2], F16)
        sign_sum = sb("sign_sum", [P, 1])
        n_higher = sb("n_higher", [P, 1], F16)
        start16 = sb("start16", [P, 3], F16)
        same16 = sb("same16", [P, P], F16)
        half_expert = sb("half_expert", [P, P])
        count = sb("count", [P, 2])
        offs = sb("offs", [P, 2])
        place, at = shared(arena_b, 0, [P, TILES, EXPERTS_B], I32)
        place2, at = shared(arena_b, at, [P, TILES, EXPERTS_B], I32)
        hi16, at = shared(arena_b, at, [P, TILES, EXPERTS_B], F16)
        lo16, at = shared(arena_b, at, [P, TILES, EXPERTS_B], F16)
        slot_hi = sb("slot_hi", [P, 2, 8, 16], F16)
        slot_lo = sb("slot_lo", [P, 16, EXPERTS_B], F16)
        oh_hi = sb("oh_hi", [P, 4, 2, 8, 16], F16)
        oh_id = sb("oh_id", [P, 4, 2, 8, 16], F16)
        oh_lo = sb("oh_lo", [P, 4, 16, EXPERTS_B], F16)
        picked = sb("picked", [P, 2, 16, 16])
        ids_f = sb("ids_f", [P, 2, 16])
        ids_x = sb("ids_x", [P, 2, 8, 16])
        idx = sb("idx", [P, EXPERTS_B], I32)
        idx_w, id_row, id_win = (sb(n, [P, EXPERTS_B], I32) for n in ("idx_w", "id_row", "id_win"))
        rows_b, _ = shared(scratch, 0, [P, 4, 4, ROW_B])
        wu_sb, at = shared(arena, 0, [P, 2, FF_B])
        wd_sb, at = shared(arena, at, [P, 2, 4, 3, P])
        bu_sb = sb("bu_sb", [P, GROUPS_B, 3])
        act_b, _ = shared(arena_b, 0, [P, 2, 3, 512])
        y_b, at = shared(arena, at, [P, 2, 4, P])
        bd_sb, at = shared(arena, at, [P, 2, 512])
        bd_sb = bd_sb[0:1]

        ld_x = [sem(f"ld_x{i}") for i in range(4)]
        ld_conv = sem("ld_conv")
        ld_ident = sem("ld_ident")
        ld_w = sem("ld_w")
        dve_seq = sem("dve_seq")
        dve_n = Tally()
        s_zero = sem("s_zero")
        s_pad = sem("s_pad")

        a_sqrt, b_sqrt, c_sqrt, d_sqrt = (sem(f"{s}_sqrt") for s in "abcd")
        a_var, b_var, c_var, d_var = (sem(f"{s}_var") for s in "abcd")
        a_xn = sem("a_xn")
        a_tr = sem("a_tr")
        a_pad = sem("a_pad")
        a_conv = sem("a_conv")
        a_relu = sem("a_relu")
        a_back = sem("a_back")
        a_res = sem("a_res")

        b_xn, b_tr, b_xt, b_logit = (sem(f"b_{s}") for s in ("xn", "tr", "xt", "logit"))
        b_tab = sem("b_tab")
        b_sub, b_exp, b_gate, b_gtab, b_gtr = (sem(f"b_{s}") for s in ("sub", "exp", "gate", "gtab", "gtr"))
        b_cnt, b_sum, b_tot, b_off, b_pos, b_ptr = (sem(f"b_{s}") for s in ("cnt", "sum", "tot", "off", "pos", "ptr"))
        b_oh, b_ohmm, b_ids, b_idt, b_idx, b_int, b_key, b_digit, b_cand, b_sign, b_won, b_higher, b_nsum = (
            sem(f"b_{s}") for s in ("oh", "ohmm", "ids", "idt", "idx", "int", "key", "digit", "cand", "sign", "won",
                                    "higher", "nsum"))
        b_xg, b_xgt, b_up, b_act, b_down, b_y = (
            sem(f"b_{s}") for s in ("xg", "xgt", "up", "act", "down", "y"))
        b_w = [sem(f"b_w{i}") for i in range(2)]
        b_gath = [sem(f"b_gath{i}") for i in range(4)]
        b_sc = [sem(f"b_sc{i}") for i in range(2)]
        b_init = sem("b_init")
        b_ohhi, b_ohid = sem("b_ohhi"), sem("b_ohid")
        done = sem("done")
        c_ld = [sem(f"c_ld{i}") for i in range(4)]
        (c_sum, c_rel, c_one, c_xn, c_tr, c_xt, c_qkv, c_q, c_k, c_v, c_s, c_sb, c_mx, c_sub, c_exp, c_pt,
         c_pe, c_av, c_o, c_res, c_va, c_vb, c_qb, c_qz) = (sem(f"c_{s}") for s in (
             "sum", "rel", "one", "xn", "tr", "xt", "qkv", "q", "k", "v", "s", "sb", "mx", "sub", "exp",
             "pt", "pe", "av", "o", "res", "va", "vb", "qb", "qz"))
        (d_xn, d_tr, d_xt, d_log, d_dm, d_ex, d_sel, d_pre, d_map, d_oh, d_ohp, d_oht, d_inv, d_idx) = (
            sem(f"d_{s}") for s in ("xn", "tr", "xt", "log", "dm", "ex", "sel", "pre", "map", "oh", "ohp", "oht",
                                    "inv", "idx"))
        d_tab = sem("d_tab")
        d_lane = sem("d_lane")
        d_wt, d_wi, d_ximg, d_xback = (sem(f"d_{n}") for n in ("wt", "wi", "ximg", "xback"))
        c_st = sem("c_st")
        f_scaled = sem("f_scaled")
        e_tr, e_xt, e_h1, e_h3, e_silu, e_act, e_yp, e_y, e_w = (
            sem(f"e_{s}") for s in ("tr", "xt", "h1", "h3", "silu", "act", "yp", "y", "w"))
        e_ld = [sem(f"e_ld{i}") for i in range(4)]
        e_st = [sem(f"e_st{i}") for i in range(4)]
        f_back = [sem(f"f_back{i}") for i in range(BLOCKS)]
        f_sum = sem("f_sum")

        x_v = x.rearrange("(t p) c -> p t c", p=P)
        out_v = out.rearrange("(t p) c -> p t c", p=P)

        block = ctx.enter_context(nc.Block())

        CONV_LOADS = [(conv_sb[:], conv_w.rearrange("p (t c) -> p t c", t=TAPS)), (conv_bs[:], conv_b)]
        LOADS = [(cst[:, P:], const[:, P:]), (wr_sb[:], w_router), (br_sb[:], router_bias.partition_broadcast(P)),
                 (bu_sb[:], up_bias),
                 (wqkv[:], qkv_w), (qkb[:], qk_bias), (vb_sb[:], v_bias.partition_broadcast(P)), (rel[:, 0, :], rel_bias),
                 (rel[:, 1, :], rel_bias), (msk[:], mask.rearrange("h p j -> p h j")), (gw[:], gate_w),
                 (w13_sb[:, :, 0, :], w1), (w13_sb[:, :, 1, :], w3), (w2_sb[:], w2)]

        def reload(queue, src, dst):
            src_v = src.rearrange("(t p) c -> p t c", p=P)
            for c in range(4):
                queue.dma_start(dst[:, 8 * c:8 * c + 8], src_v[:, 8 * c:8 * c + 8]).then_inc(c_ld[c], 16)

        def experts_of(n, engine):
            words = nc.values_load_multi_w_load_instructions(
                packed_i[0:1, bass.ds(n, 1), :].rearrange("p n k -> p (n k)"), engines=(engine,),
                min_val=0, max_val=8 ** DIGITS - 1)[1]
            return [(words[k // DIGITS] >> (3 * (k % DIGITS))) & 7 for k in range(2 * DIGITS)]

        @block.sync
        def _(sp):
            for c in range(4):
                sp.dma_start(x_tok[:, 8 * c:8 * c + 8, :], x_v[:, 8 * c:8 * c + 8, :]).then_inc(ld_x[c], 16)
            for dst, src in LOADS:
                sp.dma_start(dst, src).then_inc(ld_w, 16)
            sp.wait_ge(s_zero, 1)
            for c in range(4):
                sp.dma_start(y_odd.rearrange("(p line) c -> p (line c)", p=P)[:, 1024 * c:1024 * (c + 1)],
                             zeros[:]).then_inc(b_init, 16)
            tab_v = table.rearrange("(t p) c -> p t c", p=P)
            for n in range(BLOCKS):
                sp.wait_ge(b_xn, n + 1)
                sp.dma_start(tab_v[:, 4 * n:4 * n + 4, 0:P], xn[:, 1]).then_inc(b_tab, 16)
            sp.wait_ge(a_res, BLOCKS)
            y_windows = y_even.rearrange("(t win line col) k -> line win col t k", win=2, line=8, col=8)
            for r in range(8):
                for w in range(2):
                    at = 16 * r + 8 * w
                    sp.dma_start(y_windows[r, w], x_tok[at:at + 8]).then_inc(b_init, 16)
            sp.wait_ge(b_gate, 1)
            for j in range(4):
                sp.dma_start(tab_v[:, 8 * j:8 * j + 8, P:ROW_B], gate[:, j:TILES:4, :]).then_inc(b_gtab, 16)
            wd_v = w_down.rearrange("p (g e k c) -> p g e k c", g=GROUPS_B, e=4, k=3)

            def group_weights(g, b):
                sp.dma_start(wu_sb[:, b, :], w_up[:, bass.ds(g, 1), :]).then_inc(b_w[b], 16)
                sp.dma_start(wd_sb[:, b], wd_v[:, bass.ds(g, 1)]).then_inc(b_w[b], 16)
                sp.dma_start(bd_sb[:, b, :], down_bias[bass.ds(g, 1), :]).then_inc(b_w[b], 16)

            for b in range(2):
                group_weights(b, b)
            with sp.Fori(1, GROUPS_B // 2) as i:
                for b in range(2):
                    sp.wait_ge(b_down, 2 * i + b + 1)
                    group_weights(2 * i + b, b)
            for k in range(2):
                sp.wait_ge(b_sc[k], 16 * 16)
            reload(sp, y_even, x_tok)
            normed_v = normed.rearrange("(t p) c -> p t c", p=P)
            for n in range(BLOCKS):
                sp.wait_ge(d_xn, n + 1)
                sp.dma_start(normed_v[:, 4 * n:4 * n + 4, :], extra[:, 4 * n:4 * n + 4, :]).then_inc(d_tab, 16)
            sp.wait_ge(c_res, 2 + TILES)
            x_windows = x_image.rearrange("(t line win col) k -> win line col t k", line=8, win=2, col=8)
            for w in range(2):
                for r in range(8):
                    at = WIN * w + 8 * r
                    sp.dma_start(x_windows[w, r], x_tok[at:at + 8]).then_inc(d_ximg, 16)
            sp.wait_ge(d_ximg, 16 * 16)
            sp.dma_start(x_tok[:], x_image.rearrange("(t p) c -> p t c", p=P)).then_inc(d_xback, 16)
            results_v = results[0:PAIRS, :].rearrange("(k t p) c -> k p t c", k=2, p=P)
            for b in range(4):
                sp.wait_ge(e_st[b], 16 * TILES_D // 4)
            for n in range(BLOCKS):
                for k, dst in enumerate((back1, back2)):
                    sp.dma_start(dst[:, 4 * n:4 * n + 4, :],
                                 results_v[k, :, 4 * n:4 * n + 4, :]).then_inc(f_back[n], 16)
            for n in range(BLOCKS):
                sp.wait_ge(f_sum, n + 1)
                sp.dma_start(out_v[:, 4 * n:4 * n + 4, :], x_tok[:, 4 * n:4 * n + 4, :]).then_inc(done, 16)
            sp.wait_ge(done, 16 * BLOCKS)

        @block.gpsimd
        def _(pool):
            nc.gpsimd.memset(scratch[:], 0.0).then_inc(s_pad, 1)
            nc.gpsimd.memset(ones_row[:], 1.0).then_inc(s_pad, 1)
            nc.gpsimd.memset(zeros[:], 0.0).then_inc(s_zero, 1)
            pool.wait_ge(b_tab, 16 * BLOCKS)
            pool.wait_ge(b_gtab, 64)
            pool.wait_ge(b_idx, 2)
            pool.wait_ge(b_init, 16 * (4 + 16))
            LAG = 4
            for g in range(GROUPS_B + LAG):
                done_g = g - LAG
                if done_g >= 0:
                    pool.wait_ge(b_y, 2 + done_g + 1)
                for k in range(4):
                    if done_g >= 0:
                        e = 4 * done_g + k
                        if e > 1:
                            pool.wait_ge(b_sc[k % 2], 16 * (e // 2))
                        nc.gpsimd.indirect_dma_start(
                            out=(y_even, y_odd)[k % 2][:, :],
                            out_offset=bass.IndirectOffsetOnAxis(ap=idx_w[:, e:e + 1], axis=0),
                            in_=y_b[:, done_g % 2, k, :], in_offset=None, bounds_check=TOKENS - 1,
                            oob_is_err=True, compute_op=ALU.add,
                        ).then_inc(b_sc[k % 2], 16)
                    if g < GROUPS_B and k % 2:
                        for e in (4 * g + k - 1, 4 * g + k):
                            nc.gpsimd.indirect_dma_start(
                                out=rows_b[:, g % 4, e % 4, :], out_offset=None, in_=table[:, :],
                                in_offset=bass.IndirectOffsetOnAxis(ap=idx[:, e:e + 1], axis=0),
                                bounds_check=TOKENS - 1, oob_is_err=True,
                            ).then_inc(b_gath[g % 4], 16)

            nc.gpsimd.memset(q_x[:], 0.0).then_inc(c_qz, 1)
            pool.sem_inc(c_res, 2)
            for c in range(1, CHUNKS_C):
                pool.wait_ge(c_ld[c], 16 * 2)
                pool.wait_ge(c_sum, c)
                tiles = slice(8 * c, 8 * c + 8)
                nc.gpsimd.tensor_tensor(x_tok[:, tiles, :], x_tok[:, tiles, :], extra[:, tiles, :],
                                        ALU.add).then_inc(c_sum, 1)

            def value_bias(t, b):
                pool.wait_ge(c_xn, t + 1)
                xs = x_tok[:, bass.ds(t, 1), :]
                nc.gpsimd.tensor_tensor(xs, xs, vb_sb[:].unsqueeze(1), ALU.add).then_inc(c_vb, 1)

            def values(t, b):
                pool.wait_ge(c_va, t + 1)
                pool.wait_ge(c_av, t + 1)
                nc.gpsimd.tensor_tensor(
                    v_x[:, b, :, :, :, 0:HDIM].rearrange("p w a h d -> p (w a) h d"),
                    extra[:, bass.ds(t, 1), :].rearrange("p o (a d) -> p (o a) d", d=HDIM).unsqueeze(2)
                    .to_broadcast([P, 16, 2, HDIM]),
                    C("half").unsqueeze(1).unsqueeze(3).to_broadcast([P, 16, 2, HDIM]), ALU.mult).then_inc(c_v, 1)

            def minus_peak(t, b):
                pool.wait_ge(c_mx, t + 1)
                v = score[:, b, :].rearrange("p (h j) -> p h j", j=WIN)
                nc.gpsimd.tensor_tensor(v, v, peak[:, b, :].unsqueeze(2).to_broadcast([P, HEADS, WIN]),
                                        ALU.subtract).then_inc(c_sub, 1)

            def residual(t, b):
                pool.wait_ge(c_o, 7 + t + 1)
                pool.wait_ge(c_vb, t + 1)
                xs = x_tok[:, bass.ds(t, 1), :]
                nc.gpsimd.tensor_tensor(xs, xs, att[:, b:b + 1, :], ALU.add).then_inc(c_res, 1)

            staggered(pool, TILES, [(residual, 8), (values, 6), (minus_peak, 4), (value_bias, 1)])
            for k in range(2):
                pairs = slice(TILES * k, TILES * (k + 1))
                pool.wait_ge(d_oh, k + 1)
                nc.gpsimd.tensor_tensor(oh_value[:, pairs, 1, :], oh_tile[:, pairs, :],
                                        C("pair_no")[:, pairs].unsqueeze(2).to_broadcast([P, TILES, TILES_D]),
                                        ALU.mult).then_inc(d_oht, 1)
            pool.wait_ge(d_tab, 16 * BLOCKS)
            pool.wait_ge(d_idx, 1)

            def gather(t):
                nc.gpsimd.indirect_dma_start(
                    out=rows_d[:, t % 4, :], out_offset=None, in_=normed[:, :],
                    in_offset=bass.IndirectOffsetOnAxis(ap=gather_i[:, t:t + 1], axis=0),
                    bounds_check=TOKENS - 1, oob_is_err=True).then_inc(e_ld[t % 4], 16)

            def scatter(t):
                pool.wait_ge(e_y, 2 + t + 1)
                nc.gpsimd.indirect_dma_start(
                    out=results[:, :],
                    out_offset=bass.IndirectOffsetOnAxis(ap=dest_i[:, t:t + 1], axis=0),
                    in_=y_d[:, t % 4, :], in_offset=None, bounds_check=PAIRS + TILES_D * P - 1,
                    oob_is_err=True).then_inc(e_st[t % 4], 16)

            for t in range(4):
                gather(t)
            pool.wait_ge(d_idx, 2)
            for t in range(TILES_D):
                if t + 4 < TILES_D:
                    pool.wait_ge(e_tr, t + 1)
                    gather(t + 4)
                if t > 0:
                    scatter(t - 1)
            scatter(TILES_D - 1)

        @block.vector
        def _(dve):
            def stats_of(tiles):
                for t in range(tiles.start, tiles.stop):
                    ins = nc.vector.bn_stats(stats[:, t, :], x_tok[:, t, :])
                ins.then_inc(dve_seq, 1)
                dve.wait_ge(dve_seq, dve_n.next())

            def variance(tiles, var_ready, eps):
                even, odd = stats[:, tiles, 1], stats[:, tiles, 4]
                nc.vector.tensor_tensor(gap[:, tiles], even, odd, ALU.subtract)
                nc.vector.tensor_tensor(mean[:, tiles], even, odd, ALU.add)
                nc.vector.tensor_tensor(spread[:, tiles], stats[:, tiles, 2], stats[:, tiles, 5],
                                        ALU.add).then_inc(dve_seq, 1)
                dve.wait_ge(dve_seq, dve_n.next())
                nc.vector.tensor_scalar(mean[:, tiles], mean[:, tiles], 0.5, None, ALU.mult)
                nc.vector.scalar_tensor_tensor(gap[:, tiles], gap[:, tiles], 0.25, gap[:, tiles], ALU.mult, ALU.mult)
                nc.vector.tensor_scalar(spread[:, tiles], spread[:, tiles], 1.0 / P, eps, ALU.mult,
                                        ALU.add).then_inc(dve_seq, 1)
                dve.wait_ge(dve_seq, dve_n.next())
                nc.vector.tensor_tensor(var_eps[:, tiles], spread[:, tiles], gap[:, tiles],
                                        ALU.add).then_inc(var_ready, 1)

            def inverse_root(tiles, sqrt_done, n):
                dve.wait_ge(sqrt_done, n)
                nc.vector.reciprocal(rstd[:, tiles], std[:, tiles]).then_inc(dve_seq, 1)
                dve.wait_ge(dve_seq, dve_n.next())

            def norm(dst, t):
                return nc.vector.tensor_scalar(dst, x_tok[:, bass.ds(t, 1), :], mean[:, bass.ds(t, 1)],
                                               rstd[:, bass.ds(t, 1)], ALU.subtract, ALU.mult)

            def block_variance(n, var_ready, eps):
                tiles = slice(4 * n, 4 * n + 4)
                stats_of(tiles)
                variance(tiles, var_ready, eps)

            def block_norm(n, slot, sqrt_done, ready):
                inverse_root(slice(4 * n, 4 * n + 4), sqrt_done, n + 1)
                for k in range(4):
                    ins = norm(xn[:, slot, k, :], 4 * n + k)
                ins.then_inc(ready, 1)

            def variance_a(n):
                if n % 2 == 0:
                    dve.wait_ge(ld_x[n // 2], 16)
                block_variance(n, a_var, 1e-6)

            def norm_a(n):
                if n > 0:
                    dve.wait_ge(a_tr, n)
                block_norm(n, 0, a_sqrt, a_xn)

            def residual(n):
                dve.wait_ge(a_back, n + 1)
                dve.wait_ge(a_xn, n + 1)
                xs = x_tok[:, 4 * n:4 * n + 4, :]
                nc.vector.tensor_tensor(xs, psum[:, 4 + n % 2, :].rearrange("p (t c) -> p t c", c=P), xs,
                                        ALU.add).then_inc(a_res, 1)

            def variance_b(n):
                dve.wait_ge(a_res, n + 1)
                block_variance(n, b_var, 1e-5)

            def norm_b(n):
                if n > 0:
                    dve.wait_ge(b_tr, n)
                    dve.wait_ge(b_tab, 16 * n)
                block_norm(n, 1, b_sqrt, b_xn)

            short_pipeline(BLOCKS, [(variance_a, 0), (norm_a, 0), (norm_b, 4), (residual, 3), (variance_b, 3)])

            dve.wait_ge(b_logit, BLOCKS)
            dve.wait_ge(ld_w, 16 * len(LOADS))
            logits = psum[:, 6:8, :].rearrange("p a (t e) -> p (a t) e", e=EXPERTS_B)
            nc.vector.tensor_tensor(gate[:].rearrange("p (g j) e -> p g j e", j=4),
                                    logits.rearrange("p (j g) e -> p g j e", j=4),
                                    br_sb[:].unsqueeze(1).unsqueeze(1).to_broadcast([P, 8, 4, EXPERTS_B]),
                                    ALU.add).then_inc(dve_seq, 1)
            dve.wait_ge(dve_seq, dve_n.next())
            nc.vector.tensor_reduce(top[:], gate[:], AX.X, ALU.max).then_inc(dve_seq, 1)
            dve.wait_ge(dve_seq, dve_n.next())
            nc.vector.tensor_tensor(gate[:], gate[:], top[:].unsqueeze(2).to_broadcast([P, TILES, EXPERTS_B]),
                                    ALU.subtract).then_inc(b_sub, 1)
            dve.wait_ge(b_exp, 1)
            nc.vector.tensor_reduce(total[:], gate[:], AX.X, ALU.add).then_inc(dve_seq, 1)
            dve.wait_ge(dve_seq, dve_n.next())
            nc.vector.reciprocal(inv[:], total[:]).then_inc(dve_seq, 1)
            dve.wait_ge(dve_seq, dve_n.next())
            nc.vector.tensor_tensor(gate[:], gate[:], inv[:].unsqueeze(2).to_broadcast([P, TILES, EXPERTS_B]),
                                    ALU.mult).then_inc(b_gate, 1)

            nc.vector.tensor_copy(same16[:], C("same_expert")).then_inc(dve_seq, 1)
            nc.vector.tensor_scalar(half_expert[:], C("same_expert"), 0.5, None, ALU.mult).then_inc(dve_seq, 1)
            nc.vector.memset(start16[:, 0:2], 0.0).then_inc(dve_seq, 1)
            nc.vector.memset(start16[:, 2:3], TOKENS / 2 / 4).then_inc(dve_seq, 1)
            nc.vector.memset(need[:], float(CAP)).then_inc(dve_seq, 1)
            nc.vector.tensor_copy(cand[:], C("first_candidates")).then_inc(b_cand, 1)
            for _ in range(5):
                dve_n.next()

            def banks(row):
                return row.rearrange("p (a n) -> p a n", a=2)

            dve.wait_ge(b_gtr, 2)
            for d in range(RANK_DIGITS):
                shift = DIGIT_BITS * (RANK_DIGITS - 1 - d)
                nc.vector.tensor_scalar(banks(gate_bits[:, d]),
                                        psum[:, 0:2, :].bitcast(I32), shift, (1 << DIGIT_BITS) - 1,
                                        ALU.arith_shift_right, ALU.bitwise_and).then_inc(b_int, 1)
            dve.wait_ge(dve_seq, dve_n.now())

            def rank_rounds(d):
                for k in range(len(STRIDES)):
                    number = len(STRIDES) * d + k
                    dve.wait_ge(b_cand, number + d + 1)
                    for c in range(2):
                        nc.vector.tensor_scalar(is_above[:, c], key[:], cand[:, c + 1:c + 2], None, ALU.is_ge,
                                                ALU.add, accum_out=n_reach[:, c:c + 1]).then_inc(b_cnt, 1)
                    nc.vector.tensor_tensor(moved[:], cand[:], C("move")[:, 4 * k:4 * k + 4],
                                            ALU.add).then_inc(dve_seq, 1)
                    dve_n.next()
                    dve.wait_ge(b_sum, number + 1)
                    nc.vector.tensor_scalar(reached[:], psum[:, 2, 0:3], need[:, 0:1], None, ALU.is_ge, ALU.add,
                                            accum_out=strides_won[:]).then_inc(b_won, 1)
                    dve.wait_ge(dve_seq, dve_n.now())
                    dve.wait_ge(b_won, number + 1)
                    nc.vector.scalar_tensor_tensor(cand[:], C("won")[:, 4 * k:4 * k + 4], strides_won[:, 0:1],
                                                   moved[:], ALU.mult, ALU.add).then_inc(b_cand, 1)
                dve.wait_ge(b_cand, len(STRIDES) * (d + 1) + d + 1)
                nc.vector.tensor_scalar(thr_digit[:, bass.ds(d, 1)], cand[:, 0:1], -1.0, None,
                                        ALU.add).then_inc(dve_seq, 1)
                dve_n.next()

            dve.wait_ge(b_digit, 1)
            nc.vector.tensor_copy(key[:], digit16[:, 0]).then_inc(b_key, 1)
            dve.wait_ge(b_key, 1)
            with dve_n.loop(dve, RANK_DIGITS - 1, len(STRIDES) + 3) as d:
                rank_rounds(d)
                nc.vector.tensor_scalar(is_above[:, 0], key[:], cand[:, 0:1], None, ALU.is_gt, ALU.add,
                                        accum_out=n_higher[:]).then_inc(b_higher, 1)
                dve.wait_ge(b_higher, d + 1)
                dve.wait_ge(b_digit, RANK_DIGITS)
                nc.vector.scalar_tensor_tensor(key[:], key[:], cand[:, 0:1], digit16[:, bass.ds(d + 1, 1)],
                                               ALU.is_equal, ALU.mult).then_inc(dve_seq, 1)
                dve_n.next()
                dve.wait_ge(b_nsum, d + 1)
                nc.vector.tensor_tensor(need[:], need[:], psum[:, 3, 4:5], ALU.subtract).then_inc(dve_seq, 1)
                dve.wait_ge(dve_seq, dve_n.next())
                nc.vector.tensor_copy(cand[:], C("first_candidates")).then_inc(b_cand, 1)
            rank_rounds(RANK_DIGITS - 1)
            dve.wait_ge(dve_seq, dve_n.now())
            for d in range(RANK_DIGITS - 1):
                nc.vector.tensor_scalar(thr_digit[:, d:d + 1], thr_digit[:, d:d + 1],
                                        DIGIT_BITS * (RANK_DIGITS - 1 - d), None,
                                        ALU.logical_shift_left).then_inc(dve_seq, 1)
                dve_n.next()
            dve.wait_ge(dve_seq, dve_n.now())
            nc.vector.scalar_tensor_tensor(thr[:], thr_digit[:, 0:1], thr_digit[:, 1:2], thr_digit[:, 2:3],
                                           ALU.bitwise_or, ALU.bitwise_or).then_inc(dve_seq, 1)
            dve.wait_ge(dve_seq, dve_n.next())
            nc.vector.tensor_scalar(banks(above), psum[:, 0:2, :], thr[:].bitcast(F32), None, ALU.is_gt, ALU.add,
                                    accum_out=count[:, 0:1]).then_inc(b_tot, 1)
            nc.vector.tensor_scalar(banks(tied), psum[:, 0:2, :], thr[:].bitcast(F32), None, ALU.is_equal, ALU.add,
                                    accum_out=count[:, 1:2]).then_inc(b_tot, 1)
            dve.wait_ge(b_tot, 2)
            nc.vector.tensor_tensor_scan(n_above, zeros[:], above, 0.0, ALU.add, ALU.add).then_inc(dve_seq, 1)
            dve_n.next()
            nc.vector.tensor_tensor_scan(n_tied, zeros[:], tied, 0.0, ALU.add, ALU.add).then_inc(dve_seq, 1)
            dve_n.next()
            dve.wait_ge(b_off, 1)
            nc.vector.tensor_copy(offs[:], psum[:, 3, 0:2]).then_inc(dve_seq, 1)
            dve.wait_ge(dve_seq, dve_n.next())
            nc.vector.scalar_tensor_tensor(n_above, n_above, offs[:, 0:1], above, ALU.add, ALU.mult).then_inc(dve_seq, 1)
            dve_n.next()
            nc.vector.scalar_tensor_tensor(n_tied, n_tied, offs[:, 1:2], tied, ALU.add, ALU.mult).then_inc(dve_seq, 1)
            dve.wait_ge(dve_seq, dve_n.next())
            nc.vector.scalar_tensor_tensor(n_above, n_above, -1.0, n_tied, ALU.add, ALU.add).then_inc(b_pos, 1)

            nc.vector.tensor_copy(slot_hi[:].rearrange("p h a e -> p (h a e)"), C("slot_hi")).then_inc(dve_seq, 1)
            dve_n.next()
            nc.vector.tensor_copy(slot_lo[:].rearrange("p a e -> p (a e)"), C("slot_lo")).then_inc(dve_seq, 1)
            dve_n.next()
            dve.wait_ge(b_ptr, 2)
            nc.vector.tensor_copy(place[:].rearrange("p (a t) e -> p a (t e)", a=2), psum[:, 0:2, :]).then_inc(dve_seq, 1)
            dve.wait_ge(dve_seq, dve_n.next())
            nc.vector.tensor_scalar(place2[:], place[:], 4, None, ALU.arith_shift_right).then_inc(dve_seq, 1)
            dve.wait_ge(dve_seq, dve_n.next())
            nc.vector.tensor_copy(hi16[:], place2[:]).then_inc(dve_seq, 1)
            dve.wait_ge(dve_seq, dve_n.next())
            nc.vector.tensor_scalar(place2[:], place[:], 15, None, ALU.bitwise_and).then_inc(dve_seq, 1)
            dve.wait_ge(dve_seq, dve_n.next())
            nc.vector.tensor_copy(lo16[:], place2[:]).then_inc(dve_seq, 1)
            dve.wait_ge(dve_seq, dve_n.next())
            with dve.Fori(0, TILES // 4) as i:
                for k in range(4):
                    u, b = 4 * i + k, k
                    dve.wait_ge(b_ohmm, u + 1)
                    nc.vector.tensor_tensor(oh_hi[:, b], hi16[:, bass.ds(u, 1), :].rearrange("p o (h e) -> p (o h) e", h=2)
                                            .unsqueeze(2).to_broadcast([P, 2, 8, 16]),
                                            slot_hi[:], ALU.is_equal).then_inc(b_ohhi, 1)
                    nc.vector.tensor_tensor(oh_lo[:, b], lo16[:, bass.ds(u, 1), :].to_broadcast([P, 16, EXPERTS_B]),
                                            slot_lo[:], ALU.is_equal).then_inc(b_oh, 1)
            dve.wait_ge(b_ohmm, 4 + TILES)
            for h in range(2):
                nc.vector.tensor_tensor(picked[:, h], psum[:, 4 + h, 0:256].rearrange("p (l e) -> p l e", e=16),
                                        C("same_e16").unsqueeze(1).to_broadcast([P, 16, 16]),
                                        ALU.mult).then_inc(dve_seq, 1)
                dve_n.next()
            dve.wait_ge(dve_seq, dve_n.now())
            nc.vector.tensor_reduce(ids_f[:], picked[:], AX.X, ALU.add).then_inc(dve_seq, 1)
            dve.wait_ge(dve_seq, dve_n.next())
            nc.vector.tensor_tensor(ids_x[:], ids_f[:].unsqueeze(2).to_broadcast([P, 2, 8, 16]),
                                    C("same_slot_hi").unsqueeze(1).unsqueeze(3).to_broadcast([P, 2, 8, 16]),
                                    ALU.mult).then_inc(b_ids, 1)
            dve.wait_ge(b_idt, 1)
            nc.vector.tensor_scalar(idx[:], psum[:, 2, 0:EXPERTS_B], float(ID_SHIFT), None, ALU.add).then_inc(b_idx, 1)
            dve.wait_ge(b_idx, 1)
            nc.vector.tensor_scalar(idx_w[:], idx[:], TOKENS - P + 7, None, ALU.bitwise_and)
            nc.vector.tensor_scalar(id_row[:], idx[:], 7 * 16, 1, ALU.bitwise_and, ALU.arith_shift_right)
            nc.vector.tensor_scalar(id_win[:], idx[:], 8, 3, ALU.bitwise_and, ALU.logical_shift_left).then_inc(dve_seq, 1)
            dve.wait_ge(dve_seq, dve_n.next())
            nc.vector.tensor_tensor(idx_w[:], idx_w[:], id_row[:], ALU.bitwise_or).then_inc(dve_seq, 1)
            dve.wait_ge(dve_seq, dve_n.next())
            nc.vector.tensor_tensor(idx_w[:], idx_w[:], id_win[:], ALU.bitwise_or).then_inc(b_idx, 1)

            dve.sem_inc(b_y, 2)
            dve.sem_inc(b_xgt, 2)

            def group_rows(g):
                dve.wait_ge(b_xg, g + 1)
                nc.vector.tensor_copy(xt[:, g % 2, :], psum[:, g % 2, :]).then_inc(b_xgt, 1)

            group_rows(0)
            for g in range(GROUPS_B):
                if g + 1 < GROUPS_B:
                    group_rows(g + 1)
                b = g % 2
                dve.wait_ge(b_down, g + 3)
                if g > 1:
                    for k in range(2):
                        dve.wait_ge(b_sc[k], 32 * g - 32)
                for k in range(4):
                    ins = nc.vector.tensor_scalar(y_b[:, b, k, :], psum[:, 5 + b, P * k:P * (k + 1)],
                                                  rows_b[:, g % 4, k, P + 4 * g + k:P + 4 * g + k + 1], None, ALU.mult)
                ins.then_inc(b_y, 1)

            def heads(ap):
                return ap.rearrange("p (h j) -> p h j", j=WIN)

            for w in range(2):
                nc.vector.tensor_tensor(heads(rel[:, w, :]), heads(rel[:, w, :]),
                                        msk[:, w, :].unsqueeze(1).to_broadcast([P, HEADS, WIN]),
                                        ALU.add).then_inc(c_rel, 1)
                nc.vector.tensor_copy(v_x[:, w, :, :, :, HDIM].rearrange("p w a h -> p (w a) h"),
                                      C("half").unsqueeze(1).to_broadcast([P, 16, 2])).then_inc(c_one, 1)
            dve.wait_ge(c_rel, 2)

            def chunk(c):
                return slice(8 * c, 8 * c + 8)

            def chunk_variance(c):
                dve.wait_ge(c_sum, c + 1)
                stats_of(chunk(c))
                variance(chunk(c), c_var, 1e-6)

            def later_chunks(t, b):
                if isinstance(t, int) and 2 < t <= CHUNKS_C + 1:
                    inverse_root(chunk(t - 2), c_sqrt, t - 1)
                if isinstance(t, int) and 0 < t < CHUNKS_C:
                    chunk_variance(t)

            dve.wait_ge(c_ld[0], 16 * 2)
            nc.vector.tensor_tensor(x_tok[:, chunk(0), :], x_tok[:, chunk(0), :], extra[:, chunk(0), :],
                                    ALU.add).then_inc(c_sum, 1)
            chunk_variance(0)
            inverse_root(chunk(0), c_sqrt, 1)
            dve.sem_inc(c_k, 1)
            dve.sem_inc(c_sb, 2)
            dve.sem_inc(c_o, 7)

            def norm_tile(t, b):
                dve.wait_ge(c_tr, t + 1)
                norm(xn[:, b, 0, :], t).then_inc(c_xn, 1)

            def keys(t, b):
                dve.wait_ge(c_q, t + 1)
                dve.wait_ge(c_va, t + 1)
                dve.wait_ge(c_s, t + 1)
                for h in range(2):
                    ins = nc.vector.scalar_tensor_tensor(
                        k_x[:, b, h], psum[:, 1, P + WIN * h:P + WIN * (h + 1)].unsqueeze(1).to_broadcast([P, 8, WIN]),
                        qkb[:, 1, h:h + 1], C("head_of_8").unsqueeze(2).to_broadcast([P, 8, WIN]), ALU.add, ALU.mult)
                ins.then_inc(c_k, 1)

            def add_bias(t, b):
                dve.wait_ge(c_s, 2 + t + 1)
                dve.wait_ge(c_exp, t + 1)
                nc.vector.tensor_tensor(score[:, b, :].rearrange("p (q n) -> p q n", q=2),
                                        psum[:, 2 + 2 * b:4 + 2 * b, :],
                                        rel[:, b, :].rearrange("p (q n) -> p q n", q=2), ALU.add).then_inc(c_sb, 1)

            def find_peak(t, b):
                dve.wait_ge(c_sb, 2 + t + 1)
                nc.vector.tensor_reduce(peak[:, b, :], heads(score[:, b, :]), AX.X, ALU.max).then_inc(c_mx, 1)

            def normalize(t, b):
                dve.wait_ge(c_av, 2 + t + 1)
                dve.wait_ge(c_res, t + 1)
                o = psum[:, 0, P:P + HEADS * (HDIM + 1)].rearrange("p (h d) -> p h d", d=HDIM + 1)
                nc.vector.reciprocal(inv_sum[:, b, :], o[:, :, HDIM]).then_inc(c_one, 1)
                dve.wait_ge(c_one, 2 + t + 1)
                nc.vector.tensor_tensor(att[:, b, :].rearrange("p (h d) -> p h d", d=HDIM), o[:, :, 0:HDIM],
                                        inv_sum[:, b, :].unsqueeze(2).to_broadcast([P, HEADS, HDIM]),
                                        ALU.mult).then_inc(c_o, 1)

            def tile_stats(t, b):
                dve.wait_ge(c_res, 2 + t + 1)
                nc.vector.bn_stats(stats[:, bass.ds(t, 1), :], x_tok[:, bass.ds(t, 1), :]).then_inc(c_st, 1)

            early, late = slice(0, 4 * EARLY_D), slice(4 * EARLY_D, TILES)

            def norm_block(n):
                dve.wait_ge(c_v, 4 * n + 4)
                for k in range(4):
                    ins = norm(extra[:, 4 * n + k:4 * n + k + 1, :], 4 * n + k)
                ins.then_inc(d_xn, 1)

            def early_norm(t, b):
                if isinstance(t, int) and t == early.stop - 1:
                    dve.wait_ge(c_st, early.stop)
                    variance(early, d_var, 1e-5)
                first = early.stop + 1
                if isinstance(t, int) and t == first:
                    inverse_root(early, d_sqrt, 1)
                if isinstance(t, int) and first <= t < first + EARLY_D:
                    norm_block(t - first)

            staggered(dve, TILES, [(normalize, 8), (add_bias, 4), (find_peak, 4), (keys, 2), (norm_tile, 0),
                                   (later_chunks, 0), (tile_stats, 9), (early_norm, 9)])

            dve.wait_ge(c_st, TILES)
            variance(late, d_var, 1e-5)
            inverse_root(late, d_sqrt, 2)
            for n in range(EARLY_D, BLOCKS):
                norm_block(n)

            def link(ins):
                ins.then_inc(dve_seq, 1)
                dve.wait_ge(dve_seq, dve_n.next())

            def wide(ap):
                return ap.unsqueeze(2).to_broadcast(TE)

            rank8 = C("rank8").unsqueeze(1).to_broadcast(TE)
            nc.vector.tensor_copy(tri_b[:], C("tri"))
            nc.vector.tensor_copy(lane_b[:], C("lane"))
            nc.vector.tensor_copy(tile_no_b[:], C("tile_no"))
            nc.vector.memset(ones_b[:], 1.0)
            dve.wait_ge(d_log, BLOCKS)
            link(nc.vector.tensor_copy(lg[:].rearrange("p t e -> p (t e)"), psum[:, 2, 0:TILES * EXPERTS_D]))

            def best(top_of, onehot):
                link(nc.vector.tensor_reduce(top_of[:], lg[:], AX.X, ALU.max))
                link(nc.vector.tensor_tensor(hit[:], lg[:], wide(top_of[:]), ALU.is_equal))
                link(nc.vector.tensor_tensor(hit[:], hit[:], rank8, ALU.mult))
                link(nc.vector.tensor_reduce(rank[:], hit[:], AX.X, ALU.max))
                link(nc.vector.tensor_tensor(onehot[:], rank8, wide(rank[:]), ALU.is_equal))

            best(peak1, first)
            link(nc.vector.scalar_tensor_tensor(lg[:], first[:], -3.0e38, lg[:], ALU.mult, ALU.add))
            best(peak2, second)
            nc.vector.tensor_tensor(ratio[:], peak2[:], peak1[:], ALU.subtract).then_inc(d_dm, 1)
            nc.vector.tensor_tensor(chosen[:], first[:], second[:], ALU.add).then_inc(d_sel, 1)
            dve.wait_ge(d_ex, 1)
            link(nc.vector.tensor_scalar(weight2, ratio[:], 1.0, None, ALU.add))
            link(nc.vector.reciprocal(weight1, weight2))
            nc.vector.tensor_tensor(weight2, ratio[:], weight1, ALU.mult).then_inc(d_wt, 1)
            dve.wait_ge(d_pre, 1)
            inside = psum[:, 3, 0:256].rearrange("p (t e) -> p t e", e=EXPERTS_D)
            link(nc.vector.tensor_copy(n_tile[:], psum[:, 3, 256:512].rearrange("p (t e) -> p e t", e=EXPERTS_D)))
            link(nc.vector.tensor_tensor_scan(n_run[:].rearrange("p e t -> p (e t)"), C("restart"),
                                              n_tile[:].rearrange("p e t -> p (e t)"), 0.0, ALU.mult, ALU.add))
            link(nc.vector.tensor_scalar(tiles_i[:], n_run[:, :, TILES - 1], float(P - 1), None, ALU.add))
            link(nc.vector.tensor_scalar(tiles_i[:], tiles_i[:], 7, None, ALU.arith_shift_right))
            link(nc.vector.tensor_copy(tiles_f[:], tiles_i[:]))
            link(nc.vector.tensor_tensor_scan(end_tile[:], zeros[:, 0:EXPERTS_D], tiles_f[:], 0.0, ALU.add, ALU.add))
            link(nc.vector.tensor_tensor(base[:], end_tile[:], tiles_f[:], ALU.subtract))
            link(nc.vector.tensor_scalar(base[:], base[:], float(P), -1.0, ALU.mult, ALU.add))
            link(nc.vector.tensor_tensor(n_run[:], n_run[:], n_tile[:], ALU.subtract))
            link(nc.vector.tensor_tensor(n_run[:], n_run[:], base[:].unsqueeze(2).to_broadcast([P, EXPERTS_D, TILES]),
                                         ALU.add))
            link(nc.vector.tensor_tensor(slot_f[:], inside, n_run[:].rearrange("p e t -> p t e"), ALU.add))
            for k, onehot in enumerate((first, second)):
                link(nc.vector.tensor_tensor(hit[:], slot_f[:], onehot[:], ALU.mult))
                link(nc.vector.tensor_reduce(slot_of[:, k, :], hit[:], AX.X, ALU.add))
            link(nc.vector.tensor_copy(slot_i[:], slot_of[:]))
            pair_list = "p k t -> p (k t)"
            link(nc.vector.tensor_scalar(part_i[:], slot_i[:], P - 1, None, ALU.bitwise_and))
            link(nc.vector.tensor_copy(slot_lane[:], part_i[:].rearrange(pair_list)))
            link(nc.vector.tensor_scalar(part_i[:], slot_i[:], 7, None, ALU.arith_shift_right))
            link(nc.vector.tensor_copy(slot_tile[:], part_i[:].rearrange(pair_list)))
            for k in range(2):
                pairs = slice(TILES * k, TILES * (k + 1))
                n_p = [P, TILES, TILES_D]
                nc.vector.tensor_tensor(oh_tile[:, pairs, :], tile_no_b[:].unsqueeze(1).to_broadcast(n_p),
                                        slot_tile[:, pairs].unsqueeze(2).to_broadcast(n_p),
                                        ALU.is_equal).then_inc(d_oh, 1)
                nc.vector.tensor_tensor(oh_lane[:, pairs, :], lane_b[:].unsqueeze(1).to_broadcast([P, TILES, P]),
                                        slot_lane[:, pairs].unsqueeze(2).to_broadcast([P, TILES, P]),
                                        ALU.is_equal).then_inc(d_lane, 1)
            link(nc.vector.tensor_tensor(past[:], C("tile_no").unsqueeze(2).to_broadcast([P, TILES_D, EXPERTS_D]),
                                         end_tile[:].unsqueeze(1).to_broadcast([P, TILES_D, EXPERTS_D]), ALU.is_ge))
            nc.vector.memset(tile_e[:, TILES_D:], 0.0)
            link(nc.vector.tensor_reduce(tile_e[:, 0:TILES_D], past[:], AX.X, ALU.add))
            link(nc.vector.tensor_scalar(tile_e[:], tile_e[:], float(EXPERTS_D - 1), None, ALU.min))
            for k in range(2):
                first_of = tile_e[:, DIGITS * k:DIGITS * k + TILES_D].rearrange("p (n d) -> p n d", d=UNROLL_D)
                ins = nc.vector.tensor_tensor(digits[:, k], first_of[:, :, 0:DIGITS],
                                              C("digit").unsqueeze(1).to_broadcast([P, TILES_D // UNROLL_D, DIGITS]),
                                              ALU.mult)
            link(ins)
            link(nc.vector.tensor_reduce(packed[:], digits[:].rearrange("p k n d -> p n k d"), AX.X, ALU.add))
            nc.vector.tensor_copy(packed_i[:], packed[:]).then_inc(d_map, 1)
            dve.wait_ge(d_inv, 1)
            link(nc.vector.tensor_copy(pair_f[:], psum[:, 4, 0:TILES_D]))
            link(nc.vector.scalar_tensor_tensor(pair_f[:], psum[:, 4, TILES_D:2 * TILES_D], float(P), pair_f[:],
                                                ALU.mult, ALU.add))
            link(nc.vector.tensor_scalar(gather_i[:], pair_f[:], float(TOKENS - P), None, ALU.add))
            nc.vector.tensor_scalar(gather_i[:], gather_i[:], TOKENS - 1, None, ALU.bitwise_and).then_inc(d_idx, 1)
            link(nc.vector.scalar_tensor_tensor(dest_f[:], pair_f[:], 0.0, C("spare_row"), ALU.is_equal, ALU.mult))
            link(nc.vector.tensor_tensor(dest_f[:], dest_f[:], pair_f[:], ALU.add))
            link(nc.vector.tensor_scalar(dest_i[:], dest_f[:], float(-P), None, ALU.add))
            nc.vector.tensor_scalar(dest_row[:], dest_i[:], 7 * 8, 1, ALU.bitwise_and, ALU.logical_shift_left)
            link(nc.vector.tensor_scalar(dest_win[:], dest_i[:], WIN, 3, ALU.bitwise_and, ALU.arith_shift_right))
            link(nc.vector.tensor_scalar(dest_i[:], dest_i[:], (1 << 15) - P + 7, None, ALU.bitwise_and))
            link(nc.vector.tensor_tensor(dest_row[:], dest_row[:], dest_win[:], ALU.bitwise_or))
            nc.vector.tensor_tensor(dest_i[:], dest_i[:], dest_row[:], ALU.bitwise_or).then_inc(d_idx, 1)
            dve.wait_ge(d_wi, 1)
            link(nc.vector.tensor_copy(weights_i[:].rearrange("p k t -> p (k t)"), psum[:, 7, 0:2 * TILES]))
            dve.sem_inc(e_act, 2)

            def product(t, b):
                dve.wait_ge(e_silu, 2 + t + 1)
                dve.wait_ge(e_h3, t + 1)
                dve.wait_ge(e_yp, t + 1)
                nc.vector.tensor_tensor(act_d[:, b, :], silu_d[:, b, :], psum[:, 3 + b, 0:FF_D],
                                        ALU.mult).then_inc(e_act, 1)

            def tile_weights(b, e):
                nc.vector.tensor_copy(w13_t[:, b], w13_sb[:, bass.ds(e, 1), :, :]
                                      .rearrange("p e k h -> p (e k) h")).then_inc(e_w, 1)

            def step(t, b, e_later):
                product(t, b)
                tile_weights(b, e_later)

            dve.wait_ge(d_map, 1)
            e = experts_of(0, mybir.EngineType.DVE)
            tile_weights(0, e[0])
            tile_weights(1, e[1])
            with dve.Fori(0, TILES_D // UNROLL_D - 1) as i:
                e = experts_of(i, mybir.EngineType.DVE)
                for k in range(UNROLL_D):
                    step(UNROLL_D * i + k, k % 2, e[k + 2])
            e = experts_of(TILES_D // UNROLL_D - 1, mybir.EngineType.DVE)
            for t in range(TILES_D - UNROLL_D, TILES_D - 2):
                step(t, t % 2, e[t % UNROLL_D + 2])
            for t in range(TILES_D - 2, TILES_D):
                product(t, t % 2)

            dve.wait_ge(d_xback, 16)
            for n in range(BLOCKS):
                dve.wait_ge(f_back[n], 16 * 2)
                for t in range(4 * n, 4 * n + 4):
                    ins = nc.vector.scalar_tensor_tensor(x_tok[:, t, :], back1[:, t, :], weights_i[:, 0, t:t + 1],
                                                         x_tok[:, t, :], ALU.mult, ALU.add)
                link(ins)
                dve.wait_ge(f_scaled, n + 1)
                tiles = slice(4 * n, 4 * n + 4)
                nc.vector.tensor_tensor(x_tok[:, tiles, :], x_tok[:, tiles, :], back2[:, tiles, :],
                                        ALU.add).then_inc(f_sum, 1)

        @block.scalar
        def _(act):
            act.dma_start(ident, const[:, 0:P]).then_inc(ld_ident, 16)
            for dst, src in CONV_LOADS:
                act.dma_start(dst, src).then_inc(ld_conv, 16)

            def chunk_root(c):
                act.wait_ge(c_var, c + 1)
                nc.scalar.activation(std[:, 8 * c:8 * c + 8], var_eps[:, 8 * c:8 * c + 8],
                                     ACT.Sqrt).then_inc(c_sqrt, 1)

            def later_roots(t, b):
                if isinstance(t, int) and 1 < t <= CHUNKS_C:
                    chunk_root(t - 1)

            def block_root(n, var_ready, sqrt_done):
                act.wait_ge(var_ready, n + 1)
                nc.scalar.activation(std[:, 4 * n:4 * n + 4], var_eps[:, 4 * n:4 * n + 4],
                                     ACT.Sqrt).then_inc(sqrt_done, 1)

            def pad(n):
                if n == 0:
                    act.wait_ge(s_pad, 1)
                act.wait_ge(a_tr, n + 1)
                nc.scalar.copy(xpad[:, 2 * n:2 * n + 2, 1:SIDE + 1, 1:SIDE + 1],
                               psum[:, 0, :].rearrange("p (n a c) -> p n a c", n=2, a=SIDE)).then_inc(a_pad, 1)

            def relu(n):
                if n == 0:
                    act.wait_ge(ld_conv, 16 * len(CONV_LOADS))
                act.wait_ge(a_conv, n + 1)
                if n > 1:
                    act.wait_ge(a_back, n - 1)
                nc.scalar.activation(conv_t[:, n % 2, :], psum[:, 2 + n % 2, :], ACT.Relu,
                                     bias=conv_bs[:, 0:1]).then_inc(a_relu, 1)

            def evac_b(n):
                act.wait_ge(b_tr, n + 1)
                if n > 1:
                    act.wait_ge(b_logit, n - 1)
                nc.scalar.copy(xt[:, n % 2, :], psum[:, 1, :]).then_inc(b_xt, 1)

            short_pipeline(BLOCKS, [(lambda n: block_root(n, a_var, a_sqrt), 0), (pad, 0), (relu, 2),
                                    (lambda n: block_root(n, b_var, b_sqrt), 4), (evac_b, 5)])
            act.wait_ge(b_sub, 1)
            nc.scalar.activation(gate[:], gate[:], ACT.Exp).then_inc(b_exp, 1)
            for d in range(RANK_DIGITS):
                act.wait_ge(b_int, d + 1)
                nc.scalar.activation(digit16[:, d], gate_bits[:, d], ACT.Copy, bias=1.0).then_inc(b_digit, 1)
            act.wait_ge(b_key, 1)
            with act.Fori(0, RANK_DIGITS - 1) as d:
                for k in range(len(STRIDES)):
                    act.wait_ge(b_cand, (len(STRIDES) + 1) * d + k + 1)
                    nc.scalar.activation(signs16[:], key[:], ACT.Sign, bias=cand[:, 3:4],
                                         accum_out=sign_sum[:]).then_inc(b_sign, 1)
            for k in range(len(STRIDES)):
                act.wait_ge(b_cand, (len(STRIDES) + 1) * (RANK_DIGITS - 1) + k + 1)
                nc.scalar.activation(signs16[:], key[:], ACT.Sign, bias=cand[:, 3:4],
                                     accum_out=sign_sum[:]).then_inc(b_sign, 1)
            token0 = const_at["token_id"][0]
            with act.Fori(0, TILES // 4) as i:
                for k in range(4):
                    u, b = 4 * i + k, k
                    act.wait_ge(b_ohhi, u + 1)
                    act.wait_ge(b_ohmm, u + 1)
                    nc.scalar.activation(oh_id[:, b].rearrange("p h a e -> p (h a e)"),
                                         oh_hi[:, b].rearrange("p h a e -> p (h a e)"), ACT.Copy,
                                         scale=cst[:, bass.ds(token0 + u, 1)]).then_inc(b_ohid, 1)
            act.sem_inc(b_act, 3)
            with act.Fori(0, GROUPS_B // 2) as i:
                for b in range(2):
                    g = 2 * i + b
                    for c, (_, n) in enumerate(CHUNKS_B):
                        act.wait_ge(b_up, 3 * g + c + 1)
                        nc.scalar.activation(act_b[0:n, b, c, :], psum[0:n, 2 + c, :], ACT.Silu,
                                             bias=bu_sb[0:n, bass.ds(g, 1), c]).then_inc(b_act, 1)

            for k in range(2):
                act.wait_ge(b_sc[k], 16 * 16)
            reload(act, y_odd, extra)
            chunk_root(0)
            nc.scalar.mul(qb_scaled[:], qkb[:, 0, :], SCALE).then_inc(c_qb, 1)
            act.sem_inc(c_xt, 1)
            act.sem_inc(c_exp, 2)
            act.sem_inc(c_pe, 2)
            act.wait_ge(c_qb, 1)
            act.wait_ge(c_qz, 1)

            def evac_normed(t, b):
                act.wait_ge(c_tr, 2 + t + 1)
                act.wait_ge(c_qkv, t + 1)
                nc.scalar.copy(xt[:, b, 0:P], psum[:, 0, 0:P]).then_inc(c_xt, 1)

            def evac_query_value(t, b):
                act.wait_ge(c_qkv, 2 + t + 1)
                act.wait_ge(c_s, t + 1)
                for w in range(2):
                    rows = slice(WIN * w, WIN * (w + 1))
                    for h in range(2):
                        ins = nc.scalar.activation(q_x[rows, b, h, WIN * w:WIN * (w + 1)],
                                                   psum[rows, 1, WIN * h:WIN * (h + 1)], ACT.Identity,
                                                   bias=qb_scaled[rows, h:h + 1], scale=SCALE)
                ins.then_inc(c_q, 1)
                nc.scalar.copy(extra[:, bass.ds(t, 1), :], psum[:, 1:2, 2 * P:3 * P]).then_inc(c_va, 1)

            def exponent(t, b):
                act.wait_ge(c_sub, t + 1)
                act.wait_ge(c_pt, 2 * t + 2)
                nc.scalar.activation(prob[:, b, :], score[:, b, :], ACT.Exp).then_inc(c_exp, 1)

            def evac_prob(t, b):
                act.wait_ge(c_av, t + 1)
                for h in range(2):
                    act.wait_ge(c_pt, 4 + 2 * t + h + 1)
                    nc.scalar.copy(prob_t[:, b, 512 * h:512 * h + 512], psum[:, 6 + h, :]).then_inc(c_pe, 1)

            def evac_block(n):
                act.wait_ge(d_tr, n + 1)
                nc.scalar.copy(xt[:, n % 2, :], psum[:, 3 + n % 2, :]).then_inc(d_xt, 1)

            def early_block(t, b):
                if isinstance(t, int) and t == 4 * EARLY_D + 3:
                    act.wait_ge(d_var, 1)
                    nc.scalar.activation(std[:, 0:4 * EARLY_D], var_eps[:, 0:4 * EARLY_D],
                                         ACT.Sqrt).then_inc(d_sqrt, 1)
                if isinstance(t, int) and t == TILES - 1:
                    evac_block(0)

            def late_root():
                act.wait_ge(d_var, 2)
                nc.scalar.activation(std[:, 4 * EARLY_D:], var_eps[:, 4 * EARLY_D:], ACT.Sqrt).then_inc(d_sqrt, 1)

            act.sem_inc(d_xt, 2)
            staggered(act, TILES, [(evac_query_value, 2), (evac_normed, 1), (later_roots, 0), (exponent, 5),
                                   (evac_prob, 6), (early_block, 6)])
            for n in range(1, BLOCKS):
                if n == EARLY_D - 1:
                    late_root()
                evac_block(n)
            act.wait_ge(d_dm, 1)
            nc.scalar.activation(ratio[:], ratio[:], ACT.Exp).then_inc(d_ex, 1)

            for k in range(2):
                pairs = slice(TILES * k, TILES * (k + 1))
                act.wait_ge(d_oh, k + 1)
                nc.scalar.activation(oh_value[:, pairs, 0, :], oh_tile[:, pairs, :], ACT.Copy,
                                     scale=C("partition")).then_inc(d_ohp, 1)

            act.sem_inc(e_silu, 2)
            act.sem_inc(e_xt, 1)
            act.sem_inc(e_y, 2)

            def rows_t(t, b):
                act.wait_ge(e_tr, t + 1)
                nc.scalar.copy(xt_d[:, b, :], psum[:, 0, 0:P]).then_inc(e_xt, 1)

            def silu(t, b):
                act.wait_ge(e_h1, t + 1)
                act.wait_ge(e_act, t + 1)
                nc.scalar.activation(silu_d[:, b, :], psum[:, 1 + b, 0:FF_D], ACT.Silu).then_inc(e_silu, 1)

            def step(t, b):
                c = b % 2
                if not (isinstance(t, int) and t == TILES_D - 1):
                    silu(t + 1, 1 - c)
                if not (isinstance(t, int) and t >= TILES_D - 2):
                    rows_t(t + 2, c)
                if not (isinstance(t, int) and t == 0):
                    evac_y(t - 1, (b + 3) % 4)

            def evac_y(t, b):
                act.wait_ge(e_yp, 2 + t + 1)
                if not (isinstance(t, int) and t < 4):
                    act.wait_ge(e_st[b], 4 * (t - b))
                nc.scalar.copy(y_d[:, b, :], psum[:, 5 + b % 2, 0:P]).then_inc(e_y, 1)

            rows_t(0, 0)
            rows_t(1, 1)
            silu(0, 0)
            rounds(act, TILES_D, 4, step, head=2)
            evac_y(TILES_D - 1, (TILES_D - 1) % 4)

            for n in range(BLOCKS):
                act.wait_ge(f_back[n], 16 * 2)
                for t in range(4 * n, 4 * n + 4):
                    ins = nc.scalar.activation(back2[:, t, :], back2[:, t, :], ACT.Copy, scale=weights_i[:, 1, t:t + 1])
                ins.then_inc(f_scaled, 1)

        @block.tensor
        def _(pe):
            def transpose(dst, src):
                return nc.tensor.transpose(dst, src, ident)

            def transpose_a(n):
                pe.wait_ge(a_xn, n + 1)
                if n == 0:
                    pe.wait_ge(ld_ident, 16)
                if n > 0:
                    pe.wait_ge(a_pad, n)
                for k in range(4):
                    ins = transpose(psum[:, 0, P * k:P * (k + 1)], xn[:, 0, k, :])
                ins.then_inc(a_tr, 1)

            def convolve(n):
                if n == 0:
                    pe.wait_ge(ld_conv, 16 * len(CONV_LOADS))
                pe.wait_ge(a_pad, n + 1)
                if n > 1:
                    pe.wait_ge(a_relu, n - 1)
                for tap in range(TAPS):
                    dy, dx = tap // 3, tap % 3
                    ins = nc.tensor.matmul(psum[:, 2 + n % 2, :], conv_sb[:, tap, :],
                                           xpad[:, 2 * n:2 * n + 2, dy:dy + SIDE, dx:dx + SIDE],
                                           start=tap == 0, stop=tap == TAPS - 1)
                ins.then_inc(a_conv, 1)

            def transpose_back(n):
                pe.wait_ge(a_relu, n + 1)
                if n > 1:
                    pe.wait_ge(a_res, n - 1)
                for k in range(4):
                    ins = transpose(psum[:, 4 + n % 2, P * k:P * (k + 1)], conv_t[:, n % 2, P * k:P * (k + 1)])
                ins.then_inc(a_back, 1)

            def transpose_b(n):
                pe.wait_ge(b_xn, n + 1)
                if n > 0:
                    pe.wait_ge(b_xt, n)
                for k in range(4):
                    ins = transpose(psum[:, 1, P * k:P * (k + 1)], xn[:, 1, k, :])
                ins.then_inc(b_tr, 1)

            def route(n):
                if n == 0:
                    pe.wait_ge(ld_w, 16 * len(LOADS))
                pe.wait_ge(b_xt, n + 1)
                for k in range(4):
                    t = 4 * n + k
                    ins = nc.tensor.matmul(psum[:, 6 + t // 16, EXPERTS_B * (t % 16):EXPERTS_B * (t % 16 + 1)],
                                           xt[:, n % 2, P * k:P * (k + 1)], wr_sb[:], start=True, stop=True)
                ins.then_inc(b_logit, 1)

            short_pipeline(BLOCKS, [(transpose_a, 0), (transpose_b, 5), (convolve, 1), (transpose_back, 2),
                                    (route, 6)])
            pe.sem_inc(b_down, 2)
            pe.wait_ge(b_gate, 1)
            for g in range(8):
                ins = transpose(psum[:, g // 4, P * (g % 4):P * (g % 4 + 1)],
                                gate[:, 4 * g:4 * g + 4, :].rearrange("p j e -> p (j e)"))
                if g % 4 == 3:
                    ins.then_inc(b_gtr, 1)
            def rank_rounds(d):
                for k in range(len(STRIDES)):
                    number = len(STRIDES) * d + k
                    if not (isinstance(number, int) and number == 0):
                        pe.wait_ge(b_won, number)
                    nc.tensor.matmul(psum[:, 2, 0:3], same16[:], start16[:], start=True, stop=False,
                                     skip_group_check=True)
                    pe.wait_ge(b_sign, number + 1)
                    nc.tensor.matmul(psum[:, 2, 2:3], half_expert[:], sign_sum[:], start=False, stop=False,
                                     skip_group_check=True)
                    pe.wait_ge(b_cnt, 2 * number + 2)
                    nc.tensor.matmul(psum[:, 2, 0:2], same16[:], n_reach[:], start=False, stop=True,
                                     skip_group_check=True).then_inc(b_sum, 1)

            def higher(d):
                pe.wait_ge(b_higher, d + 1)
                nc.tensor.matmul(psum[:, 3, 4:5], same16[:], n_higher[:], start=True, stop=True,
                                 skip_group_check=True).then_inc(b_nsum, 1)

            pe.wait_ge(b_key, 1)
            rank_rounds(0)
            higher(0)
            with pe.Fori(1, RANK_DIGITS - 1) as d:
                rank_rounds(d)
                higher(d)
            rank_rounds(RANK_DIGITS - 1)
            pe.wait_ge(b_tot, 2)
            nc.tensor.matmul(psum[:, 3, 0:2], C("earlier_segment"), count[:, 0:2], start=True, stop=False,
                             skip_group_check=True)
            nc.tensor.matmul(psum[:, 3, 1:2], C("same_expert"), count[:, 0:1], start=False, stop=True,
                             skip_group_check=True).then_inc(b_off, 1)
            pe.wait_ge(b_pos, 1)
            for g in range(8):
                ins = transpose(psum[:, g // 4, P * (g % 4):P * (g % 4 + 1)], n_above[:, P * g:P * (g + 1)])
                if g % 4 == 3:
                    ins.then_inc(b_ptr, 1)
            pe.sem_inc(b_ohmm, 4)
            for u in range(TILES):
                pe.wait_ge(b_oh, u + 1)
                pe.wait_ge(b_ohid, u + 1)
                for h in range(2):
                    ins = nc.tensor.matmul(psum[:, 4 + h, 0:256], oh_id[:, u % 4, h].rearrange("p a e -> p (a e)"),
                                           oh_lo[:, u % 4, :, 16 * h:16 * h + 16], start=u == 0, stop=u == TILES - 1)
                ins.then_inc(b_ohmm, 1)

            pe.wait_ge(b_ids, 1)
            for h in range(2):
                ins = nc.tensor.matmul(psum[:, 2, 16 * h:16 * h + 16], ids_x[:, h].rearrange("p a l -> p (a l)"),
                                       C("same_e16"), start=True, stop=True)
            ins.then_inc(b_idt, 1)

            def group_rows(g):
                pe.wait_ge(b_gath[g % 4], 64 * (g // 4) + 64)
                pe.wait_ge(b_xgt, g + 1)
                for k in range(4):
                    ins = transpose(psum[:, g % 2, P * k:P * (k + 1)], rows_b[:, g % 4, k, 0:P])
                ins.then_inc(b_xg, 1)

            group_rows(0)
            for g in range(GROUPS_B):
                b = g % 2
                pe.wait_ge(b_xgt, 2 + g + 1)
                pe.wait_ge(b_w[b], 48 * (g // 2 + 1))
                for c, (f, n) in enumerate(CHUNKS_B):
                    pe.wait_ge(b_act, 3 * g + c + 1)
                    nc.tensor.matmul(psum[0:n, 2 + c, :], wu_sb[:, b, f:f + n], xt[:, b, :], start=True,
                                     stop=True).then_inc(b_up, 1)
                if g + 1 < GROUPS_B:
                    group_rows(g + 1)
                pe.wait_ge(b_y, g + 1)
                nc.tensor.matmul(psum[:, 5 + b, :], ones_row[:], bd_sb[:, b, :], start=True, stop=False,
                                 skip_group_check=True)
                for c, (f, n) in enumerate(CHUNKS_B):
                    pe.wait_ge(b_act, 3 + 3 * g + c + 1)
                    for k in range(4):
                        ins = nc.tensor.matmul(psum[:, 5 + b, P * k:P * (k + 1)],
                                               act_b[0:n, b, c, P * k:P * (k + 1)], wd_sb[0:n, b, k, c, :],
                                               start=False, stop=c == 2, skip_group_check=True)
                ins.then_inc(b_down, 1)

            pe.sem_inc(c_tr, 2)
            pe.sem_inc(c_qkv, 2)
            pe.sem_inc(c_s, 2)
            pe.sem_inc(c_pt, 4)
            pe.sem_inc(c_av, 2)

            def products(t, b):
                pe.wait_ge(c_xt, 1 + t + 1)
                pe.wait_ge(c_k, t + 1)
                for k in range(4):
                    for w in range(2):
                        nc.tensor.matmul(psum[WIN * w:WIN * (w + 1), 1, WIN * k:WIN * (k + 1)],
                                         wqkv[:, WIN * k:WIN * (k + 1)], xt[:, b, WIN * w:WIN * (w + 1)],
                                         start=True, stop=True)
                for w in range(2):
                    for h in range(2):
                        o = psum[WIN * h:WIN * h + WIN, 1, 2 * P + WIN * w:2 * P + WIN * (w + 1)]
                        cols = slice(2 * P + WIN * h, 2 * P + WIN * (h + 1))
                        ins = nc.tensor.matmul(o, xt[:, b, WIN * w:WIN * (w + 1)], wqkv[:, cols], start=True, stop=True)
                ins.then_inc(c_qkv, 1)

            def transpose_normed(t, b):
                pe.wait_ge(c_xn, t + 1)
                pe.wait_ge(c_xt, t + 1)
                pe.wait_ge(c_o, t + 1)
                transpose(psum[:, 0, 0:P], xn[:, b, 0, :]).then_inc(c_tr, 1)

            def scores(t, b):
                pe.wait_ge(c_q, t + 1)
                pe.wait_ge(c_k, 1 + t + 1)
                pe.wait_ge(c_sb, t + 1)
                for h in range(2):
                    ins = nc.tensor.matmul(psum[:, 2 + 2 * b + h, :], q_x[:, b, h, :],
                                           k_x[:, b, h].rearrange("p h j -> p (h j)"), start=True, stop=True)
                ins.then_inc(c_s, 1)

            def transpose_prob(t, b):
                pe.wait_ge(c_exp, 2 + t + 1)
                for h in range(2):
                    pe.wait_ge(c_pe, 2 * t + h + 1)
                    for k in range(4):
                        at = 512 * h + P * k
                        ins = transpose(psum[:, 6 + h, P * k:P * (k + 1)], prob[:, b, at:at + P])
                    ins.then_inc(c_pt, 1)

            def weigh_values(t, b):
                pe.wait_ge(c_pe, 2 + 2 * t + 2)
                pe.wait_ge(c_v, t + 1)
                pe.wait_ge(c_o, 7 + t)
                last = min(t + 6, TILES - 1) if isinstance(t, int) else t + 6
                pe.wait_ge(c_xt, 1 + last + 1)
                for pair in range(8):
                    for w in range(2):
                        n = 2 * (HDIM + 1)
                        ins = nc.tensor.matmul(psum[WIN * w:WIN * (w + 1), 0, P + n * pair:P + n * (pair + 1)],
                                               prob_t[:, b, P * pair + WIN * w:P * pair + WIN * (w + 1)],
                                               v_x[:, b, w, pair].rearrange("p h d -> p (h d)"), start=True, stop=True)
                ins.then_inc(c_av, 1)

            pe.wait_ge(c_one, 2)
            def gate_block(n):
                if n == 0:
                    pe.wait_ge(c_sb, 2 + TILES)
                if n < BLOCKS:
                    pe.wait_ge(d_xn, n + 1)
                    pe.wait_ge(d_xt, n + 1)
                    for k in range(4):
                        ins = transpose(psum[:, 3 + n % 2, P * k:P * (k + 1)], extra[:, 4 * n + k, :])
                    ins.then_inc(d_tr, 1)
                if n > 0:
                    pe.wait_ge(d_xt, 2 + n)
                    for k in range(4):
                        t = 4 * (n - 1) + k
                        ins = nc.tensor.matmul(psum[:, 2, EXPERTS_D * t:EXPERTS_D * (t + 1)],
                                               xt[:, (n - 1) % 2, P * k:P * (k + 1)], gw[:], start=True, stop=True)
                    ins.then_inc(d_log, 1)

            def early_gate(t, b):
                if isinstance(t, int) and t >= TILES - 3:
                    gate_block(t - (TILES - 3))

            staggered(pe, TILES, [(products, 2), (transpose_normed, 1), (scores, 3), (transpose_prob, 6),
                                  (weigh_values, 7), (early_gate, 7)])

            for n in range(3, BLOCKS + 1):
                gate_block(n)
            pe.wait_ge(d_sel, 1)
            flat = chosen[:].rearrange("p t e -> p (t e)")
            nc.tensor.matmul(psum[:, 3, 0:256], tri_b[:], flat, start=True, stop=True)
            nc.tensor.matmul(psum[:, 3, 256:512], ones_b[:], flat, start=True, stop=True).then_inc(d_pre, 1)

            pe.wait_ge(d_wt, 1)
            nc.tensor.matmul(psum[:, 7, 0:2 * TILES], C("to_window"), weights[:].rearrange("p k t -> p (k t)"),
                             start=True, stop=True).then_inc(d_wi, 1)
            for j in range(2 * TILES):
                if j % TILES == 0:
                    pe.wait_ge(d_lane, j // TILES + 1)
                    pe.wait_ge(d_oht, j // TILES + 1)
                    pe.wait_ge(d_ohp, j // TILES + 1)
                ins = nc.tensor.matmul(psum[:, 4, 0:2 * TILES_D], oh_lane[:, j, :],
                                       oh_value[:, j].rearrange("p a n -> p (a n)"), start=j == 0,
                                       stop=j == 2 * TILES - 1)
            ins.then_inc(d_inv, 1)
            pe.wait_ge(d_map, 1)
            pe.wait_ge(d_idx, 2)

            def rows_t(t, b):
                pe.wait_ge(e_ld[b], 4 * (t - b) + 16)
                pe.wait_ge(e_xt, t + 1)
                transpose(psum[:, 0, 0:P], rows_d[:, b, :]).then_inc(e_tr, 1)

            def up(k, bank, ready, b):
                for c in range(0, FF_D, P):
                    ins = nc.tensor.matmul(psum[:, bank, c:c + P], w13_t[:, b, k, c:c + P], xt_d[:, b, :],
                                           start=True, stop=True)
                ins.then_inc(ready, 1)

            def first_up(t, b):
                pe.wait_ge(e_w, t + 1)
                pe.wait_ge(e_xt, 1 + t + 1)
                pe.wait_ge(e_silu, t + 1)
                up(0, 1 + b, e_h1, b)

            def second_up(t, b):
                pe.wait_ge(e_act, t + 1)
                up(1, 3 + b, e_h3, b)

            def step(t, b, e):
                c = b % 2
                if not (isinstance(t, int) and t == TILES_D - 1):
                    first_up(t + 1, 1 - c)
                    second_up(t + 1, 1 - c)
                if not (isinstance(t, int) and t >= TILES_D - 2):
                    rows_t(t + 2, (b + 2) % 4)
                pe.wait_ge(e_act, 2 + t + 1)
                pe.wait_ge(e_y, t + 1)
                for k in range(CHUNKS_D):
                    ins = nc.tensor.matmul(psum[:, 5 + c, 0:P], act_d[:, c, P * k:P * (k + 1)],
                                           w2_sb[:, bass.ds(e, 1), k, :], start=k == 0, stop=k == CHUNKS_D - 1)
                ins.then_inc(e_yp, 1)

            pe.sem_inc(e_yp, 2)
            rows_t(0, 0)
            rows_t(1, 1)
            e = experts_of(0, mybir.EngineType.PE)
            first_up(0, 0)
            second_up(0, 0)
            step(0, 0, e[0])
            with pe.Fori(0, (TILES_D - 1) // UNROLL_D) as i:
                e = experts_of(i, mybir.EngineType.PE)
                for k in range(UNROLL_D):
                    step(UNROLL_D * i + (k + 1), (k + 1) % 4, e[k + 1])
            rest = (TILES_D - 1) % UNROLL_D
            e = experts_of(TILES_D // UNROLL_D - 1, mybir.EngineType.PE)
            for k in range(rest):
                t = TILES_D - rest + k
                step(t, t % 4, e[k + 1])


_IN_NAMES = ["x", "conv_w", "conv_b", "w_router", "b_router", "w_up", "b_up", "w_down", "b_down",
             "qkv_w", "qk_bias", "v_bias", "rel_bias", "mask", "gate_w", "w1", "w3", "w2", "const"]


def lay_out(inputs):
    import numpy as np
    a = {k: np.asarray(v) for k, v in inputs.items()}
    k = a["L0_conv_kernel"]
    width = k.shape[2]
    conv = np.zeros((P, TAPS, P), k.dtype)
    for g in range(P // width):
        s = slice(g * width, (g + 1) * width)
        conv[s, :, s] = k.reshape(TAPS, width, P)[:, :, s].transpose(1, 0, 2)
    up = a["L0_ffn_W_up"]
    b_up = np.zeros((GROUPS_B, 3 * P), up.dtype)
    b_up[:, :FF_B] = a["L0_ffn_b_up"]
    down = np.zeros((EXPERTS_B, 3 * P, P), up.dtype)
    down[:, :FF_B] = a["L0_ffn_W_down"]
    w0 = np.stack(np.meshgrid(np.arange(8), np.arange(8), indexing="ij")).reshape(2, -1)
    rel = w0[:, :, None] - w0[:, None, :] + 7
    rel = rel[0] * 15 + rel[1]
    bias = a["L1_conv_bias_table"][rel].transpose(0, 2, 1)
    qb = a["L1_conv_qkv_b"]
    w2 = a["L1_ffn_w2"]
    v_cols = np.arange(P).reshape(HEADS // 2, 2, HDIM).transpose(1, 0, 2).ravel()
    qkv_cols = np.concatenate([np.arange(2 * P), 2 * P + v_cols])
    return {
        "x": a["x"].reshape(TOKENS, P),
        "conv_w": conv.reshape(P, TAPS * P),
        "conv_b": a["L0_conv_bias"].reshape(P, 1),
        "w_router": a["L0_ffn_W_router"],
        "b_router": a["L0_ffn_b_router"],
        "w_up": up.transpose(1, 0, 2),
        "b_up": b_up.reshape(GROUPS_B, 3, P).transpose(2, 0, 1),
        "w_down": down.reshape(EXPERTS_B, 3, P, P).transpose(2, 0, 1, 3).reshape(P, -1),
        "b_down": a["L0_ffn_b_down"].reshape(GROUPS_B, 4 * P),
        "qkv_w": a["L1_conv_qkv_w"].T[:, qkv_cols],
        "qk_bias": np.tile(qb[:2 * P].reshape(4, P // 2).T, (2, 1)).reshape(P, 2, 2),
        "v_bias": qb[2 * P:].reshape(1, P),
        "rel_bias": np.concatenate([bias, bias]).reshape(P, HEADS * WIN),
        "mask": window_mask(),
        "gate_w": a["L1_ffn_gate_w"].T,
        "w1": a["L1_ffn_w1"].transpose(2, 0, 1),
        "w3": a["L1_ffn_w3"].transpose(2, 0, 1),
        "w2": w2.transpose(2, 0, 1).reshape(CHUNKS_D, P, EXPERTS_D, P).transpose(1, 2, 0, 3),
    }


def kernel(**inputs):
    import numpy as _np
    import concourse.bacc as _bacc
    from concourse import mybir as _mybir
    from concourse.bass_utils import run_bass_kernel_spmd as _run

    nc = _bacc.Bacc("TRN2", target_bir_lowering=False, num_devices=1)
    laid = lay_out(inputs)
    laid["const"], const_at = constants()
    arrays, args = {}, []
    for name in _IN_NAMES:
        a = _np.ascontiguousarray(laid[name])
        arrays[f"in_{name}_dram"] = a
        args.append(nc.dram_tensor(f"in_{name}_dram", a.shape, _mybir.dt.from_np(a.dtype), kind="ExternalInput").ap())
    args.append(nc.dram_tensor("out_0_dram", (TOKENS, P), F32, kind="ExternalOutput").ap())
    metaformer(nc, const_at, *args)
    r = _run(nc, [arrays], core_ids=[0])
    return r.results[0]["out_0_dram"].reshape(IMAGES, SIDE, SIDE, P)
```
